# Optimizing a Trainium2 kernel written in Bass

```python
import numpy as np
import jax
import jax.numpy as jnp

def _softmax(x, axis=-1):
    return jax.nn.softmax(x, axis=axis)

def _gelu(x):
    return jax.nn.gelu(x, approximate=True)

def _silu(x):
    return jax.nn.silu(x)

def _sigmoid(x):
    return jax.nn.sigmoid(x)

def _layernorm(x, axis=-1, eps=1e-05):
    m = jnp.mean(x, axis=axis, keepdims=True)
    v = jnp.var(x, axis=axis, keepdims=True)
    return (x - m) / jnp.sqrt(v + eps)

def _scatter_add(tgt, idx, src, axis=0):
    return tgt.at[idx].add(src)

def _segment_sum(src, seg, n):
    return jax.ops.segment_sum(src, seg, n)
kernel_name = 'mk_prb_d2_jaxref_r4_43e25d'

def setup_inputs(seed: int=0):
    np.random.seed(seed)
    _w = jnp.asarray

    def _L0_attn_setup():
        import jax, jax.numpy as jnp
        import numpy as np
        D_MODEL = 256
        D_STATE = 16
        D_CONV = 3
        EXPAND = 2
        MLP_RATIO = 4
        HEADDIM = 64
        D_INNER = EXPAND * D_MODEL
        NHEADS = D_INNER // HEADDIM
        CONV_DIM = D_INNER + 2 * D_STATE
        D_IN_PROJ = 2 * D_INNER + 2 * D_STATE + NHEADS

        def rmsnorm(x, w, eps=1e-06):
            return x * jax.lax.rsqrt(jnp.mean(x * x, axis=-1, keepdims=True) + eps) * w

        def silu(x):
            return x * jax.nn.sigmoid(x)

        def causal_depthwise_conv(x, w, b):
            B, L, C = x.shape
            K = w.shape[1]
            xp = jnp.pad(x, ((0, 0), (K - 1, 0), (0, 0)))
            out = b
            for k in range(K):
                out = out + w[:, k] * xp[:, k:k + L, :]
            return out

        def mamba2(h, W_in, conv_w, conv_b, dt_bias, A_log, D, norm_gate_w, W_out):
            B, L, _ = h.shape
            zxbcdt = h @ W_in
            z = zxbcdt[..., :D_INNER]
            xBC = zxbcdt[..., D_INNER:D_INNER + CONV_DIM]
            dt = jax.nn.softplus(zxbcdt[..., D_INNER + CONV_DIM:] + dt_bias)
            xBC = silu(causal_depthwise_conv(xBC, conv_w, conv_b))
            x = xBC[..., :D_INNER].reshape(B, L, NHEADS, HEADDIM)
            Bmat = xBC[..., D_INNER:D_INNER + D_STATE]
            Cmat = xBC[..., D_INNER + D_STATE:]
            A = -jnp.exp(A_log)
            dA = jnp.exp(dt * A)
            dBx = jnp.einsum('blhp,bln,blh->blhpn', x, Bmat, dt)

            def step(state, inp):
                dA_t, dBx_t = inp
                state = state * dA_t[:, :, None, None] + dBx_t
                return (state, state)
            s0 = jnp.zeros((B, NHEADS, HEADDIM, D_STATE), dtype=h.dtype)
            _, states = jax.lax.scan(step, s0, (jnp.moveaxis(dA, 1, 0), jnp.moveaxis(dBx, 1, 0)))
            y = jnp.einsum('lbhpn,bln->blhp', states, Cmat)
            y = y + D[None, None, :, None] * x
            y = y.reshape(B, L, D_INNER)
            y = rmsnorm(y * silu(z), norm_gate_w, eps=1e-05)
            return y @ W_out
        key = jax.random.key(seed)
        ks = jax.random.split(key, 12)
        f = jnp.float32
        d = {}
        d['x'] = jax.random.normal(ks[0], (2, 512, D_MODEL), dtype=f)
        d['norm1_w'] = jnp.ones((D_MODEL,), f)
        d['W_in'] = jax.random.normal(ks[1], (D_MODEL, D_IN_PROJ), f) * D_MODEL ** (-0.5)
        d['conv_w'] = jax.random.normal(ks[2], (CONV_DIM, D_CONV), f) * 0.2
        d['conv_b'] = jnp.zeros((CONV_DIM,), f)
        d['dt_bias'] = jnp.log(jnp.expm1(jax.random.uniform(ks[3], (NHEADS,), f, 0.001, 0.1)))
        d['A_log'] = jnp.log(jax.random.uniform(ks[4], (NHEADS,), f, 1.0, 16.0))
        d['D'] = jnp.ones((NHEADS,), f)
        d['norm_gate_w'] = jnp.ones((D_INNER,), f)
        d['W_out'] = jax.random.normal(ks[5], (D_INNER, D_MODEL), f) * D_INNER ** (-0.5)
        d['norm2_w'] = jnp.ones((D_MODEL,), f)
        d['mlp_w1'] = jax.random.normal(ks[6], (D_MODEL, D_MODEL * MLP_RATIO), f) * D_MODEL ** (-0.5)
        d['mlp_b1'] = jnp.zeros((D_MODEL * MLP_RATIO,), f)
        d['mlp_w2'] = jax.random.normal(ks[7], (D_MODEL * MLP_RATIO, D_MODEL), f) * (D_MODEL * MLP_RATIO) ** (-0.5)
        d['mlp_b2'] = jnp.zeros((D_MODEL,), f)
        return d
    _L0_attn_in = _L0_attn_setup()

    def _L0_ffn_setup():
        import jax, jax.numpy as jnp
        import numpy as np
        D_MODEL = 256
        DEPTH = 8
        M = 2 ** DEPTH
        N_INTERNAL = M - 1
        B, T = (8, 1024)

        def _leaf_probs(gate):
            BT = gate.shape[0]
            lp = jnp.ones((BT, M), dtype=gate.dtype)
            for level in range(DEPTH):
                n = 2 ** level
                half = M // (2 * n)
                g = gate[:, n - 1:2 * n - 1]
                f = jnp.stack([1.0 - g, g], axis=-1)
                f = jnp.broadcast_to(f[..., None], (BT, n, 2, half))
                lp = lp * f.reshape(BT, M)
            return lp
        key = jax.random.key(seed)
        ks = jax.random.split(key, 7)
        x = jax.random.normal(ks[0], (B, T, D_MODEL), dtype=jnp.float32)
        Wq = jax.random.normal(ks[1], (D_MODEL, D_MODEL), dtype=jnp.float32) * 0.02
        routers = jax.random.normal(ks[2], (N_INTERNAL, D_MODEL), dtype=jnp.float32) * 0.02
        leaf_keys = jax.random.normal(ks[3], (M, D_MODEL), dtype=jnp.float32) * 0.02
        leaf_values = jax.random.normal(ks[4], (M, D_MODEL), dtype=jnp.float32) * 0.02
        Wout_w = jax.random.normal(ks[5], (D_MODEL, D_MODEL), dtype=jnp.float32) * 0.02
        Wout_b = jax.random.normal(ks[6], (D_MODEL,), dtype=jnp.float32) * 0.02
        return {'x': x, 'Wq': Wq, 'routers': routers, 'leaf_keys': leaf_keys, 'leaf_values': leaf_values, 'Wout_w': Wout_w, 'Wout_b': Wout_b}
    _L0_ffn_in = _L0_ffn_setup()

    def _L1_attn_setup():
        import jax, jax.numpy as jnp
        import numpy as np
        D_MODEL = 256
        D_STATE = 64
        D_CONV = 4
        EXPAND = 2
        HEADDIM = 128
        NGROUPS = 1
        D_INNER = EXPAND * D_MODEL
        NHEADS = D_INNER // HEADDIM
        CONV_DIM = D_INNER + 2 * NGROUPS * D_STATE
        D_IN_PROJ = 2 * D_INNER + 2 * NGROUPS * D_STATE + NHEADS
        BATCH, SEQLEN = (2, 512)
        DT_MIN, DT_MAX, DT_FLOOR = (0.001, 0.1, 0.0001)
        RMS_EPS = 1e-05

        def _mamba2_forward(u, in_proj_w, conv_w, conv_b, dt_bias, A_log, D_param, norm_w, out_proj_w):
            B, L, _ = u.shape
            zxbcdt = jnp.einsum('bld,ed->ble', u, in_proj_w)
            z = zxbcdt[..., :D_INNER]
            xBC = zxbcdt[..., D_INNER:D_INNER + CONV_DIM]
            dt = jax.nn.softplus(zxbcdt[..., D_INNER + CONV_DIM:] + dt_bias)
            xc = jnp.swapaxes(xBC, 1, 2)
            xc = jax.lax.conv_general_dilated(xc, conv_w, window_strides=(1,), padding=[(D_CONV - 1, 0)], feature_group_count=CONV_DIM)
            xc = jax.nn.silu(xc + conv_b[None, :, None])
            xBC = jnp.swapaxes(xc, 1, 2)
            x = xBC[..., :D_INNER].reshape(B, L, NHEADS, HEADDIM)
            Bmat = xBC[..., D_INNER:D_INNER + D_STATE]
            Cmat = xBC[..., D_INNER + D_STATE:]
            A = -jnp.exp(A_log)

            def step(state, inp):
                dt_t, x_t, B_t, C_t = inp
                dA = jnp.exp(dt_t * A)[:, :, None, None]
                state = state * dA + dt_t[:, :, None, None] * x_t[:, :, :, None] * B_t[:, None, None, :]
                y_t = jnp.einsum('bhpn,bn->bhp', state, C_t) + D_param[None, :, None] * x_t
                return (state, y_t)
            state0 = jnp.zeros((B, NHEADS, HEADDIM, D_STATE), u.dtype)
            inputs = (jnp.moveaxis(dt, 1, 0), jnp.moveaxis(x, 1, 0), jnp.moveaxis(Bmat, 1, 0), jnp.moveaxis(Cmat, 1, 0))
            _, ys = jax.lax.scan(step, state0, inputs)
            y = jnp.moveaxis(ys, 0, 1).reshape(B, L, D_INNER)
            yg = y * jax.nn.silu(z)
            rms = jax.lax.rsqrt(jnp.mean(yg * yg, axis=-1, keepdims=True) + RMS_EPS)
            yn = yg * rms * norm_w
            return jnp.einsum('ble,de->bld', yn, out_proj_w)
        key = jax.random.key(seed)
        ks = jax.random.split(key, 8)
        u = jax.random.normal(ks[0], (BATCH, SEQLEN, D_MODEL), jnp.float32)
        in_proj_w = jax.random.normal(ks[1], (D_IN_PROJ, D_MODEL), jnp.float32) * 0.02
        conv_w = jax.random.normal(ks[2], (CONV_DIM, 1, D_CONV), jnp.float32) * 0.2
        conv_b = jax.random.normal(ks[3], (CONV_DIM,), jnp.float32) * 0.02
        dt = jnp.exp(jax.random.uniform(ks[4], (NHEADS,)) * (jnp.log(DT_MAX) - jnp.log(DT_MIN)) + jnp.log(DT_MIN))
        dt = jnp.maximum(dt, DT_FLOOR)
        dt_bias = dt + jnp.log(-jnp.expm1(-dt))
        A_log = jnp.log(jax.random.uniform(ks[5], (NHEADS,), minval=1.0, maxval=16.0))
        D_param = jnp.ones((NHEADS,), jnp.float32)
        norm_w = jnp.ones((D_INNER,), jnp.float32)
        out_proj_w = jax.random.normal(ks[6], (D_MODEL, D_INNER), jnp.float32) * 0.02
        return {'u': u, 'in_proj_w': in_proj_w, 'conv_w': conv_w, 'conv_b': conv_b, 'dt_bias': dt_bias, 'A_log': A_log, 'D_param': D_param, 'norm_w': norm_w, 'out_proj_w': out_proj_w}
    _L1_attn_in = _L1_attn_setup()

    def _L1_ffn_setup():
        import jax, jax.numpy as jnp
        import numpy as np
        from math import ceil
        CAPACITY_FACTOR = 2.0
        MIN_CAPACITY = 4
        key = jax.random.key(seed)
        ks = jax.random.split(key, 4)
        B, S, D, Di, E = (4, 512, 256, 1024, 8)
        x = jax.random.normal(ks[0], (B, S, D), dtype=jnp.float32)
        Wr = jax.random.normal(ks[1], (D, E), dtype=jnp.float32) * D ** (-0.5)
        W1 = jax.random.normal(ks[2], (E, D, Di), dtype=jnp.float32) * D ** (-0.5)
        b1 = jnp.zeros((E, Di), dtype=jnp.float32)
        W2 = jax.random.normal(ks[3], (E, Di, D), dtype=jnp.float32) * Di ** (-0.5)
        b2 = jnp.zeros((E, D), dtype=jnp.float32)
        return {'x': x, 'Wr': Wr, 'W1': W1, 'b1': b1, 'W2': W2, 'b2': b2}
    _L1_ffn_in = _L1_ffn_setup()
    _d = {'L0_attn_x': _L0_attn_in['x'], 'L0_attn_norm1_w': _L0_attn_in['norm1_w'], 'L0_attn_W_in': _L0_attn_in['W_in'], 'L0_attn_conv_w': _L0_attn_in['conv_w'], 'L0_attn_conv_b': _L0_attn_in['conv_b'], 'L0_attn_dt_bias': _L0_attn_in['dt_bias'], 'L0_attn_A_log': _L0_attn_in['A_log'], 'L0_attn_D': _L0_attn_in['D'], 'L0_attn_norm_gate_w': _L0_attn_in['norm_gate_w'], 'L0_attn_W_out': _L0_attn_in['W_out'], 'L0_attn_norm2_w': _L0_attn_in['norm2_w'], 'L0_attn_mlp_w1': _L0_attn_in['mlp_w1'], 'L0_attn_mlp_b1': _L0_attn_in['mlp_b1'], 'L0_attn_mlp_w2': _L0_attn_in['mlp_w2'], 'L0_attn_mlp_b2': _L0_attn_in['mlp_b2'], 'L0_ffn_Wq': _L0_ffn_in['Wq'], 'L0_ffn_routers': _L0_ffn_in['routers'], 'L0_ffn_leaf_keys': _L0_ffn_in['leaf_keys'], 'L0_ffn_leaf_values': _L0_ffn_in['leaf_values'], 'L0_ffn_Wout_w': _L0_ffn_in['Wout_w'], 'L0_ffn_Wout_b': _L0_ffn_in['Wout_b'], 'L1_attn_in_proj_w': _L1_attn_in['in_proj_w'], 'L1_attn_conv_w': _L1_attn_in['conv_w'], 'L1_attn_conv_b': _L1_attn_in['conv_b'], 'L1_attn_dt_bias': _L1_attn_in['dt_bias'], 'L1_attn_A_log': _L1_attn_in['A_log'], 'L1_attn_D_param': _L1_attn_in['D_param'], 'L1_attn_norm_w': _L1_attn_in['norm_w'], 'L1_attn_out_proj_w': _L1_attn_in['out_proj_w'], 'L1_ffn_Wr': _L1_ffn_in['Wr'], 'L1_ffn_W1': _L1_ffn_in['W1'], 'L1_ffn_b1': _L1_ffn_in['b1'], 'L1_ffn_W2': _L1_ffn_in['W2'], 'L1_ffn_b2': _L1_ffn_in['b2']}
    _x0 = _d['L0_attn_x']
    _d['L0_attn_x'] = jax.random.normal(jax.random.fold_in(jax.random.key(seed), 1), (2, 2048, 256), dtype=_x0.dtype)
    del _x0
    return _d

def reference(L0_attn_x, L0_attn_norm1_w, L0_attn_W_in, L0_attn_conv_w, L0_attn_conv_b, L0_attn_dt_bias, L0_attn_A_log, L0_attn_D, L0_attn_norm_gate_w, L0_attn_W_out, L0_attn_norm2_w, L0_attn_mlp_w1, L0_attn_mlp_b1, L0_attn_mlp_w2, L0_attn_mlp_b2, L0_ffn_Wq, L0_ffn_routers, L0_ffn_leaf_keys, L0_ffn_leaf_values, L0_ffn_Wout_w, L0_ffn_Wout_b, L1_attn_in_proj_w, L1_attn_conv_w, L1_attn_conv_b, L1_attn_dt_bias, L1_attn_A_log, L1_attn_D_param, L1_attn_norm_w, L1_attn_out_proj_w, L1_ffn_Wr, L1_ffn_W1, L1_ffn_b1, L1_ffn_W2, L1_ffn_b2):

    def _L0_attn_ref(x, norm1_w, W_in, conv_w, conv_b, dt_bias, A_log, D, norm_gate_w, W_out, norm2_w, mlp_w1, mlp_b1, mlp_w2, mlp_b2):
        import jax, jax.numpy as jnp
        import numpy as np
        D_MODEL = 256
        D_STATE = 16
        D_CONV = 3
        EXPAND = 2
        MLP_RATIO = 4
        HEADDIM = 64
        D_INNER = EXPAND * D_MODEL
        NHEADS = D_INNER // HEADDIM
        CONV_DIM = D_INNER + 2 * D_STATE
        D_IN_PROJ = 2 * D_INNER + 2 * D_STATE + NHEADS

        def rmsnorm(x, w, eps=1e-06):
            return x * jax.lax.rsqrt(jnp.mean(x * x, axis=-1, keepdims=True) + eps) * w

        def silu(x):
            return x * jax.nn.sigmoid(x)

        def causal_depthwise_conv(x, w, b):
            B, L, C = x.shape
            K = w.shape[1]
            xp = jnp.pad(x, ((0, 0), (K - 1, 0), (0, 0)))
            out = b
            for k in range(K):
                out = out + w[:, k] * xp[:, k:k + L, :]
            return out

        def mamba2(h, W_in, conv_w, conv_b, dt_bias, A_log, D, norm_gate_w, W_out):
            B, L, _ = h.shape
            zxbcdt = h @ W_in
            z = zxbcdt[..., :D_INNER]
            xBC = zxbcdt[..., D_INNER:D_INNER + CONV_DIM]
            dt = jax.nn.softplus(zxbcdt[..., D_INNER + CONV_DIM:] + dt_bias)
            xBC = silu(causal_depthwise_conv(xBC, conv_w, conv_b))
            x = xBC[..., :D_INNER].reshape(B, L, NHEADS, HEADDIM)
            Bmat = xBC[..., D_INNER:D_INNER + D_STATE]
            Cmat = xBC[..., D_INNER + D_STATE:]
            A = -jnp.exp(A_log)
            dA = jnp.exp(dt * A)
            dBx = jnp.einsum('blhp,bln,blh->blhpn', x, Bmat, dt)

            def step(state, inp):
                dA_t, dBx_t = inp
                state = state * dA_t[:, :, None, None] + dBx_t
                return (state, state)
            s0 = jnp.zeros((B, NHEADS, HEADDIM, D_STATE), dtype=h.dtype)
            _, states = jax.lax.scan(step, s0, (jnp.moveaxis(dA, 1, 0), jnp.moveaxis(dBx, 1, 0)))
            y = jnp.einsum('lbhpn,bln->blhp', states, Cmat)
            y = y + D[None, None, :, None] * x
            y = y.reshape(B, L, D_INNER)
            y = rmsnorm(y * silu(z), norm_gate_w, eps=1e-05)
            return y @ W_out
        h = rmsnorm(x, norm1_w)
        h = mamba2(h, W_in, conv_w, conv_b, dt_bias, A_log, D, norm_gate_w, W_out)
        x = x + h
        h = rmsnorm(x, norm2_w)
        h = silu(h @ mlp_w1 + mlp_b1) @ mlp_w2 + mlp_b2
        return x + h

    def _L0_ffn_ref(x, Wq, routers, leaf_keys, leaf_values, Wout_w, Wout_b):
        import jax, jax.numpy as jnp
        import numpy as np
        D_MODEL = 256
        DEPTH = 8
        M = 2 ** DEPTH
        N_INTERNAL = M - 1
        B, T = (8, 1024)

        def _leaf_probs(gate):
            BT = gate.shape[0]
            lp = jnp.ones((BT, M), dtype=gate.dtype)
            for level in range(DEPTH):
                n = 2 ** level
                half = M // (2 * n)
                g = gate[:, n - 1:2 * n - 1]
                f = jnp.stack([1.0 - g, g], axis=-1)
                f = jnp.broadcast_to(f[..., None], (BT, n, 2, half))
                lp = lp * f.reshape(BT, M)
            return lp
        Bv, Tv, d = x.shape
        q = jnp.einsum('btd,ed->bte', x, Wq)
        q_flat = q.reshape(Bv * Tv, d)
        gate = jax.nn.sigmoid(q_flat @ routers.T)
        leaf_prob = _leaf_probs(gate)
        ret = (leaf_prob @ leaf_values).reshape(Bv, Tv, d)
        return jnp.einsum('btd,ed->bte', ret, Wout_w) + Wout_b

    def _L1_attn_ref(u, in_proj_w, conv_w, conv_b, dt_bias, A_log, D_param, norm_w, out_proj_w):
        import jax, jax.numpy as jnp
        import numpy as np
        D_MODEL = 256
        D_STATE = 64
        D_CONV = 4
        EXPAND = 2
        HEADDIM = 128
        NGROUPS = 1
        D_INNER = EXPAND * D_MODEL
        NHEADS = D_INNER // HEADDIM
        CONV_DIM = D_INNER + 2 * NGROUPS * D_STATE
        D_IN_PROJ = 2 * D_INNER + 2 * NGROUPS * D_STATE + NHEADS
        BATCH, SEQLEN = (2, 512)
        DT_MIN, DT_MAX, DT_FLOOR = (0.001, 0.1, 0.0001)
        RMS_EPS = 1e-05

        def _mamba2_forward(u, in_proj_w, conv_w, conv_b, dt_bias, A_log, D_param, norm_w, out_proj_w):
            B, L, _ = u.shape
            zxbcdt = jnp.einsum('bld,ed->ble', u, in_proj_w)
            z = zxbcdt[..., :D_INNER]
            xBC = zxbcdt[..., D_INNER:D_INNER + CONV_DIM]
            dt = jax.nn.softplus(zxbcdt[..., D_INNER + CONV_DIM:] + dt_bias)
            xc = jnp.swapaxes(xBC, 1, 2)
            xc = jax.lax.conv_general_dilated(xc, conv_w, window_strides=(1,), padding=[(D_CONV - 1, 0)], feature_group_count=CONV_DIM)
            xc = jax.nn.silu(xc + conv_b[None, :, None])
            xBC = jnp.swapaxes(xc, 1, 2)
            x = xBC[..., :D_INNER].reshape(B, L, NHEADS, HEADDIM)
            Bmat = xBC[..., D_INNER:D_INNER + D_STATE]
            Cmat = xBC[..., D_INNER + D_STATE:]
            A = -jnp.exp(A_log)

            def step(state, inp):
                dt_t, x_t, B_t, C_t = inp
                dA = jnp.exp(dt_t * A)[:, :, None, None]
                state = state * dA + dt_t[:, :, None, None] * x_t[:, :, :, None] * B_t[:, None, None, :]
                y_t = jnp.einsum('bhpn,bn->bhp', state, C_t) + D_param[None, :, None] * x_t
                return (state, y_t)
            state0 = jnp.zeros((B, NHEADS, HEADDIM, D_STATE), u.dtype)
            inputs = (jnp.moveaxis(dt, 1, 0), jnp.moveaxis(x, 1, 0), jnp.moveaxis(Bmat, 1, 0), jnp.moveaxis(Cmat, 1, 0))
            _, ys = jax.lax.scan(step, state0, inputs)
            y = jnp.moveaxis(ys, 0, 1).reshape(B, L, D_INNER)
            yg = y * jax.nn.silu(z)
            rms = jax.lax.rsqrt(jnp.mean(yg * yg, axis=-1, keepdims=True) + RMS_EPS)
            yn = yg * rms * norm_w
            return jnp.einsum('ble,de->bld', yn, out_proj_w)
        return _mamba2_forward(u, in_proj_w, conv_w, conv_b, dt_bias, A_log, D_param, norm_w, out_proj_w)

    def _L1_ffn_ref(x, Wr, W1, b1, W2, b2):
        import jax, jax.numpy as jnp
        import numpy as np
        from math import ceil
        CAPACITY_FACTOR = 2.0
        MIN_CAPACITY = 4
        B, S, D = x.shape
        E = Wr.shape[1]
        N = B * S
        k = max(MIN_CAPACITY, ceil(N * CAPACITY_FACTOR / E))
        xt = x.reshape(N, D)
        scores = jax.nn.softmax(xt @ Wr, axis=-1)
        G, idx = jax.lax.top_k(scores.T, k)
        X_in = xt[idx]
        h = jax.nn.gelu(jnp.einsum('ekd,edh->ekh', X_in, W1) + b1[:, None, :], approximate=False)
        X_e = jnp.einsum('ekh,ehd->ekd', h, W2) + b2[:, None, :]
        contrib = (G[..., None] * X_e).reshape(E * k, D)
        out = jnp.zeros((N, D), dtype=x.dtype).at[idx.reshape(-1)].add(contrib)
        return out.reshape(B, S, D)
    x = L0_attn_x
    xn = _layernorm(x, axis=-1)
    x = x + _L0_attn_ref(xn, L0_attn_norm1_w, L0_attn_W_in, L0_attn_conv_w, L0_attn_conv_b, L0_attn_dt_bias, L0_attn_A_log, L0_attn_D, L0_attn_norm_gate_w, L0_attn_W_out, L0_attn_norm2_w, L0_attn_mlp_w1, L0_attn_mlp_b1, L0_attn_mlp_w2, L0_attn_mlp_b2) + _L0_ffn_ref(xn, L0_ffn_Wq, L0_ffn_routers, L0_ffn_leaf_keys, L0_ffn_leaf_values, L0_ffn_Wout_w, L0_ffn_Wout_b)
    xn = _layernorm(x, axis=-1)
    x = x + _L1_attn_ref(xn, L1_attn_in_proj_w, L1_attn_conv_w, L1_attn_conv_b, L1_attn_dt_bias, L1_attn_A_log, L1_attn_D_param, L1_attn_norm_w, L1_attn_out_proj_w) + _L1_ffn_ref(xn, L1_ffn_Wr, L1_ffn_W1, L1_ffn_b1, L1_ffn_W2, L1_ffn_b2)
    return x

_drawn_inputs = setup_inputs


def setup_inputs(seed=0):
    import zlib

    import numpy as np

    out = dict(_drawn_inputs(seed))
    spreads = {'L0_attn_norm1_w': (1.0, 0.2),
     'L0_attn_conv_b': (0.0, 0.1),
     'L0_attn_D': (1.0, 0.2),
     'L0_attn_norm_gate_w': (1.0, 0.2),
     'L0_attn_norm2_w': (1.0, 0.2),
     'L0_attn_mlp_b1': (0.0, 0.3),
     'L0_attn_mlp_b2': (0.0, 0.1),
     'L1_attn_D_param': (1.0, 0.2),
     'L1_attn_norm_w': (1.0, 0.2),
     'L1_ffn_b1': (0.0, 0.628),
     'L1_ffn_b2': (0.0, 0.427)}
    factors = {'L0_attn_dt_bias': 7.217,
     'L0_attn_A_log': 8.0,
     'L0_ffn_Wq': 8.0,
     'L0_ffn_routers': 8.0,
     'L0_ffn_leaf_values': 8.0,
     'L0_ffn_Wout_w': 8.0,
     'L0_ffn_Wout_b': 5.879,
     'L1_attn_dt_bias': 8.0,
     'L1_attn_A_log': 8.0}
    for name, (base, spread) in spreads.items():
        noise = np.random.default_rng([zlib.crc32(name.encode()), seed]).standard_normal(out[name].shape)
        drawn = base * np.exp(spread * noise) if base else spread * noise
        out[name] = jnp.asarray(drawn.astype(out[name].dtype))
    for name, factor in factors.items():
        out[name] = (out[name] * factor).astype(out[name].dtype)
    return out
```

```python
import concourse.bass as bass
from concourse import mybir
from contextlib import ExitStack

P = 128
D = 256
KD = D // P
DI = 512
T = 512
CH = 4
NB, SEQ = 2, 2048
NT = NB * SEQ
STEPS = NT // T
TILES = NT // P
NE = 8
HID = 1024
HB = HID // P
CAP = NT * 2 // NE
LEAVES = 256
ROW = D + NE
LIM = -110.0

fp32 = mybir.dt.float32
bf16 = mybir.dt.bfloat16
i32 = mybir.dt.int32
u32 = mybir.dt.uint32
ALU = mybir.AluOpType
ACT = mybir.ActivationFunctionType
AXX = mybir.AxisListType.X


W0 = 32
PREPPED = 33
DF0, DN, DB0, DF1 = 31, 9, 11, 56


class Signal:

    def __init__(self, sem, per):
        self.sem, self.per = sem, per


def wait(eng, signal, step, n):
    value = step * signal.per + n
    if isinstance(value, int) and value <= 0:
        return
    eng.wait_ge(signal.sem, value)


class Chain:

    def __init__(self, sem, per):
        self.links, self.step, self.n = Signal(sem, per), None, 0

    def begin(self, step):
        self.step, self.n = step, 0

    def put(self, ins):
        self.n += 1
        ins.then_inc(self.links.sem, 1)

    def see(self, eng, back=0):
        wait(eng, self.links, self.step, self.n - back)

    def end(self):
        assert self.n == self.links.per, (self.n, self.links.per)


class Layer:

    def __init__(self, name, taps, state, heads, cpart, tree):
        self.name, self.taps, self.state, self.heads, self.cpart = name, taps, state, heads, cpart
        self.hp = DI // heads
        self.tree = tree
        self.halo = taps - 1
        self.segs = heads * P // 512
        head = (["xnT0", "xnT1", "hT0", "hT1", "dt", "gate0", "gate1"] if tree else ["dt"])
        head += ["bc", "x0", "x1", "x2", "x3"]
        order = ["z0", "xt0"]
        for c in range(CH):
            if c + 1 < CH:
                order += [f"z{c+1}", f"xt{c+1}"]
            order += [f"inter{c}", f"state{c}"]
        self.front = head + order
        assert len(self.front) % 2 == 0
        self.back = (["lT0", "lT1", "h2T0", "h2T1"] + [f"up{k}" for k in range(HB)]
                     + [f"down{c}" for c in range(CH)] + ["nT0", "nT1", "rt0", "rt1"]) if tree else []


LAYERS = [Layer("m0", 3, 16, 8, 32, True), Layer("m1", 4, 64, 4, 64, False)]


def program(nc, d, out):
    ctx = ExitStack()
    with ctx:
        def sb(name, shape, dt=fp32):
            return ctx.enter_context(nc.sbuf_tensor(name, shape, dt))

        def sem(name):
            return ctx.enter_context(nc.semaphore(name))

        def sig(name, per=1):
            return Signal(sem(name), per)

        SC = sb("SC", [P, TILES, NE])
        ident = sb("ident", [P, P])
        triU = sb("triU", [P, P])
        strL = sb("strL", [P, P])
        ones = sb("ones", [P, P])
        flags = sb("flags", [P, STEPS + 1])
        nhalf = sb("nhalf", [P, 8])
        W = []
        for L in LAYERS:
            w = {}
            n = L.name
            w["bc"] = sb(n + "wbc", [P, KD, P])
            w["dt"] = sb(n + "wdt", [P, KD, L.heads])
            w["conv"] = sb(n + "conv", [P, 5, L.taps + 1])
            w["dtb"] = sb(n + "dtb", [P, L.heads])
            w["A"] = sb(n + "A", [P, L.heads])
            w["D"] = sb(n + "D", [P, L.heads])
            w["gn"] = sb(n + "gn", [P, CH])
            W.append(w)
        n1w = sb("n1w", [P, KD])
        n2w = sb("n2w", [P, KD])
        wr = sb("wr", [P, KD, NE])
        EW = sb("EW", [P, 2, 2 * KD * HID])
        w1 = EW[:, 0, 0:KD * HID].rearrange("p (k n) -> p k n", k=KD)
        w2 = EW[:, 0, KD * HID:].rearrange("p (k n) -> p k n", k=HB)
        wg = EW[:, 1, 0:KD * LEAVES].rearrange("p (k n) -> p k n", k=KD)
        wv = EW[:, 1, 512:1024].rearrange("p (k n) -> p k n", k=KD)
        W0BIG = sb("m0big", [P, 3, KD * DI])
        for w, big in zip(W, (W0BIG[:, :, :], EW[:, 1, 1024:4096].rearrange("p (a n) -> p a n", a=3))):
            w["z"] = big[:, 0, :].rearrange("p (k n) -> p k n", k=KD)
            w["x"] = big[:, 1, :].rearrange("p (k n) -> p k n", k=KD)
            w["out"] = big[:, 2, :].rearrange("p (k n) -> p k n", k=CH)
        b1 = sb("b1", [P, HB])
        b2 = sb("b2", [P, 2, D])

        thr = sb("thr", [P, NE], i32)
        cand = sb("cand", [P, NE], i32)
        okm = sb("okm", [P, NE], i32)
        bit = sb("bit", [P, 1], i32)
        hits = sb("hits", [P, TILES, NE], bf16)
        cnt = sb("cnt", [P, NE])
        eb1 = sb("eb1", [P, 2, HB])

        mamba_room = ExitStack()
        outer, ctx = ctx, mamba_room
        mv = sb("mv", [P, CH, 2])
        st6 = sb("st6", [P, CH, 6])
        ve = sb("ve", [P, 2 * CH])
        rs = sb("rs", [P, 2 * CH])
        xin = sb("xin", [P, CH, D])
        xp = sb("xp", [P, CH, D])
        xn = sb("xn", [P, CH, D])
        xr3 = sb("xr3", [P, D])
        h = sb("h", [P, CH, D])
        xnT = sb("xnT", [P, KD, T])
        hT = sb("hT", [P, KD, T])
        xbuf = sb("xbuf", [P, 5, T + 4])
        u = sb("u", [P, 5, T])
        th = sb("th", [P, 2, T])
        Ct = sb("Ct", [64, T])
        dts = sb("dts", [P, 8, CH * 8])
        ex = sb("ex", [P, 3, CH * 8])
        dtv = sb("dtv", [P, 3, CH * 8])
        S = sb("S", [64, DI])
        thz = sb("thz", [P, DI])
        zs = sb("zs", [P, 2, DI])
        R = sb("R", [P, 8 * P])
        E = sb("E", [P, 2, 8 * P])
        Gm = sb("Gm", [P, 2, P])
        Xsb = sb("Xsb", [P, 2, DI])
        Xdt = sb("Xdt", [P, 2, DI])
        Xs = sb("Xs", [P, 2, DI])
        XD = sb("XD", [P, 2, DI])
        Bs = sb("Bs", [P, 2, 64])
        yb = sb("yb", [P, 2, DI])
        junk = sb("junk", [P, DI], bf16)
        ssq = sb("ssq", [P, 2 * CH])
        ry = sb("ry", [P, 2 * CH])
        yT = sb("yT", [P, CH, P])
        x2 = sb("x2", [P, CH, D])
        tg = sb("tg", [P, CH, LEAVES])
        lp = sb("lp", [P, 2, CH, LEAVES // 2])
        leaf = sb("leaf", [P, CH, LEAVES])
        lT = sb("lT", [P, KD, T])
        h2T = sb("h2T", [P, KD, T])
        xb = sb("xb", [P, CH, D])
        tt = sb("tt", [P, 2, T])
        am = sb("am", [P, HB, T])
        wq, wrT, lvT, woT = (am[:, k, :].rearrange("p (k n) -> p k n", k=KD) for k in range(4))
        nst = sb("nst", [P, 6])
        nmv = sb("nmv", [P, CH, 2])
        nve = sb("nve", [P, CH])
        nrs = sb("nrs", [P, CH])
        xo = sb("xo", [P, CH, D])
        nT = sb("nT", [P, KD, T])
        sm = sb("sm", [P, 3, CH])
        sx = sb("sx", [P, 2, CH, NE])

        mamba_room.close()
        ctx = outer
        eb2 = sb("eb2", [P, 2, D])
        GE = sb("GE", [P, 2, NE, TILES])
        incl = sb("incl", [P, 2, NE, TILES])
        totS = sb("totS", [P, 2, NE, TILES])
        posx = sb("posx", [P, 2, NE, TILES])
        reset = sb("reset", [P, 2, NE, TILES])
        sel = sb("sel", [P, NE, TILES])
        slot = sb("slot", [P, NE, TILES])
        sloti = sb("sloti", [P, NE, TILES], i32)
        hii = sb("hii", [P, NE, TILES], i32)
        loi = sb("loi", [P, NE, TILES], i32)
        hif = sb("hif", [P, NE, TILES])
        lof = sb("lof", [P, NE, TILES])
        need = sb("need", [P, NE])
        iotaf = sb("iotaf", [P, P])
        iotab = sb("iotab", [P, P], bf16)
        pidx = sb("pidx", [P, 1])
        tidx = sb("tidx", [P, NE, TILES])
        oh8 = sb("oh8", [P, NE * TILES, 8])
        OHR = sb("OHR", [P, NE * TILES, 16], bf16)
        OL = sb("OL", [P, 4, P], bf16)
        idxf = sb("idxf", [P, NE, 16])
        IDX = sb("IDX", [P, NE * 8], u32)
        idxc = sb("idxc", [P, 4, 4], u32)
        xg = sb("xg", [P, 2, 4, ROW])
        xT = sb("xT", [P, KD, T])
        eam = sb("eam", [P, 2, HB, T])
        gcol = sb("gcol", [P, 2, 4])
        ye = sb("ye", [P, 2, 4, D])

        bank = [ctx.enter_context(nc.psum_tensor(f"bank{k}", [P, 512], fp32)) for k in range(8)]
        FRONT, BACK = bank[0:2], bank[2:4]
        SEG, INTRA, YO, MISC = bank[4:8]
        CUM = MISC[:, 0:96]
        GP = MISC[:, 128:256]
        BTP = MISC[:, 256:320]
        CNT = MISC[:, 384:392]

        xnT_d = nc.dram_tensor("xnT_d", [STEPS, P, KD, T], fp32).ap()
        x1_d = nc.dram_tensor("x1_d", [NT, D], fp32).ap()
        rows_d = nc.dram_tensor("rows_d", [NT, ROW], fp32).ap()
        x_rows = d["L0_attn_x"].rearrange("b t d -> (b t) d")
        out_rows = out.rearrange("b t d -> (b t) d")

        x_loaded = sig("x_loaded", 16)
        w_loaded = sem("w_loaded")
        wide_loaded = sem("wide_loaded")
        consts = sem("consts")
        prep = Chain(sem("prep"), 0)
        prepped = sem("prepped")
        fused_full = sem("fused_full")
        a_exp = sem("a_exp")
        pool_prep = sem("pool_prep")
        phase = sem("phase")
        places = sem("places")

        class Signals:
            pass

        sets = []
        for L in LAYERS:
            s, n = Signals(), L.name + "_"
            half = len(L.front) // 2
            s.f_full = [sig(n + f"front_full{k}", half) for k in range(2)]
            s.seg_full = sig(n + "seg_full", CH * L.segs)
            s.intra_full = sig(n + "intra_full", CH)
            s.yo_full = sig(n + "yo_full", 2 * CH)
            s.cum_full, s.ex = sig(n + "cum_full"), sig(n + "decay_exps")
            s.g_full, s.gm = sig(n + "g_full", CH), sig(n + "g_masked", CH)
            s.v = sig(n + "dt_read")
            s.t1 = sig(n + "inter_read", CH)
            s.bs = sig(n + "b_rows_ready", CH)
            s.hT = sig(n + "hT_ready", 2 if L.tree else 16)
            s.e_in, s.e_out = sig(n + "dt_exp_in"), sig(n + "dt_exp_out")
            s.a = sig(n + "decay_log_ready")
            s.w_end = sig(n + "dt_to_end_ready")
            s.xb = sig(n + "proj_ready", 5)
            s.halo = sig(n + "halo_kept", 5)
            s.u = sig(n + "conv_ready", 5)
            s.th = sig(n + "conv_tanh", 5)
            s.xc = sig(n + "conv_silu", 6)
            s.thz = sig(n + "z_tanh", CH)
            s.zs = sig(n + "z_silu", CH)
            s.R = sig(n + "decay_terms", CH)
            s.E = sig(n + "decays", CH * L.segs)
            s.M = sig(n + "mask_ready", CH * L.segs)
            s.xsb = sig(n + "x_rows_ready", CH)
            s.xdt = sig(n + "x_dt_ready", CH)
            s.xs = sig(n + "x_end_ready", CH)
            s.xd = sig(n + "x_D_ready", CH)
            s.S = sig(n + "state_ready", CH + 1)
            s.y0 = sig(n + "y_sum_ready", CH)
            s.yg = sig(n + "y_gated", CH)
            s.ssq = sig(n + "y_squares", CH)
            s.ry = sig(n + "y_rms", CH)
            s.yT = sig(n + "yT_ready", CH)
            s.x2 = sig(n + "mixed", CH)
            sets.append(s)
        mv_sig = sig("var_ready")
        rs_sig = sig("rstd_ready")
        xn_sig = sig("xn_ready", CH)
        h_sig = sig("h_ready", CH)
        kept_sig = sig("xn3_kept")
        xnT_sig = sig("xnT_ready", 2)
        tg_sig = sig("gate_tanh", 2)
        leaf_sig = sig("leaves_ready")
        lT_sig = sig("leavesT_ready", 2)
        b_full = [sig(f"back_full{k}", len(LAYERS[0].back) // 2) for k in range(2)]
        sq2 = sig("x2_squares", CH)
        r2_sig = sig("x2_rms")
        h2_sig = sig("h2_ready", CH)
        h2T_sig = sig("h2T_ready", 2)
        xb_sig = sig("residual_ready")
        act2 = sig("up_tanh", 2 * HB)
        am_sig = sig("up_silu", HB)
        x1_sig = sig("x1_ready", CH)
        rt_sig = sig("router_read", 2)
        nve_sig = sig("next_var", CH)
        nrs_sig = sig("next_rstd", CH)
        xo_sig = sig("next_xn", CH)
        nT_sig = sig("next_xnT", 2)
        smx_sig = sig("router_shifted")
        sme_sig = sig("router_exp")
        sc_sig = sig("scores_ready")
        rows_stored = sig("rows_stored", 16)
        x1_stored = sig("x1_stored", 16)
        xp_sig = sig("x_residual_ready")
        nT_stored = sig("nT_stored", 16)
        sc_stored = sig("scores_stored", 16)
        out_stored = sig("mixed_stored", 16 * CH)
        x1_loaded = sig("x1_loaded", 16)

        cnt_sig = sig("hits_counted", CH)
        ph0 = sem("first_count")
        rt_chain = sem("routing_steps")
        ge_ready, pre_full, idx_full, idx_ready = (sem(n) for n in ("above_ready", "prefix_full", "slots_full", "index_ready"))
        iotas = sem("iotas")
        ol_ready = sig("onehot_ready", TILES)
        ol_used = sig("onehot_used", TILES)
        HS = 4
        idxc_sig = sig("index_copied", HS)
        gathered = [sig(f"gathered{q}", 64 * HS // 2) for q in range(2)]
        xt_full = sig("tokensT_full", 2 * HS)
        xt_sig = sig("tokensT_ready", 2 * HS)
        eup_full = sig("e_up_full", HB * HS)
        gelu_sig = sig("gelu_ready", HB * HS)
        edown_full = sig("e_down_full", 4 * HS)
        gcol_sig = sig("gates_ready", HS)
        edown_read = sig("e_down_read", 4 * HS)
        ye_sig = sig("weighted_ready", 4 * HS)
        scattered = [sig(f"scattered{q}", 64 * HS // 2) for q in range(2)]
        ew_loaded = [sig(f"expert_loaded{j}", 64) for j in range(2)]

        def apart(eng):
            eng.sem_inc(places, 1)

        def front_use(L, name):
            n = L.front.index(name)
            return n % 2, n // 2

        def back_use(name):
            n = LAYERS[0].back.index(name)
            return n % 2, n // 2

        def front_wait(eng, L, s, i, name):
            k, m = front_use(L, name)
            wait(eng, s.f_full[k], i, m + 1)
            return FRONT[k]

        def back_wait(eng, b, name):
            k, m = back_use(name)
            wait(eng, b_full[k], b, m + 1)
            return BACK[k]

        def front_reader(s, name):
            kind, n = name.rstrip("0123"), int(name[-1]) if name[-1].isdigit() else 0
            return {"xnT": (xnT_sig, n + 1), "hT": (s.hT, n + 1), "dt": (s.v, 1), "gate": (tg_sig, n + 1),
                    "bc": (s.xb, 1), "x": (s.xb, n + 2), "z": (s.zs, n + 1), "xt": (s.xsb, n + 1),
                    "inter": (s.t1, n + 1), "state": (s.S, n + 2)}[kind]

        def back_reader(name):
            kind, n = name.rstrip("01234567"), int(name[-1])
            return {"h2T": (h2T_sig, n + 1), "lT": (lT_sig, n + 1), "up": (act2, 2 * n + 2),
                    "down": (x1_sig, n + 1), "nT": (nT_sig, n + 1), "rt": (rt_sig, n + 1)}[
                        "h2T" if name.startswith("h2T") else kind]

        def open_front(pe, L, s, i, name):
            n = L.front.index(name)
            before, step = (L.front[n - 2], i) if n >= 2 else (L.front[n - 2], i - 1)
            signal, count = front_reader(s, before)
            wait(pe, signal, step, count)
            return FRONT[n % 2]

        def open_back(pe, b, name):
            use = LAYERS[0].back
            n = use.index(name)
            before, step = (use[n - 2], b) if n >= 2 else (use[n - 2], b - 1)
            signal, count = back_reader(before)
            wait(pe, signal, step, count)
            return BACK[n % 2]

        def filled(ins, s, L, name):
            ins.then_inc(s.f_full[front_use(L, name)[0]].sem, 1)

        def back_filled(ins, name):
            ins.then_inc(b_full[back_use(name)[0]].sem, 1)

        block = ctx.enter_context(nc.Block())

        @block.sync
        def _(sp):
            def load(dst, src, s, n=16):
                sp.dma_start(dst, src).then_inc(s, 16)

            def rows(name, n):
                return d[name].partition_broadcast(P)

            def load_x(i):
                wait(sp, h_sig, i, 0)
                wait(sp, xp_sig, i, 0)
                sp.dma_start(xin[:, :, :], x_rows[bass.ds(T * i, T), :].rearrange("(c p) d -> p c d", p=P)
                             ).then_inc(x_loaded.sem, 16)

            load_x(0)
            load(n1w[:, :], d["n1w"], w_loaded)
            for k, L in enumerate(LAYERS):
                w, n = W[k], L.name
                load(w["z"][:, :, :], d[n + "_wz"].rearrange("(k p) n -> p k n", p=P), w_loaded)
                load(w["x"][:, :, :], d[n + "_wx"].rearrange("(k p) n -> p k n", p=P), w_loaded)
                load(w["bc"][:, :, :], d[n + "_wbc"].rearrange("(k p) n -> p k n", p=P), w_loaded)
                load(w["dt"][:, :, :], d[n + "_wdt"].rearrange("(k p) n -> p k n", p=P), w_loaded)
                load(w["conv"][:, :, :], d[n + "_conv"], w_loaded)
                load(w["dtb"][:, :], rows(n + "_dtb", L.heads), w_loaded)
                load(w["A"][:, :], rows(n + "_alog", L.heads), w_loaded)
                load(w["D"][:, :], rows(n + "_D", L.heads), w_loaded)
                load(w["out"][:, :, :], d[n + "_wo"].rearrange("(k p) n -> p k n", p=P), w_loaded)
                load(w["gn"][:, :], d[n + "_gn"], w_loaded)
                if k == 0:
                    load(wq, d["wq"].rearrange("(k p) n -> p k n", p=P), w_loaded)
                    load(wrT, d["routersT"].rearrange("(k p) n -> p k n", p=P), w_loaded)
                    load(lvT, d["leafT"].rearrange("(k p) n -> p k n", p=P), w_loaded)
                    load(woT, d["treeoutT"].rearrange("(k p) n -> p k n", p=P), w_loaded)
                    load(w1, d["w1"].rearrange("(k p) n -> p k n", p=P), w_loaded)
                    load(w2, d["w2"].rearrange("(k p) n -> p k n", p=P), w_loaded)
                    load(n2w[:, :], d["n2w"], w_loaded)
                    load(wr[:, :, :], d["wr"].rearrange("(k p) n -> p k n", p=P), w_loaded)
                    load(b1[:, :], d["b1"], w_loaded)
                    load(b2[:, 0, :], rows("b2", D), w_loaded)
                    load(b2[:, 1, :], rows("treeb", D), w_loaded)

            def store_back(b):
                wait(sp, xo_sig, b, CH)
                sp.dma_start(rows_d[bass.ts(b, T), 0:D].rearrange("(c p) d -> p c d", p=P),
                             xo[:, :, :]).then_inc(rows_stored.sem, 16)
                sp.dma_start(x1_d[bass.ds(T * b, T), :].rearrange("(c p) d -> p c d", p=P),
                             xb[:, :, :]).then_inc(x1_stored.sem, 16)
                wait(sp, nT_sig, b, 2)
                sp.dma_start(xnT_d[b], nT[:, :, :]).then_inc(nT_stored.sem, 16)
                wait(sp, sc_sig, b, 1)
                sp.dma_start(rows_d[bass.ts(b, T), D:ROW].rearrange("(c p) d -> p c d", p=P),
                             SC[:, bass.ts(b, CH), :]).then_inc(sc_stored.sem, 16)

            load_x(1)
            load_x(2)
            store_back(0)
            with sp.Fori(1, STEPS - 2) as b:
                load_x(b + 2)
                store_back(b)
            store_back(STEPS - 2)
            store_back(STEPS - 1)
            for s in (rows_stored, nT_stored, sc_stored, x1_stored):
                sp.wait_ge(s.sem, 16 * STEPS)
            sp.wait_ge(phase, 4)
            sp.drain().then_inc(phase, 1)

            s = sets[1]

            def load_hT(i):
                front_wait(sp, LAYERS[1], s, i - 1, "z3")
                sp.dma_start(hT[:, :, :], xnT_d[i]).then_inc(s.hT.sem, 16)

            def store_out(b, c):
                wait(sp, s.x2, b, c + 1)
                sp.dma_start(out_rows[bass.ds(b * T + c * P, P), :], x2[:, c, :]).then_inc(out_stored.sem, 16)

            def load_x1(i):
                wait(sp, s.x2, i, 0)
                sp.dma_start(xin[:, :, :], x1_d[bass.ds(T * i, T), :].rearrange("(c p) d -> p c d", p=P)
                             ).then_inc(x1_loaded.sem, 16)

            def load_expert(e, j):
                sl = bass.ds(e, 1)
                for dst, src in (
                        (EW[:, j, 0:KD * HID].rearrange("p (k n) -> p k n", k=KD),
                         d["e_w1"][sl].rearrange("a (k p) n -> p (a k) n", p=P)),
                        (EW[:, j, KD * HID:].rearrange("p (k n) -> p k n", k=HB),
                         d["e_w2"][sl].rearrange("a (k p) n -> p (a k) n", p=P)),
                        (eb1[:, j, :], d["e_b1"][sl].rearrange("a p n -> p (a n)"))):
                    sp.dma_start(dst, src).then_inc(ew_loaded[j].sem, 16)

            def load_expert_b2(e, j):
                sp.dma_start(eb2[:, j, :], d["e_b2"][bass.ds(e, 1), :].rearrange("a n -> (a n)")
                             .partition_broadcast(P)).then_inc(ew_loaded[j].sem, 16)

            load_hT(0)
            load_x1(0)
            load_expert(0, 0)
            with sp.Fori(1, STEPS) as i:
                for c in range(CH - 1):
                    store_out(i - 1, c)
                load_hT(i)
                store_out(i - 1, CH - 1)
                load_x1(i)
            for c in range(CH):
                store_out(STEPS - 1, c)
            sp.wait_ge(out_stored.sem, out_stored.per * STEPS)
            sp.wait_ge(phase, 9)
            sp.drain().then_inc(phase, 1)
            load_expert_b2(0, 0)
            load_expert(1, 1)
            load_expert_b2(1, 1)

            def next_experts(i):
                for j in range(2):
                    wait(sp, edown_full, i - 1, 4 * (2 * j + 2))
                    wait(sp, edown_read, i - 1, 4 * (2 * j + 2))
                    load_expert(2 * i + j, j)
                    load_expert_b2(2 * i + j, j)

            with sp.Fori(1, NE // 2) as i:
                next_experts(i)
            for q in range(2):
                sp.wait_ge(scattered[q].sem, scattered[q].per * NE // 2)

        pool0 = Chain(sem("pool_front0"), 23)
        poolb = Chain(sem("pool_back0"), 2)
        pool1 = Chain(sem("pool_front1"), 7)
        poolb1 = Chain(sem("pool_back1"), 1)

        @block.gpsimd
        def _(pool):
            g = nc.gpsimd
            g.memset(ident[:, :], 0.0).then_inc(consts, 1)
            g.memset(triU[:, :], 1.0).then_inc(consts, 1)
            g.memset(strL[:, :], 1.0).then_inc(consts, 1)
            g.memset(ones[:, :], 1.0).then_inc(consts, 1)
            g.memset(flags[:, :], 1.0).then_inc(consts, 1)
            g.memset(nhalf[:, :], -0.5).then_inc(consts, 1)
            pool.wait_ge(consts, 6)
            g.affine_select(out=ident[:, :], in_=ident[:, :], compare_op=ALU.not_equal, fill=1.0, base=0,
                            pattern=[[-1, P]], channel_multiplier=1).then_inc(consts, 1)
            g.affine_select(out=triU[:, :], in_=triU[:, :], compare_op=ALU.is_ge, fill=0.0, base=0,
                            pattern=[[1, P]], channel_multiplier=-1).then_inc(consts, 1)
            g.affine_select(out=strL[:, :], in_=strL[:, :], compare_op=ALU.is_ge, fill=0.0, base=-1,
                            pattern=[[-1, P]], channel_multiplier=1).then_inc(consts, 1)
            for q in range(0, STEPS + 1, STEPS // NB):
                g.memset(flags[:, q:q + 1], 0.0).then_inc(consts, 1)

            def rstd(i):
                wait(pool, mv_sig, i, 1)
                wait(pool, h_sig, i, 0)
                g.tensor_tensor(rs[:, :], ve[:, :], nhalf[:, 0:8], ALU.pow).then_inc(rs_sig.sem, 1)

            def terms(L, s, i, c, ch):
                wait(pool, s.a, i, 1)
                wait(pool, s.seg_full, i, c * L.segs)
                nh = L.heads
                v = R[:, 0:nh * P].rearrange("p (h t) -> p h t", h=nh)
                a = dtv[:, 1, c * nh:(c + 1) * nh].unsqueeze(2).to_broadcast([P, nh, P])
                g.tensor_tensor(v, triU[:, :].unsqueeze(1).to_broadcast([P, nh, P]), a,
                                ALU.mult).then_inc(s.R.sem, 1)

            def xrows(L, s, i, c):
                nh, hp, q = L.heads, L.hp, c % 2
                wait(pool, s.xsb, i, c + 1)
                wait(pool, s.w_end, i, 1)
                if c >= 2:
                    front_wait(pool, L, s, i, f"state{c-2}")
                else:
                    front_wait(pool, L, s, i - 1, f"state{c+2}")
                x3 = Xsb[:, q, :].rearrange("p (h e) -> p h e", h=nh)
                g.tensor_tensor(Xs[:, q, :].rearrange("p (h e) -> p h e", h=nh), x3,
                                dtv[:, 2, c * nh:(c + 1) * nh].unsqueeze(2).to_broadcast([P, nh, hp]),
                                ALU.mult).then_inc(s.xs.sem, 1)
                g.tensor_tensor(XD[:, q, :].rearrange("p (h e) -> p h e", h=nh), x3,
                                W[LAYERS.index(L)]["D"][:, :].unsqueeze(2).to_broadcast([P, nh, hp]),
                                ALU.mult).then_inc(s.xd.sem, 1)

            def gated(L, s, i, c, ch):
                q = c % 2
                wait(pool, s.y0, i, c + 1)
                wait(pool, s.xd, i, c + 1)
                ch.put(g.tensor_tensor(yb[:, q, :], yb[:, q, :], XD[:, q, :], ALU.add))
                ch.see(pool)
                wait(pool, s.zs, i, c + 1)
                g.tensor_tensor(yb[:, q, :], yb[:, q, :], zs[:, q, :], ALU.mult).then_inc(s.yg.sem, 1)

            def y_rms(L, s, i, c, ch):
                wait(pool, s.ssq, i, c + 1)
                wait(pool, s.x2, i, c - 3)
                apart(pool)
                ch.put(g.tensor_scalar(ry[:, c:c + 1], ssq[:, c:c + 1], 1.0 / DI, 1e-5, ALU.mult, ALU.add))
                ch.see(pool)
                g.tensor_tensor(ry[:, c:c + 1], ry[:, c:c + 1], nhalf[:, 0:1], ALU.pow).then_inc(s.ry.sem, 1)

            def back_rms(b, ch):
                wait(pool, sets[0].x2, b, CH)
                wait(pool, x1_stored, b, 0)
                wait(pool, xo_sig, b, 0)
                g.tensor_tensor(xb[:, :, :], x2[:, :, :], xp[:, :, :], ALU.add).then_inc(xb_sig.sem, 1)
                wait(pool, sq2, b, CH)
                wait(pool, h2_sig, b, 0)
                apart(pool)
                ch.put(g.tensor_scalar(ry[:, CH:], ssq[:, CH:], 1.0 / D, 1e-6, ALU.mult, ALU.add))
                ch.see(pool)
                g.tensor_tensor(ry[:, CH:], ry[:, CH:], nhalf[:, 0:CH], ALU.pow).then_inc(r2_sig.sem, 1)

            def tree(i, ch):
                wait(pool, tg_sig, i, 2)
                apart(pool)
                ch.put(g.tensor_scalar(tg[:, :, :], tg[:, :, :], 0.5, 0.5, ALU.mult, ALU.add))
                ch.see(pool)
                n = 1
                src = None
                while n < LEAVES:
                    last = 2 * n == LEAVES
                    dst = (leaf[:, :, :] if last else lp[:, (n.bit_length()) % 2, :, 0:2 * n]
                           ).rearrange("p c (n two) -> p c n two", two=2)
                    gn = tg[:, :, n - 1:2 * n - 1]
                    if last:
                        back_wait(pool, i - 1, "lT1")
                    if n == 1:
                        apart(pool)
                        ch.put(g.tensor_copy(dst[:, :, :, 1], gn))
                        ch.put(g.tensor_scalar(dst[:, :, :, 0], gn, -1.0, 1.0, ALU.mult, ALU.add))
                    else:
                        ch.put(g.tensor_tensor(dst[:, :, :, 1], src, gn, ALU.mult))
                        ch.see(pool)
                        left = g.tensor_tensor(dst[:, :, :, 0], src, dst[:, :, :, 1], ALU.subtract)
                        if last:
                            left.then_inc(leaf_sig.sem, 1)
                        else:
                            ch.put(left)
                    ch.see(pool)
                    if not last:
                        src = lp[:, (n.bit_length()) % 2, :, 0:2 * n]
                    n *= 2

            def next_rstd(b, c):
                wait(pool, nve_sig, b, c + 1)
                wait(pool, xo_sig, b, c - 3)
                g.tensor_tensor(nrs[:, c:c + 1], nve[:, c:c + 1], nhalf[:, 0:1], ALU.pow).then_inc(nrs_sig.sem, 1)

            def step0(f, b, n):
                L, s = LAYERS[0], sets[0]
                if f is not None:
                    pool0.begin(f)
                    terms(L, s, f, 0, pool0)
                if b is not None:
                    poolb.begin(b)
                    y_rms(L, s, b, 3, poolb)
                if f is not None:
                    wait(pool, xn_sig, f, CH)
                    wait(pool, s.x2, f, 0)
                    apart(pool)
                    g.tensor_copy(xr3[:, :], xn[:, CH - 1, :]).then_inc(kept_sig.sem, 1)
                if b is not None:
                    back_rms(b, poolb)
                if f is not None:
                    wait(pool, x_loaded, f, 16)
                    g.tensor_tensor(xp[:, :, :], xin[:, :, :],
                                    b2[:, 0, :].unsqueeze(1).to_broadcast([P, CH, D]), ALU.add).then_inc(xp_sig.sem, 1)
                    xrows(L, s, f, 0)
                    for c in range(CH):
                        if c + 1 < CH:
                            terms(L, s, f, c + 1, pool0)
                            xrows(L, s, f, c + 1)
                        gated(L, s, f, c, pool0)
                        if c:
                            y_rms(L, s, f, c - 1, pool0)
                    tree(f, pool0)
                if b is not None:
                    for c in range(CH):
                        next_rstd(b, c)
                    poolb.end()
                if f is not None:
                    if n is not None:
                        rstd(n)
                    pool0.end()

            rstd(0)
            pool.wait_ge(w_loaded, 16 * W0)
            g.tensor_tensor(b2[:, 0, :], b2[:, 0, :], b2[:, 1, :], ALU.add).then_inc(pool_prep, 1)
            pool.wait_ge(pool_prep, 1)
            step0(0, None, 1)
            step0(1, 0, 2)
            with pool.Fori(2, STEPS - 1) as i:
                step0(i, i - 1, i + 1)
            step0(STEPS - 1, STEPS - 2, None)
            step0(None, STEPS - 1, None)
            pool.drain().then_inc(phase, 1)
            pool.wait_ge(phase, 5)

            def step1(f, b):
                L, s = LAYERS[1], sets[1]
                if f is not None:
                    pool1.begin(f)
                    terms(L, s, f, 0, pool1)
                if b is not None:
                    poolb1.begin(b)
                    y_rms(L, s, b, 3, poolb1)
                    poolb1.end()
                if f is not None:
                    xrows(L, s, f, 0)
                    for c in range(CH):
                        if c + 1 < CH:
                            terms(L, s, f, c + 1, pool1)
                            xrows(L, s, f, c + 1)
                        gated(L, s, f, c, pool1)
                        if c:
                            y_rms(L, s, f, c - 1, pool1)
                    pool1.end()

            step1(0, None)
            step1(1, 0)
            with pool.Fori(2, STEPS) as i:
                step1(i, i - 1)
            step1(None, STEPS - 1)
            pool.drain().then_inc(phase, 1)
            pool.wait_ge(phase, 10)

            g.iota(iotaf[:, :], pattern=[[1, P]], base=0, channel_multiplier=0,
                   allow_small_or_imprecise_dtypes=True).then_inc(iotas, 1)
            g.iota(pidx[:, :], pattern=[[1, 1]], base=0, channel_multiplier=1,
                   allow_small_or_imprecise_dtypes=True).then_inc(iotas, 1)
            g.iota(tidx[:, :, :], pattern=[[0, NE], [1, TILES]], base=0, channel_multiplier=0,
                   allow_small_or_imprecise_dtypes=True).then_inc(iotas, 1)
            g.memset(reset[:, :, :, :], 1.0).then_inc(iotas, 1)
            pool.wait_ge(iotas, 4)
            g.memset(reset[:, :, :, 0:1], 0.0).then_inc(iotas, 1)
            pool.wait_ge(idx_ready, 1)

            def gather(i, s):
                k, q = s % HS, s % 2
                if s >= HS:
                    i, s = i + 1, s - HS
                wait(pool, scattered[q], i, 64 * (s // 2 - 1))
                apart(pool)
                g.tensor_copy(idxc[:, k, :], IDX[:, bass.ds(i * 16 + s * 4, 4)]).then_inc(idxc_sig.sem, 1)
                wait(pool, idxc_sig, i, s + 1)
                wait(pool, xt_full, i, 2 * (s - 1))
                wait(pool, gcol_sig, i, s - 1)
                apart(pool)
                for j in range(4):
                    g.indirect_dma_start(out=xg[:, q, j, :], out_offset=None, in_=rows_d,
                                         in_offset=bass.IndirectOffsetOnAxis(ap=idxc[:, k, j:j + 1], axis=0)
                                         ).then_inc(gathered[q].sem, 16)

            def scatter(i, s):
                wait(pool, scattered[s % 2], i, 64 * (s // 2))
                if s % 2 == 0:
                    wait(pool, scattered[1], i, 64 * (s // 2))
                for j in range(4):
                    wait(pool, ye_sig, i, 4 * s + j + 1)
                    apart(pool)
                    g.indirect_dma_start(out=out_rows, out_offset=bass.IndirectOffsetOnAxis(
                        ap=idxc[:, s, j:j + 1], axis=0), in_=ye[:, s % 2, j, :], in_offset=None,
                        compute_op=ALU.add).then_inc(scattered[s % 2].sem, 16)

            gather(0, 0)
            gather(0, 1)

            def estep(i, more):
                for s in range(HS):
                    if more or s < 2:
                        gather(i, s + 2)
                    scatter(i, s)

            estep(0, True)
            with pool.Fori(1, NE // 2 - 1) as i:
                estep(i, True)
            estep(NE // 2 - 1, False)
            for q in range(2):
                pool.wait_ge(scattered[q].sem, scattered[q].per * NE // 2)

        @block.scalar
        def _(act):
            a = nc.scalar

            act.wait_ge(w_loaded, 16 * W0)
            for w in W:
                a.activation(w["A"][:, :], w["A"][:, :], ACT.Exp).then_inc(a_exp, 1)

            def head(L, s, i):
                if L.tree:
                    for k in range(KD):
                        p = front_wait(act, L, s, i, f"xnT{k}")
                        wait(act, s.f_full[front_use(L, "gate1")[0]], i - 1, front_use(L, "gate1")[1] + 1)
                        ins = a.activation(xnT[:, k, :], p[:, :], ACT.Copy)
                        ins.then_inc(xnT_sig.sem, 1)
                    for k in range(KD):
                        p = front_wait(act, L, s, i, f"hT{k}")
                        wait(act, s.f_full[front_use(L, "z3")[0]], i - 1, front_use(L, "z3")[1] + 1)
                        a.activation(hT[:, k, :], p[:, :], ACT.Copy).then_inc(s.hT.sem, 1)
                wait(act, s.e_in, i, 1)
                n = CH * L.heads
                a.activation(dts[:, 1, 0:n], dts[:, 1, 0:n], ACT.Exp).then_inc(s.e_out.sem, 1)
                if L.tree:
                    wait(act, leaf_sig, i, 0)
                    for k in range(2):
                        p = front_wait(act, L, s, i, f"gate{k}")
                        ins = a.activation(tg[:, 2 * k:2 * k + 2, :], p[:, :].rearrange("p (c n) -> p c n", c=2),
                                           ACT.Tanh, scale=0.5)
                        ins.then_inc(tg_sig.sem, 1)
                names = ["bc", "x0", "x1", "x2", "x3"]
                for j in range(6):
                    if j < 5:
                        blk = (j - 1) % 5
                        p = front_wait(act, L, s, i, names[j])
                        wait(act, s.halo, i - 1, j + 1)
                        a.activation(xbuf[:, blk, L.halo:L.halo + T], p[:, :], ACT.Copy).then_inc(s.xb.sem, 1)
                    if j >= 1:
                        blk = (j - 2) % 5
                        wait(act, s.u, i, j)
                        wait(act, s.xc, i, j - 1)
                        a.activation(th[:, (j - 1) % 2, :], u[:, blk, :], ACT.Tanh).then_inc(s.th.sem, 1)
                wait(act, s.cum_full, i, 1)
                a.activation(ex[:, :, 0:n], CUM.rearrange("p (j n) -> p j n", j=3)[:, :, 0:n],
                             ACT.Exp).then_inc(s.ex.sem, 1)

            def chunk(L, s, i, c):
                q = c % 2
                p = front_wait(act, L, s, i, f"z{c}")
                wait(act, s.zs, i, c)
                a.activation(thz[:, :], p[:, :], ACT.Tanh).then_inc(s.thz.sem, 1)
                p = front_wait(act, L, s, i, f"xt{c}")
                wait(act, s.xdt, i, c - 1)
                wait(act, s.xd, i, c - 1)
                a.activation(Xsb[:, q, :], p[:, :], ACT.Copy).then_inc(s.xsb.sem, 1)
                wait(act, s.intra_full, i, c - 1)
                for j in range(L.segs):
                    wait(act, s.seg_full, i, c * L.segs + j + 1)
                    a.activation(E[:, q, 512 * j:512 * (j + 1)], SEG[:, :], ACT.Exp).then_inc(s.E.sem, 1)

            def square(L, s, i, c):
                wait(act, s.yg, i, c + 1)
                wait(act, s.ssq, i, c)
                if L.tree and c == 0:
                    wait(act, sq2, i, 0)
                a.activation(junk[:, :], yb[:, c % 2, :], ACT.Square,
                             accum_out=ssq[:, c:c + 1]).then_inc(s.ssq.sem, 1)

            def transposed(L, s, i, c):
                wait(act, s.yo_full, i, 2 * c + 1)
                a.activation(yT[:, :, :], YO[:, :].rearrange("p (k t) -> p k t", k=CH),
                             ACT.Copy).then_inc(s.yT.sem, 1)

            def square2(b, c):
                wait(act, sets[0].x2, b, c + 1)
                if c == 0:
                    wait(act, sets[0].ssq, b, CH)
                wait(act, sq2, b, c)
                a.activation(junk[:, 0:D], x2[:, c, :], ACT.Square,
                             accum_out=ssq[:, CH + c:CH + c + 1]).then_inc(sq2.sem, 1)

            def up(b, k):
                p = back_wait(act, b, f"up{k}")
                wait(act, am_sig, b, k - 1)
                back_wait(act, b - 1, "down3")
                a.activation(am[:, k, :], p[:, :], ACT.Identity, bias=b1[:, k:k + 1]).then_inc(act2.sem, 1)
                ins = a.activation(tt[:, k % 2, :], p[:, :], ACT.Tanh, bias=b1[:, k:k + 1])
                ins.then_inc(act2.sem, 1)

            def step0(f, b):
                L, s = LAYERS[0], sets[0]
                if f is not None:
                    head(L, s, f)
                if b is not None:
                    square(L, s, b, 3)
                    transposed(L, s, b, 3)
                    for c in range(CH - 1):
                        square2(b, c)
                if f is not None:
                    chunk(L, s, f, 0)
                if b is not None:
                    square2(b, CH - 1)
                    for k in range(KD):
                        p = back_wait(act, b, f"lT{k}")
                        back_wait(act, b - 1, "down3")
                        a.activation(lT[:, k, :], p[:, :], ACT.Copy).then_inc(lT_sig.sem, 1)
                    for k in range(KD):
                        p = back_wait(act, b, f"h2T{k}")
                        back_wait(act, b - 1, "up7")
                        a.activation(h2T[:, k, :], p[:, :], ACT.Copy).then_inc(h2T_sig.sem, 1)
                for c in range(CH):
                    if b is not None:
                        up(b, 2 * c)
                        up(b, 2 * c + 1)
                    if f is not None:
                        if c + 1 < CH:
                            chunk(L, s, f, c + 1)
                        if c:
                            square(L, s, f, c - 1)
                            transposed(L, s, f, c - 1)
                if b is not None:
                    for k in range(2):
                        p = back_wait(act, b, f"nT{k}")
                        back_wait(act, b - 1, "rt1")
                        wait(act, nT_stored, b, 0)
                        a.activation(nT[:, :, 2 * P * k:2 * P * (k + 1)],
                                     p[:, :].rearrange("p (k n) -> p k n", k=KD), ACT.Copy).then_inc(nT_sig.sem, 1)
                    wait(act, smx_sig, b, 1)
                    a.activation(sx[:, 1, :, :], sx[:, 0, :, :], ACT.Exp).then_inc(sme_sig.sem, 1)

            step0(0, None)
            step0(1, 0)
            with act.Fori(2, STEPS) as i:
                step0(i, i - 1)
            step0(None, STEPS - 1)
            act.drain().then_inc(phase, 1)
            act.wait_ge(phase, 5)

            def step1(f, b):
                L, s = LAYERS[1], sets[1]
                if f is not None:
                    head(L, s, f)
                if b is not None:
                    square(L, s, b, 3)
                    transposed(L, s, b, 3)
                if f is not None:
                    chunk(L, s, f, 0)
                    for c in range(CH):
                        if c + 1 < CH:
                            chunk(L, s, f, c + 1)
                        if c:
                            square(L, s, f, c - 1)
                            transposed(L, s, f, c - 1)

            step1(0, None)
            step1(1, 0)
            with act.Fori(2, STEPS) as i:
                step1(i, i - 1)
            step1(None, STEPS - 1)
            act.drain().then_inc(phase, 1)
            act.wait_ge(phase, 10)

            def estep(i):
                for s in range(HS):
                    for k in range(KD):
                        wait(act, xt_full, i, 2 * s + k + 1)
                        wait(act, eup_full, i, HB * s)
                        a.activation(xT[:, k, :], bank[k][:, :], ACT.Copy).then_inc(xt_sig.sem, 1)
                    for k in range(HB):
                        wait(act, eup_full, i, HB * s + k + 1)
                        wait(act, edown_full, i, 4 * (s - 1))
                        a.activation(eam[:, s % 2, k, :], bank[2 + k % 2][:, :], ACT.Gelu,
                                     bias=eb1[:, s // 2, k:k + 1]).then_inc(gelu_sig.sem, 1)

            estep(0)
            with act.Fori(1, NE // 2) as i:
                estep(i)

        dve0 = Chain(sem("dve_front0"), DF0)
        dven = Chain(sem("dve_norm"), DN)
        dveb = Chain(sem("dve_back0"), DB0)
        dve1 = Chain(sem("dve_front1"), DF1)

        @block.vector
        def _(dve):
            v = nc.vector

            dve.wait_ge(w_loaded, 16 * W0)
            count = 0

            def scale(out_, factor, second=None):
                nonlocal count
                v.tensor_scalar(out_, out_, factor, second, ALU.mult,
                                ALU.mult if second is not None else ALU.bypass).then_inc(prepped, 1)
                count += 1

            for L, w in zip(LAYERS, W):
                for k in range(KD):
                    if L.tree:
                        scale(w["z"][:, k, :], n1w[:, k:k + 1], 0.5)
                        for n in ("x", "bc", "dt"):
                            scale(w[n][:, k, :], n1w[:, k:k + 1])
                        scale(w1[:, k, :], n2w[:, k:k + 1], 0.5)
                    else:
                        scale(w["z"][:, k, :], 0.5)
                scale(w["conv"][:, :, :], 0.5)
                for k in range(CH):
                    scale(w["out"][:, k, :], w["gn"][:, k:k + 1])
            scale(b1[:, :], 0.5)
            dve.wait_ge(a_exp, 2)
            for w in W:
                scale(w["A"][:, :], -1.0)
            v.memset(S[:, :], 0.0).then_inc(prepped, 1)
            v.memset(Ct[:, :], 0.0).then_inc(prepped, 1)
            v.memset(xbuf[:, :, 0:4], 0.0).then_inc(prepped, 1)
            v.memset(Bs[:, :, :], 0.0).then_inc(prepped, 1)
            count += 4
            dve.wait_ge(fused_full, 1)
            for k in range(KD):
                v.tensor_copy(wg[:, k, :], BACK[k][:, 0:LEAVES]).then_inc(prepped, 1)
                v.tensor_copy(wv[:, k, :], BACK[k][:, LEAVES:2 * LEAVES]).then_inc(prepped, 1)
                count += 2
            assert count == PREPPED, count
            dve.wait_ge(prepped, PREPPED)
            dve.wait_ge(consts, 9 + NB + 1)

            def norm(i):
                dven.begin(i)
                wait(dve, x_loaded, i, 16)
                for c in range(CH):
                    dven.put(v.bn_stats(st6[:, c, :], xin[:, c, :]))
                dven.see(dve)
                wait(dve, rs_sig, i, 0)
                apart(dve)
                for c in range(CH):
                    dven.put(v.bn_aggr(mv[:, c, :], st6[:, c, :]))
                dven.see(dve)
                dven.put(v.tensor_scalar(ve[:, 0:CH], mv[:, :, 1], 1e-5, None, ALU.add))
                v.tensor_scalar(ve[:, CH:], mv[:, :, 1], 1.0 + 1e-6, 1e-11, ALU.mult,
                                ALU.add).then_inc(mv_sig.sem, 1)
                dven.end()

            def softplus(L, s, i, ch, part):
                n, nh = CH * L.heads, L.heads
                w = W[LAYERS.index(L)]
                t = [dts[:, k, 0:n] for k in range(8)]

                def op(ins):
                    ch.put(ins)
                    ch.see(dve)

                if part == 0:
                    p = front_wait(dve, L, s, i, "dt")
                    v3 = t[0].rearrange("p (c h) -> p c h", c=CH)
                    v.tensor_tensor(v3, p[:, 0:n].rearrange("p (c h) -> p c h", c=CH),
                                    w["dtb"][:, :].unsqueeze(1).to_broadcast([P, CH, nh]),
                                    ALU.add).then_inc(s.v.sem, 1)
                    wait(dve, s.v, i, 1)
                    v.scalar_tensor_tensor(out=t[1], in0=t[0], scalar=-1.0, in1=t[0], op0=ALU.mult,
                                           op1=ALU.min).then_inc(s.e_in.sem, 1)
                    return
                wait(dve, s.e_out, i, 1)
                op(v.tensor_scalar(t[2], t[1], 2.0, None, ALU.add))
                op(v.reciprocal(t[3], t[2]))
                op(v.tensor_tensor(t[2], t[1], t[3], ALU.mult))
                op(v.tensor_tensor(t[3], t[2], t[2], ALU.mult))
                op(v.tensor_scalar(t[4], t[3], 1.0 / 17, None, ALU.mult))
                for k in (15, 13, 11, 9, 7, 5, 3):
                    op(v.scalar_tensor_tensor(out=t[4], in0=t[4], scalar=1.0 / k, in1=t[3], op0=ALU.add,
                                              op1=ALU.mult))
                op(v.scalar_tensor_tensor(out=t[5], in0=t[4], scalar=1.0, in1=t[2], op0=ALU.add, op1=ALU.mult))
                op(v.tensor_scalar(t[6], t[0], 0.0, 0.5, ALU.max, ALU.mult))
                op(v.tensor_tensor(t[5], t[5], t[6], ALU.add))
                wait(dve, s.seg_full, i, 0)
                op(v.tensor_scalar(dtv[:, 0, 0:n], t[5], 2.0, None, ALU.mult))
                op(v.tensor_tensor(t[7].rearrange("p (c h) -> p c h", c=CH),
                                   dtv[:, 0, 0:n].rearrange("p (c h) -> p c h", c=CH),
                                   w["A"][:, :].unsqueeze(1).to_broadcast([P, CH, nh]), ALU.mult))
                v.tensor_scalar(dtv[:, 1, 0:n], t[7], LIM, None, ALU.max).then_inc(s.a.sem, 1)

            def conv(L, s, i, j, ch):
                blk = (j - 1) % 5
                w = W[LAYERS.index(L)]["conv"]
                wait(dve, s.xb, i, j + 1)
                if j == 0:
                    front_wait(dve, L, s, i - 1, "xt3")
                    wait(dve, s.g_full, i - 1, CH)
                ch.put(v.tensor_scalar(u[:, blk, :], xbuf[:, blk, 0:T], w[:, blk, 0:1],
                                       w[:, blk, L.taps:L.taps + 1], ALU.mult, ALU.add))
                for k in range(1, L.taps):
                    ch.see(dve)
                    ins = v.scalar_tensor_tensor(out=u[:, blk, :], in0=xbuf[:, blk, k:k + T],
                                                 scalar=w[:, blk, k:k + 1], in1=u[:, blk, :], op0=ALU.mult,
                                                 op1=ALU.add)
                    if k < L.taps - 1:
                        ch.put(ins)
                    else:
                        ins.then_inc(s.u.sem, 1)
                v.tensor_scalar(xbuf[:, blk, 0:L.halo], xbuf[:, blk, T:T + L.halo],
                                flags[:, bass.ds(i + 1, 1)], None, ALU.mult).then_inc(s.halo.sem, 1)

            def silu(L, s, i, j, ch):
                blk = (j - 1) % 5
                wait(dve, s.th, i, j + 1)
                if j == 0:
                    n, cp = L.state, L.cpart
                    v.scalar_tensor_tensor(out=Ct[0:n, :], in0=th[cp:cp + n, 0, :], scalar=1.0,
                                           in1=u[cp:cp + n, 4, :], op0=ALU.add,
                                           op1=ALU.mult).then_inc(s.xc.sem, 1)
                    v.scalar_tensor_tensor(out=u[0:n, 4, :], in0=th[0:n, 0, :], scalar=1.0,
                                           in1=u[0:n, 4, :], op0=ALU.add, op1=ALU.mult).then_inc(s.xc.sem, 1)
                else:
                    v.scalar_tensor_tensor(out=u[:, blk, :], in0=th[:, j % 2, :], scalar=1.0, in1=u[:, blk, :],
                                           op0=ALU.add, op1=ALU.mult).then_inc(s.xc.sem, 1)

            def head(L, s, i, ch):
                if L.tree:
                    wait(dve, rs_sig, i, 1)
                    for c in range(CH):
                        if c == 0:
                            front_wait(dve, L, s, i - 1, "xnT1")
                            wait(dve, kept_sig, i, 0)
                        v.tensor_scalar(xn[:, c, :], xin[:, c, :], mv[:, c, 0:1], rs[:, c:c + 1],
                                        ALU.subtract, ALU.mult).then_inc(xn_sig.sem, 1)
                    front_wait(dve, L, s, i - 1, "hT1")
                    for c in range(CH):
                        v.tensor_scalar(h[:, c, :], xin[:, c, :], mv[:, c, 0:1],
                                        rs[:, CH + c:CH + c + 1], ALU.subtract, ALU.mult).then_inc(h_sig.sem, 1)
                softplus(L, s, i, ch, 0)
                conv(L, s, i, 0, ch)
                softplus(L, s, i, ch, 1)
                for j in range(1, 5):
                    conv(L, s, i, j, ch)
                    silu(L, s, i, j - 1, ch)
                silu(L, s, i, 4, ch)
                n = CH * L.heads
                wait(dve, s.ex, i, 1)
                wait(dve, s.xs, i, 0)
                v.tensor_tensor(dtv[:, 2, 0:n], dtv[:, 0, 0:n], ex[:, 1, 0:n], ALU.mult).then_inc(s.w_end.sem, 1)
                v.tensor_scalar(S[:, :], S[:, :], flags[0:64, bass.ds(i, 1)], None,
                                ALU.mult).then_inc(s.S.sem, 1)

            def chunk(L, s, i, c, ch):
                q, nh, hp = c % 2, L.heads, L.hp
                k, _ = front_use(L, f"z{c}")
                wait(dve, s.thz, i, c + 1)
                wait(dve, s.yg, i, c - 1)
                v.scalar_tensor_tensor(out=zs[:, q, :], in0=thz[:, :], scalar=1.0, in1=FRONT[k][:, :],
                                       op0=ALU.add, op1=ALU.mult).then_inc(s.zs.sem, 1)
                wait(dve, s.g_full, i, c + 1)
                if not L.tree:
                    threshold(i, c, ch)
                v.tensor_tensor(Gm[:, q, :], GP, triU[:, :], ALU.mult).then_inc(s.gm.sem, 1)
                if c >= 2:
                    front_wait(dve, L, s, i, f"state{c-2}")
                else:
                    front_wait(dve, L, s, i - 1, f"state{c+2}")
                v.tensor_copy(Bs[:, q, 0:L.state], BTP[:, 0:L.state]).then_inc(s.bs.sem, 1)
                wait(dve, s.xsb, i, c + 1)
                wait(dve, s.intra_full, i, c - 1)
                v.tensor_tensor(Xdt[:, q, :].rearrange("p (h e) -> p h e", h=nh),
                                Xsb[:, q, :].rearrange("p (h e) -> p h e", h=nh),
                                dtv[:, 0, c * nh:(c + 1) * nh].unsqueeze(2).to_broadcast([P, nh, hp]),
                                ALU.mult).then_inc(s.xdt.sem, 1)
                wait(dve, s.gm, i, c + 1)
                for j in range(L.segs):
                    wait(dve, s.E, i, c * L.segs + j + 1)
                    e3 = E[:, q, 512 * j:512 * (j + 1)].rearrange("p (h t) -> p h t", h=4)
                    v.tensor_tensor(e3, e3, Gm[:, q, :].unsqueeze(1).to_broadcast([P, 4, P]),
                                    ALU.mult).then_inc(s.M.sem, 1)

            def sums(L, s, i, c, ch):
                q, nh, hp, n = c % 2, L.heads, L.hp, 64
                ex3 = ex[:, :, c * nh:(c + 1) * nh]
                p = front_wait(dve, L, s, i, f"inter{c}")
                if c >= 2:
                    wait(dve, s.ssq, i, c - 1)
                    wait(dve, s.yo_full, i, 2 * (c - 2) + 1)
                else:
                    wait(dve, s.ssq, i - 1, c + 3)
                    wait(dve, s.yo_full, i - 1, 2 * (c + 2) + 1)
                v.tensor_tensor(yb[:, q, :].rearrange("p (h e) -> p h e", h=nh),
                                p[:, :].rearrange("p (h e) -> p h e", h=nh),
                                ex3[:, 0, :].unsqueeze(2).to_broadcast([P, nh, hp]),
                                ALU.mult).then_inc(s.t1.sem, 1)
                wait(dve, s.S, i, c + 1)
                s3 = S[:, :].rearrange("p (h e) -> p h e", h=nh)
                ch.put(v.tensor_tensor(s3, s3, ex3[0:n, 2, :].unsqueeze(2).to_broadcast([n, nh, hp]), ALU.mult))
                wait(dve, s.t1, i, c + 1)
                wait(dve, s.intra_full, i, c + 1)
                v.tensor_tensor(yb[:, q, :], yb[:, q, :], INTRA[:, :], ALU.add).then_inc(s.y0.sem, 1)
                p = front_wait(dve, L, s, i, f"state{c}")
                ch.see(dve)
                v.tensor_tensor(S[:, :], S[:, :], p[0:n, :], ALU.add).then_inc(s.S.sem, 1)

            def mixed0(s, i, c):
                wait(dve, s.yo_full, i, 2 * c + 2)
                wait(dve, s.ry, i, c + 1)
                if c == 0:
                    back_wait(dve, i - 1, "h2T1")
                v.scalar_tensor_tensor(out=x2[:, c, :], in0=YO[:, 0:D], scalar=ry[:, c:c + 1],
                                       in1=xr3[:, :] if c == CH - 1 else xn[:, c, :], op0=ALU.mult,
                                       op1=ALU.add).then_inc(s.x2.sem, 1)

            def step0(n, f, b):
                L, s = LAYERS[0], sets[0]
                if f is not None:
                    dve0.begin(f)
                    head(L, s, f, dve0)
                if b is not None:
                    dveb.begin(b)
                    wait(dve, kept_sig, b, 1)
                    mixed0(s, b, CH - 1)
                if f is not None:
                    chunk(L, s, f, 0, dve0)
                if b is not None:
                    wait(dve, r2_sig, b, 1)
                    wait(dve, xb_sig, b, 1)
                    for c in range(CH):
                        v.tensor_scalar(x2[:, c, :], x2[:, c, :], ry[:, CH + c:CH + c + 1], None,
                                        ALU.mult).then_inc(h2_sig.sem, 1)
                for c in range(CH):
                    if b is not None:
                        for k in (2 * c, 2 * c + 1):
                            wait(dve, act2, b, 2 * k + 2)
                            v.scalar_tensor_tensor(out=am[:, k, :], in0=tt[:, k % 2, :], scalar=1.0,
                                                   in1=am[:, k, :], op0=ALU.add,
                                                   op1=ALU.mult).then_inc(am_sig.sem, 1)
                    if f is not None:
                        if c + 1 < CH:
                            chunk(L, s, f, c + 1, dve0)
                        sums(L, s, f, c, dve0)
                        if c:
                            mixed0(s, f, c - 1)
                if f is not None:
                    dve0.end()
                if n is not None:
                    norm(n)
                if b is not None:
                    wait(dve, xb_sig, b, 1)
                    for c in range(CH):
                        p = back_wait(dve, b, f"down{c}")
                        v.tensor_tensor(xb[:, c, :], p[:, 0:D], xb[:, c, :], ALU.add).then_inc(x1_sig.sem, 1)
                        wait(dve, x1_sig, b, c + 1)
                        dveb.put(v.bn_stats(nst[:, 0:6], xb[:, c, :]))
                        dveb.see(dve)
                        wait(dve, xo_sig, b, c - 3)
                        apart(dve)
                        dveb.put(v.bn_aggr(nmv[:, c, :], nst[:, 0:6]))
                        dveb.see(dve)
                        wait(dve, nrs_sig, b, c - 3)
                        v.tensor_scalar(nve[:, c:c + 1], nmv[:, c, 1:2], 1e-5, None,
                                        ALU.add).then_inc(nve_sig.sem, 1)
                    back_wait(dve, b - 1, "nT1")
                    wait(dve, rows_stored, b, 0)
                    for c in range(CH):
                        wait(dve, nrs_sig, b, c + 1)
                        v.tensor_scalar(xo[:, c, :], xb[:, c, :],
                                        nmv[:, c, 0:1], nrs[:, c:c + 1], ALU.subtract,
                                        ALU.mult).then_inc(xo_sig.sem, 1)
                    for k in range(2):
                        p = back_wait(dve, b, f"rt{k}")
                        v.tensor_copy(sx[:, 0, 2 * k:2 * k + 2, :],
                                      p[:, 0:2 * NE].rearrange("p (c e) -> p c e", c=2)).then_inc(rt_sig.sem, 1)
                    wait(dve, rt_sig, b, 2)
                    dveb.put(v.tensor_reduce(sm[:, 0, :], sx[:, 0, :, :], AXX, ALU.max))
                    dveb.see(dve)
                    v.tensor_tensor(sx[:, 0, :, :], sx[:, 0, :, :],
                                    sm[:, 0, :].unsqueeze(2).to_broadcast([P, CH, NE]),
                                    ALU.subtract).then_inc(smx_sig.sem, 1)
                    wait(dve, sme_sig, b, 1)
                    dveb.put(v.tensor_reduce(sm[:, 1, :], sx[:, 1, :, :], AXX, ALU.add))
                    dveb.see(dve)
                    dveb.put(v.reciprocal(sm[:, 2, :], sm[:, 1, :]))
                    dveb.see(dve)
                    v.tensor_tensor(SC[:, bass.ts(b, CH), :], sx[:, 1, :, :],
                                    sm[:, 2, :].unsqueeze(2).to_broadcast([P, CH, NE]),
                                    ALU.mult).then_inc(sc_sig.sem, 1)
                    dveb.end()

            norm(0)
            step0(1, 0, None)
            step0(2, 1, 0)
            with dve.Fori(2, STEPS - 1) as i:
                step0(i + 1, i, i - 1)
            step0(None, STEPS - 1, STEPS - 2)
            step0(None, None, STEPS - 1)
            dve.drain().then_inc(phase, 1)
            dve.wait_ge(phase, 5)

            v.memset(S[:, :], 0.0).then_inc(prepped, 1)
            v.memset(xbuf[:, :, 0:4], 0.0).then_inc(prepped, 1)
            dve.wait_ge(prepped, PREPPED + 2)

            v.memset(thr[:, :], 0).then_inc(prepped, 1)
            v.memset(bit[:, :], 1 << 30).then_inc(prepped, 1)
            v.memset(cand[:, :], 1 << 30).then_inc(prepped, 1)
            dve.wait_ge(prepped, PREPPED + 5)
            v.tensor_tensor(hits[:, :, :], SC[:, :, :],
                            cand[:, :].bitcast(fp32).unsqueeze(1).to_broadcast([P, TILES, NE]),
                            ALU.is_ge).then_inc(ph0, 1)
            dve.wait_ge(ph0, 1)
            v.tensor_reduce(cnt[:, :], hits[:, :, :].rearrange("p t e -> p e t"), AXX, ALU.add).then_inc(ph0, 1)

            def threshold(i, c, ch):
                ch.put(v.tensor_scalar(okm[:, :], CNT, float(CAP), -1.0, ALU.is_ge, ALU.mult))
                ch.see(dve)
                ch.put(v.scalar_tensor_tensor(out=thr[:, :], in0=okm[:, :], scalar=bit[:, 0:1], in1=thr[:, :],
                                              op0=ALU.bitwise_and, op1=ALU.bitwise_or))
                ch.see(dve)
                ch.put(v.tensor_scalar(bit[:, :], bit[:, :], 1, None, ALU.logical_shift_right))
                ch.see(dve)
                ch.put(v.tensor_scalar(cand[:, :], thr[:, :], bit[:, 0:1], None, ALU.bitwise_or))
                ch.see(dve)
                ch.put(v.tensor_tensor(hits[:, :, :], SC[:, :, :],
                                       cand[:, :].bitcast(fp32).unsqueeze(1).to_broadcast([P, TILES, NE]),
                                       ALU.is_ge))
                ch.see(dve)
                v.tensor_reduce(cnt[:, :], hits[:, :, :].rearrange("p t e -> p e t"), AXX,
                                ALU.add).then_inc(cnt_sig.sem, 1)

            def mixed1(s, i, c):
                wait(dve, s.yo_full, i, 2 * c + 2)
                wait(dve, s.ry, i, c + 1)
                wait(dve, out_stored, i - 1, 16 * (c + 1))
                wait(dve, x1_loaded, i, 16)
                v.scalar_tensor_tensor(out=x2[:, c, :], in0=YO[:, 0:D], scalar=ry[:, c:c + 1],
                                       in1=xin[:, c, :],
                                       op0=ALU.mult, op1=ALU.add).then_inc(s.x2.sem, 1)

            def step1(f, b):
                L, s = LAYERS[1], sets[1]
                if f is not None:
                    dve1.begin(f)
                    head(L, s, f, dve1)
                if b is not None:
                    mixed1(s, b, CH - 1)
                if f is not None:
                    chunk(L, s, f, 0, dve1)
                    for c in range(CH):
                        if c + 1 < CH:
                            chunk(L, s, f, c + 1, dve1)
                        sums(L, s, f, c, dve1)
                        if c:
                            mixed1(s, f, c - 1)
                    dve1.end()

            step1(0, None)
            step1(1, 0)
            with dve.Fori(2, STEPS) as i:
                step1(i, i - 1)
            step1(None, STEPS - 1)
            dve.drain().then_inc(phase, 1)
            dve.wait_ge(phase, 10)

            steps = 0

            def link(ins):
                nonlocal steps
                steps += 1
                ins.then_inc(rt_chain, 1)
                dve.wait_ge(rt_chain, steps)

            SCe = SC[:, :, :].rearrange("p t e -> p e t")
            thrb = thr[:, :].bitcast(fp32).unsqueeze(2).to_broadcast([P, NE, TILES])
            link(v.tensor_tensor(GE[:, 0, :, :], SCe, thrb, ALU.is_gt))
            v.tensor_tensor(GE[:, 1, :, :], SCe, thrb, ALU.is_equal).then_inc(ge_ready, 1)
            flat = "p a e t -> p (a e t)"
            dve.wait_ge(iotas, 5)
            dve.wait_ge(ge_ready, 1)
            v.tensor_copy(iotab[:, :], iotaf[:, :]).then_inc(iotas, 1)
            dve.wait_ge(iotas, 6)
            dve.wait_ge(pre_full, 2)
            link(v.tensor_copy(totS[:, :, :, :].rearrange(flat), bank[1][:, :]))
            link(v.tensor_tensor_scan(incl[:, :, :, :].rearrange(flat), reset[:, :, :, :].rearrange(flat),
                                      totS[:, :, :, :].rearrange(flat), 0.0, ALU.mult, ALU.add))
            link(v.tensor_tensor(posx[:, :, :, :].rearrange(flat), bank[0][:, :],
                                 incl[:, :, :, :].rearrange(flat), ALU.add))
            link(v.tensor_tensor(posx[:, :, :, :], posx[:, :, :, :], totS[:, :, :, :], ALU.subtract))
            link(v.tensor_tensor(posx[:, :, :, :], posx[:, :, :, :], GE[:, :, :, :], ALU.subtract))
            link(v.tensor_scalar(need[:, :], incl[:, 0, :, TILES - 1], -1.0, float(CAP), ALU.mult, ALU.add))
            needb = need[:, :].unsqueeze(2).to_broadcast([P, NE, TILES])
            link(v.tensor_tensor(sel[:, :, :], posx[:, 1, :, :], needb, ALU.is_lt))
            link(v.tensor_tensor(sel[:, :, :], sel[:, :, :], GE[:, 1, :, :], ALU.mult))
            link(v.tensor_tensor(sel[:, :, :], sel[:, :, :], GE[:, 0, :, :], ALU.add))
            link(v.tensor_tensor(slot[:, :, :], posx[:, 1, :, :], needb, ALU.min))
            link(v.tensor_tensor(slot[:, :, :], slot[:, :, :], posx[:, 0, :, :], ALU.add))
            link(v.tensor_scalar(sel[:, :, :], sel[:, :, :], -float(NT), float(NT), ALU.mult, ALU.add))
            link(v.tensor_tensor(sloti[:, :, :], slot[:, :, :], sel[:, :, :], ALU.add))
            link(v.tensor_scalar(hii[:, :, :], sloti[:, :, :], 7, None, ALU.logical_shift_right))
            link(v.tensor_scalar(loi[:, :, :], sloti[:, :, :], P - 1, None, ALU.bitwise_and))
            link(v.tensor_copy(hif[:, :, :], hii[:, :, :]))
            link(v.tensor_copy(lof[:, :, :], loi[:, :, :]))
            hi2 = hif[:, :, :].rearrange("p e t -> p (e t)")
            t2 = tidx[:, :, :].rearrange("p e t -> p (e t)")
            link(v.tensor_tensor(oh8[:, :, :], hi2.unsqueeze(2).to_broadcast([P, NE * TILES, 8]),
                                 iotaf[:, 0:8].unsqueeze(1).to_broadcast([P, NE * TILES, 8]), ALU.is_equal))
            link(v.tensor_scalar(OHR[:, :, 0:8], oh8[:, :, :], pidx[:, 0:1], None, ALU.mult))
            v.tensor_tensor(OHR[:, :, 8:16], oh8[:, :, :], t2.unsqueeze(2).to_broadcast([P, NE * TILES, 8]),
                            ALU.mult).then_inc(ge_ready, 1)

            def onehots(e):
                for k in range(TILES):
                    wait(dve, ol_used, e, k - 3)
                    v.tensor_scalar(OL[:, k % 4, :], iotab[:, :],
                                    lof[:, :, :].rearrange("p e t -> p (e t)")[:, bass.ds(e * TILES + k, 1)],
                                    None, ALU.is_equal).then_inc(ol_ready.sem, 1)

            onehots(0)
            with dve.Fori(1, NE) as e:
                onehots(e)
            dve.wait_ge(idx_full, 1)
            link(v.tensor_copy(idxf[:, :, :].rearrange("p e n -> p (e n)"), bank[2][:, 0:NE * 16]))
            v.scalar_tensor_tensor(out=IDX[:, :].rearrange("p (e n) -> p e n", e=NE), in0=idxf[:, :, 8:16],
                                   scalar=float(P), in1=idxf[:, :, 0:8], op0=ALU.mult,
                                   op1=ALU.add).then_inc(idx_ready, 1)

            def estep(i):
                for s in range(HS):
                    q = s % 2
                    wait(dve, gathered[q], i, 64 * (s // 2 + 1))
                    wait(dve, ye_sig, i, 4 * (s - 1))
                    v.tensor_copy(gcol[:, q, :].unsqueeze(2),
                                  xg[:, q, :, bass.ds(2 * i + D + s // 2, 1)]).then_inc(gcol_sig.sem, 1)
                    wait(dve, gcol_sig, i, s + 1)
                    for j in range(4):
                        wait(dve, edown_full, i, 4 * s + j + 1)
                        wait(dve, scattered[q], i, 64 * (s // 2))
                        v.tensor_tensor(ye[:, q, j, :], bank[4 + j][:, 0:D], eb2[:, s // 2, :],
                                        ALU.add).then_inc(edown_read.sem, 1)
                        wait(dve, edown_read, i, 4 * s + j + 1)
                        v.tensor_scalar(ye[:, q, j, :], ye[:, q, j, :], gcol[:, q, j:j + 1], None,
                                        ALU.mult).then_inc(ye_sig.sem, 1)

            estep(0)
            with dve.Fori(1, NE // 2) as i:
                estep(i)

        @block.tensor
        def _(pe):
            t = nc.tensor

            def mm(out_, lhsT, rhs, first=True, last=True):
                return t.matmul(out_, lhsT, rhs, start=first, stop=last)

            pe.wait_ge(w_loaded, 16 * W0)
            for k in range(KD):
                sl = slice(k * P, (k + 1) * P)
                for j in range(KD):
                    mm(BACK[k][:, 0:LEAVES], wq[:, j, sl], wrT[:, j, :], j == 0, j == KD - 1)
                for j in range(KD):
                    last = mm(BACK[k][:, LEAVES:2 * LEAVES], lvT[:, j, sl], woT[:, j, :], j == 0, j == KD - 1)
            last.then_inc(fused_full, 1)
            pe.wait_ge(consts, 9 + NB + 1)
            pe.wait_ge(prepped, PREPPED)

            def cols(c):
                return slice(c * P, (c + 1) * P)

            def head(L, s, i):
                w = W[LAYERS.index(L)]
                if L.tree:
                    for src, name, ready in ((xn, "xnT", xn_sig), (h, "hT", h_sig)):
                        for k in range(KD):
                            p = open_front(pe, L, s, i, f"{name}{k}")
                            for c in range(CH):
                                if k == 0:
                                    wait(pe, ready, i, c + 1)
                                last = t.transpose(p[:, cols(c)], src[:, c, cols(k)], ident[:, :])
                            filled(last, s, L, f"{name}{k}")
                wait(pe, s.hT, i, s.hT.per)
                n = L.heads
                p = open_front(pe, L, s, i, "dt")
                for c in range(CH):
                    for k in range(KD):
                        last = mm(p[:, c * n:(c + 1) * n], hT[:, k, cols(c)], w["dt"][:, k, :], k == 0, k == 1)
                filled(last, s, L, "dt")
                if L.tree:
                    wait(pe, xnT_sig, i, 2)
                    for g in range(2):
                        p = open_front(pe, L, s, i, f"gate{g}")
                        for c in range(2):
                            for k in range(KD):
                                last = mm(p[:, c * LEAVES:(c + 1) * LEAVES], xnT[:, k, cols(2 * g + c)],
                                          wg[:, k, :], k == 0, k == 1)
                        filled(last, s, L, f"gate{g}")
                for j, name in enumerate(("bc", "x0", "x1", "x2", "x3")):
                    p = open_front(pe, L, s, i, name)
                    for k in range(KD):
                        lhsT = w["bc"][:, k, :] if j == 0 else w["x"][:, k, cols(j - 1)]
                        last = mm(p[:, :], lhsT, hT[:, k, :], k == 0, k == 1)
                    filled(last, s, L, name)
                wait(pe, s.a, i, 1)
                wait(pe, s.bs, i, 0)
                m = CH * n
                for j, mat in enumerate((triU, strL, ones)):
                    last = mm(CUM[:, 32 * j:32 * j + m], mat[:, :], dtv[:, 1, 0:m])
                last.then_inc(s.cum_full.sem, 1)

            def chunk(L, s, i, c):
                w = W[LAYERS.index(L)]
                q = c % 2
                p = open_front(pe, L, s, i, f"z{c}")
                for k in range(KD):
                    last = mm(p[:, :], hT[:, k, cols(c)], w["z"][:, k, :], k == 0, k == 1)
                filled(last, s, L, f"z{c}")
                if c == 0:
                    wait(pe, s.xc, i, 6)
                p = open_front(pe, L, s, i, f"xt{c}")
                for k in range(CH):
                    last = t.transpose(p[:, cols(k)], u[:, k, cols(c)], ident[:, :])
                filled(last, s, L, f"xt{c}")
                n = L.state
                wait(pe, s.bs, i, c)
                if c == 0:
                    wait(pe, s.ex, i, 1)
                if not L.tree:
                    if isinstance(i, int) and i == 0 and c == 0:
                        pe.wait_ge(ph0, 2)
                    wait(pe, cnt_sig, i, c)
                    mm(CNT, ones[:, :], cnt[:, :])
                mm(GP, u[0:n, 4, cols(c)], Ct[0:n, cols(c)])
                t.transpose(BTP[:, 0:n], u[0:n, 4, cols(c)], ident[0:n, 0:n]).then_inc(s.g_full.sem, 1)
                wait(pe, s.R, i, c + 1)
                for j in range(L.segs):
                    wait(pe, s.E, i, c * L.segs + j)
                    mm(SEG[:, :], strL[:, :], R[:, 512 * j:512 * (j + 1)]).then_inc(s.seg_full.sem, 1)

            def recur(L, s, i, c):
                q, hp = c % 2, L.hp
                p = open_front(pe, L, s, i, f"inter{c}")
                wait(pe, s.S, i, c + 1)
                filled(mm(p[:, :], Ct[:, cols(c)], S[:, :]), s, L, f"inter{c}")
                p = open_front(pe, L, s, i, f"state{c}")
                wait(pe, s.bs, i, c + 1)
                wait(pe, s.xs, i, c + 1)
                filled(mm(p[0:64, :], Bs[:, q, :], Xs[:, q, :]), s, L, f"state{c}")
                wait(pe, s.y0, i, c)
                wait(pe, s.xdt, i, c + 1)
                for j in range(L.heads):
                    if j % 4 == 0:
                        wait(pe, s.M, i, c * L.segs + j // 4 + 1)
                    last = mm(INTRA[:, j * hp:(j + 1) * hp], E[:, q, j * P:(j + 1) * P],
                              Xdt[:, q, j * hp:(j + 1) * hp])
                last.then_inc(s.intra_full.sem, 1)

            def project(L, s, i, c):
                w = W[LAYERS.index(L)]
                wait(pe, s.yg, i, c + 1)
                wait(pe, s.x2, i, c)
                for k in range(CH):
                    last = t.transpose(YO[:, cols(k)], yb[:, c % 2, cols(k)], ident[:, :])
                last.then_inc(s.yo_full.sem, 1)
                wait(pe, s.yT, i, c + 1)
                for k in range(CH):
                    last = mm(YO[:, 0:D], yT[:, k, :], w["out"][:, k, :], k == 0, k == CH - 1)
                last.then_inc(s.yo_full.sem, 1)

            def step0(f, b):
                L, s = LAYERS[0], sets[0]
                if f is not None:
                    head(L, s, f)
                if b is not None:
                    project(L, s, b, CH - 1)
                if f is not None:
                    chunk(L, s, f, 0)
                if b is not None:
                    for src, name, ready, n in ((leaf, "lT", leaf_sig, 1), (x2, "h2T", h2_sig, CH)):
                        wait(pe, ready, b, n)
                        for k in range(KD):
                            p = open_back(pe, b, f"{name}{k}")
                            for c in range(CH):
                                last = t.transpose(p[:, cols(c)], src[:, c, cols(k)], ident[:, :])
                            back_filled(last, f"{name}{k}")
                for c in range(CH):
                    if b is not None:
                        wait(pe, h2T_sig, b, 2)
                        for j in (2 * c, 2 * c + 1):
                            p = open_back(pe, b, f"up{j}")
                            for k in range(KD):
                                last = mm(p[:, :], w1[:, k, cols(j)], h2T[:, k, :], k == 0, k == 1)
                            back_filled(last, f"up{j}")
                    if f is not None:
                        if c + 1 < CH:
                            chunk(L, s, f, c + 1)
                        recur(L, s, f, c)
                        if c:
                            project(L, s, f, c - 1)
                if b is not None:
                    wait(pe, am_sig, b, HB)
                    wait(pe, lT_sig, b, 2)
                    for c in range(CH):
                        p = open_back(pe, b, f"down{c}")
                        for k in range(KD):
                            mm(p[:, 0:D], lT[:, k, cols(c)], wv[:, k, :], k == 0, False)
                        for k in range(HB):
                            last = mm(p[:, 0:D], am[:, k, cols(c)], w2[:, k, :], False, k == HB - 1)
                        back_filled(last, f"down{c}")
                    for g in range(2):
                        p = open_back(pe, b, f"nT{g}")
                        wait(pe, xo_sig, b, 2 * g + 2)
                        for k in range(KD):
                            for c in range(2):
                                last = t.transpose(p[:, (2 * k + c) * P:(2 * k + c + 1) * P],
                                                   xo[:, 2 * g + c, cols(k)], ident[:, :])
                        back_filled(last, f"nT{g}")
                    for g in range(2):
                        p = open_back(pe, b, f"rt{g}")
                        wait(pe, nT_sig, b, g + 1)
                        for c in range(2):
                            for k in range(KD):
                                last = mm(p[:, c * NE:(c + 1) * NE], nT[:, k, cols(2 * g + c)], wr[:, k, :],
                                          k == 0, k == 1)
                        back_filled(last, f"rt{g}")

            step0(0, None)
            step0(1, 0)
            with pe.Fori(2, STEPS) as i:
                step0(i, i - 1)
            step0(None, STEPS - 1)
            pe.drain().then_inc(phase, 1)
            pe.wait_ge(phase, 5)

            def step1(f, b):
                L, s = LAYERS[1], sets[1]
                if f is not None:
                    head(L, s, f)
                if b is not None:
                    project(L, s, b, CH - 1)
                if f is not None:
                    chunk(L, s, f, 0)
                    for c in range(CH):
                        if c + 1 < CH:
                            chunk(L, s, f, c + 1)
                        recur(L, s, f, c)
                        if c:
                            project(L, s, f, c - 1)

            step1(0, None)
            step1(1, 0)
            with pe.Fori(2, STEPS) as i:
                step1(i, i - 1)
            step1(None, STEPS - 1)
            pe.drain().then_inc(phase, 1)
            pe.wait_ge(phase, 10)

            pe.wait_ge(ge_ready, 1)
            ge = GE[:, :, :, :].rearrange("p a e t -> p (a e t)")
            mm(bank[0][:, :], triU[:, :], ge).then_inc(pre_full, 1)
            mm(bank[1][:, :], ones[:, :], ge).then_inc(pre_full, 1)
            pe.wait_ge(ge_ready, 2)

            def slots(e):
                for k in range(TILES):
                    wait(pe, ol_ready, e, k + 1)
                    mm(bank[2][:, bass.ds(16 * e, 16)], OL[:, k % 4, :],
                       OHR[:, bass.ds(e * TILES + k, 1), :].rearrange("p a n -> p (a n)"), k == 0,
                       k == TILES - 1).then_inc(ol_used.sem, 1)

            slots(0)
            with pe.Fori(1, NE) as e:
                slots(e)
            pe.drain().then_inc(idx_full, 1)
            pe.wait_ge(idx_ready, 1)

            def tokens_up(i, s):
                q = s % 2
                wait(pe, gathered[q], i, 64 * (s // 2 + 1))
                for k in range(KD):
                    wait(pe, xt_sig, i, 2 * s + k - 1)
                    for c in range(4):
                        last = t.transpose(bank[k][:, cols(c)], xg[:, q, c, cols(k)], ident[:, :])
                    last.then_inc(xt_full.sem, 1)
                wait(pe, xt_sig, i, 2 * (s + 1))
                if s % 2 == 0:
                    wait(pe, ew_loaded[s // 2], i, 64)
                w = EW[:, s // 2, 0:KD * HID].rearrange("p (k n) -> p k n", k=KD)
                for j in range(HB):
                    wait(pe, gelu_sig, i, HB * s + j - 1)
                    for k in range(KD):
                        last = mm(bank[2 + j % 2][:, :], w[:, k, cols(j)], xT[:, k, :], k == 0, k == 1)
                    last.then_inc(eup_full.sem, 1)

            def down(i, s):
                wait(pe, gelu_sig, i, HB * (s + 1))
                w = EW[:, s // 2, KD * HID:].rearrange("p (k n) -> p k n", k=HB)
                for c in range(4):
                    wait(pe, edown_read, i, 4 * (s - 1) + c + 1)
                    for k in range(HB):
                        last = mm(bank[4 + c][:, 0:D], eam[:, s % 2, k, cols(c)], w[:, k, :], k == 0,
                                  k == HB - 1)
                    last.then_inc(edown_full.sem, 1)

            def estep(i):
                for s in range(HS):
                    tokens_up(i, s)
                    if s:
                        down(i, s - 1)
                    elif not (isinstance(i, int) and i == 0):
                        down(i - 1, HS - 1)

            estep(0)
            with pe.Fori(1, NE // 2) as i:
                estep(i)
            down(NE // 2 - 1, HS - 1)


def kernel(**inputs):
    import numpy as np
    import concourse.bacc as bacc
    from concourse.bass_utils import run_bass_kernel_spmd as run

    def arr(name):
        return np.ascontiguousarray(inputs[name])

    def spread(a, rows, width):
        o = np.zeros((width,) + a.shape[1:], a.dtype)
        for at, lo, hi in rows:
            o[at:at + hi - lo] = a[lo:hi]
        return o

    def columns(a):
        return np.ascontiguousarray(a.reshape(-1, P).T)

    h = {"L0_attn_x": arr("L0_attn_x")}
    win = {"m0": arr("L0_attn_W_in"), "m1": arr("L1_attn_in_proj_w").T}
    cw = {"m0": arr("L0_attn_conv_w"), "m1": arr("L1_attn_conv_w")[:, 0, :]}
    cb = {"m0": arr("L0_attn_conv_b"), "m1": arr("L1_attn_conv_b")}
    for L, pre in zip(LAYERS, ("L0_attn_", "L1_attn_")):
        n, w = L.name, win[L.name]
        s, at = L.state, 2 * DI
        place = [(0, 0, s), (L.cpart, s, 2 * s)]
        h[n + "_wz"] = w[:, 0:DI]
        h[n + "_wx"] = w[:, DI:at]
        h[n + "_wbc"] = spread(w[:, at:at + 2 * s].T, place, P).T
        h[n + "_wdt"] = w[:, at + 2 * s:]
        taps = np.concatenate([cw[n], cb[n][:, None]], axis=1)
        taps = np.concatenate([taps[0:DI], spread(taps[DI:], place, P)], axis=0)
        h[n + "_conv"] = taps.reshape(5, P, L.taps + 1).transpose(1, 0, 2)
        h[n + "_dtb"] = arr(pre + "dt_bias")
        h[n + "_alog"] = arr(pre + "A_log")
    h["m0_D"], h["m1_D"] = arr("L0_attn_D"), arr("L1_attn_D_param")
    h["m0_wo"], h["m1_wo"] = arr("L0_attn_W_out"), arr("L1_attn_out_proj_w").T
    h["m0_gn"], h["m1_gn"] = columns(arr("L0_attn_norm_gate_w")), columns(arr("L1_attn_norm_w"))
    h["n1w"], h["n2w"] = columns(arr("L0_attn_norm1_w")), columns(arr("L0_attn_norm2_w"))
    h["wq"] = arr("L0_ffn_Wq")
    h["routersT"] = spread(arr("L0_ffn_routers"), [(0, 0, LEAVES - 1)], LEAVES).T
    h["leafT"] = arr("L0_ffn_leaf_values").T
    h["treeoutT"] = arr("L0_ffn_Wout_w").T
    h["w1"], h["w2"] = arr("L0_attn_mlp_w1"), arr("L0_attn_mlp_w2")
    h["b1"], h["b2"], h["treeb"] = columns(arr("L0_attn_mlp_b1")), arr("L0_attn_mlp_b2"), arr("L0_ffn_Wout_b")
    h["wr"] = arr("L1_ffn_Wr")
    h["e_w1"], h["e_w2"] = arr("L1_ffn_W1"), arr("L1_ffn_W2")
    h["e_b1"] = arr("L1_ffn_b1").reshape(NE, HB, P).transpose(0, 2, 1)
    h["e_b2"] = arr("L1_ffn_b2")

    nc = bacc.Bacc("TRN2", target_bir_lowering=False, num_devices=1)
    arrays, d = {}, {}
    for name, a in h.items():
        a = np.ascontiguousarray(a)
        arrays[f"in_{name}"] = a
        d[name] = nc.dram_tensor(f"in_{name}", a.shape, mybir.dt.from_np(a.dtype), kind="ExternalInput").ap()
    out = nc.dram_tensor("out_0", (NB, SEQ, D), fp32, kind="ExternalOutput").ap()
    program(nc, d, out)
    r = run(nc, [arrays], core_ids=[0])
    return r.results[0]["out_0"]
```

```python
import concourse.bass as bass
from concourse import mybir
from contextlib import ExitStack

P = 128
D = 256
KD = D // P
DI = 512
T = 512
CH = 4
NB, SEQ = 2, 2048
NT = NB * SEQ
STEPS = NT // T
TILES = NT // P
NE = 8
HID = 1024
HB = HID // P
CAP = NT * 2 // NE
LEAVES = 256
ROW = D + NE
LIM = -110.0

fp32 = mybir.dt.float32
bf16 = mybir.dt.bfloat16
fp32r = mybir.dt.float32r
i32 = mybir.dt.int32
u32 = mybir.dt.uint32
ALU = mybir.AluOpType
ACT = mybir.ActivationFunctionType
AXX = mybir.AxisListType.X


W_FIRST, W_REST = 17, 15
PREPPED_FIRST, PREPPED = 22, 33
NORMED_AT = 2
EARLY_UPS, LATE_UPS = (0, 1, 2, 3), ((4,), (5,), (6,), (7,))
DF0, DN, DB0, DF1, DH1 = 11, 9, 11, 24, 12


class Signal:

    def __init__(self, sem, per, base=0):
        self.sem, self.per, self.base = sem, per, base

    def wait_ge(self, eng, step, n):
        value = step * self.per + n
        if isinstance(value, int) and value <= 0:
            return
        eng.wait_ge(self.sem, value + self.base if self.base else value)


def counted(signal, per):
    return Signal(signal.sem, per, signal.base + STEPS * signal.per)


class Chain:

    def __init__(self, sem, per, base=0):
        self.links, self.step, self.n = Signal(sem, per, base), None, 0

    def after(self, per):
        then = counted(self.links, per)
        return Chain(then.sem, per, then.base)

    def begin(self, step):
        self.step, self.n = step, 0

    def resume(self, step):
        self.step = step

    def put(self, ins):
        self.n += 1
        ins.then_inc(self.links.sem, 1)

    def see(self, eng, back=0):
        self.links.wait_ge(eng, self.step, self.n - back)

    def end(self):
        assert self.n == self.links.per, (self.n, self.links.per)


class Layer:

    def __init__(self, name, taps, state, heads, cpart, tree):
        self.name, self.taps, self.state, self.heads, self.cpart = name, taps, state, heads, cpart
        self.hp = DI // heads
        self.tree = tree
        self.halo = taps - 1
        self.blocks = ["bc", "x0", "x1", "x2", "x3"]
        self.segs = heads * P // 512
        head = ["dt"] + self.blocks
        if tree:
            head = ["xnT0", "xnT1", "hT0", "hT1"] + head + ["gate0", "gate1"]
        order = ["z0", "xt0"]
        for c in range(CH):
            if c + 1 < CH:
                order += [f"z{c+1}", f"xt{c+1}"]
            order += [f"inter{c}", f"state{c}"]
        self.front = head + order if tree else order
        self.head = [] if tree else head
        assert len(self.front) % 2 == 0 and len(self.head) % 2 == 0
        self.lag = 1 if tree else 2
        self.back = (["lT0", "lT1", "h2T0", "h2T1"] + [f"up{k}" for k in range(HB)]
                     + [f"down{c}" for c in range(CH)] + ["nT0", "nT1", "rt0", "rt1"]) if tree else []


LAYERS = [Layer("m0", 3, 16, 8, 32, True), Layer("m1", 4, 64, 4, 64, False)]


def program(nc, d, out):
    ctx = ExitStack()
    with ctx:
        def sb(name, shape, dt=fp32):
            return ctx.enter_context(nc.sbuf_tensor(name, shape, dt))

        def sem(name):
            return ctx.enter_context(nc.semaphore(name))

        def sig(name, per=1):
            return Signal(sem(name), per)

        SC = sb("SC", [P, TILES, NE])
        ident = sb("ident", [P, P])
        triU = sb("triU", [P, P])
        strL = sb("strL", [P, P])
        ones = sb("ones", [P, P])
        flags = sb("flags", [P, STEPS + 1])
        nhalf = sb("nhalf", [P, 8])
        W = []
        for L in LAYERS:
            w = {}
            n = L.name
            w["bc"] = sb(n + "wbc", [P, KD, P])
            w["dt"] = sb(n + "wdt", [P, KD, L.heads])
            w["conv"] = sb(n + "conv", [P, 5, L.taps + 1])
            w["dtb"] = sb(n + "dtb", [P, L.heads])
            w["A"] = sb(n + "A", [P, L.heads])
            w["D"] = sb(n + "D", [P, L.heads])
            w["gn"] = sb(n + "gn", [P, CH])
            W.append(w)
        n1w = sb("n1w", [P, KD])
        n2w = sb("n2w", [P, KD])
        wr = sb("wr", [P, KD, NE])
        EW = sb("EW", [P, 2, 2 * KD * HID])
        w1 = EW[:, 0, 0:KD * HID].rearrange("p (k n) -> p k n", k=KD)
        w2 = EW[:, 0, KD * HID:].rearrange("p (k n) -> p k n", k=HB)
        wg = EW[:, 1, 0:KD * LEAVES].rearrange("p (k n) -> p k n", k=KD)
        wv = EW[:, 1, 512:1024].rearrange("p (k n) -> p k n", k=KD)
        W0BIG = sb("m0big", [P, 3, KD * DI])
        for w, big in zip(W, (W0BIG[:, :, :], EW[:, 1, 1024:4096].rearrange("p (a n) -> p a n", a=3))):
            w["z"] = big[:, 0, :].rearrange("p (k n) -> p k n", k=KD)
            w["x"] = big[:, 1, :].rearrange("p (k n) -> p k n", k=KD)
            w["out"] = big[:, 2, :].rearrange("p (k n) -> p k n", k=CH)
        b1 = sb("b1", [P, HB])
        b2 = sb("b2", [P, 2, D])

        thr = sb("thr", [P, NE], i32)
        cand = sb("cand", [P, NE], i32)
        okm = sb("okm", [P, NE], i32)
        bit = sb("bit", [P, 1], i32)
        hits = sb("hits", [P, TILES, NE], bf16)
        cnt = sb("cnt", [P, NE])
        eb1 = sb("eb1", [P, 2, HB])

        mamba_room = ExitStack()
        outer, ctx = ctx, mamba_room
        mv = sb("mv", [P, CH, 2])
        st6 = sb("st6", [P, CH, 6])
        ve = sb("ve", [P, 2 * CH])
        rs = sb("rs", [P, 2 * CH])
        xin = sb("xin", [P, CH, D])
        xp = sb("xp", [P, CH, D])
        xn = sb("xn", [P, CH, D])
        xr3 = sb("xr3", [P, D])
        h = sb("h", [P, CH, D])
        xnT = sb("xnT", [P, KD, T])
        hT = sb("hT", [P, KD, T])
        xbuf = sb("xbuf", [P, 5, T + 4])
        u = sb("u", [P, 5, T])
        th = sb("th", [P, 2, T])
        Ct = sb("Ct", [64, T])
        dts = sb("dts", [P, 8, CH * 8])
        ex = sb("ex", [P, 3, CH * 8])
        dtv = sb("dtv", [P, 3, CH * 8])
        ex1 = sb("ex1", [P, 3, CH * 8])
        dtv1 = sb("dtv1", [P, 3, CH * 8])
        S = sb("S", [64, DI])
        thz = sb("thz", [P, DI])
        zs = sb("zs", [P, 2, DI])
        R = sb("R", [P, 8 * P])
        E = sb("E", [P, 2, 8 * P])
        Gm = sb("Gm", [P, 2, P])
        Xsb = sb("Xsb", [P, 2, DI])
        Xdt = sb("Xdt", [P, 2, DI])
        Xs = sb("Xs", [P, 2, DI])
        XD = sb("XD", [P, 2, DI])
        Bs = sb("Bs", [P, 2, 64])
        yb = sb("yb", [P, 2, DI])
        junk = sb("junk", [P, DI], bf16)
        ssq = sb("ssq", [P, 2 * CH])
        ry = sb("ry", [P, 2 * CH])
        yT = sb("yT", [P, CH, P])
        x2 = sb("x2", [P, CH, D])
        tg = sb("tg", [P, CH, LEAVES])
        lp = sb("lp", [P, 2, CH, LEAVES // 2])
        leaf = sb("leaf", [P, CH, LEAVES])
        lT = sb("lT", [P, KD, T])
        h2T = sb("h2T", [P, KD, T])
        xb = sb("xb", [P, CH, D])
        tt = sb("tt", [P, 2, T])
        am = sb("am", [P, HB, T])
        wq, wrT, lvT, woT = (am[:, k, :].rearrange("p (k n) -> p k n", k=KD) for k in range(4))
        nst = sb("nst", [P, 6])
        nmv = sb("nmv", [P, CH, 2])
        nve = sb("nve", [P, CH])
        nrs = sb("nrs", [P, CH])
        xo = sb("xo", [P, CH, D])
        nT = sb("nT", [P, KD, T])
        sm = sb("sm", [P, 3, CH])
        sx = sb("sx", [P, 2, CH, NE])

        mamba_room.close()
        ctx = outer
        eb2 = EW[:, 1, 2048:2048 + 2 * D].rearrange("p (q n) -> p q n", q=2)
        ye = EW[:, 1, 0:2048].rearrange("p (q c n) -> p q c n", q=2, c=4)
        idxf = sb("idxf", [P, NE, 16])
        IDX = sb("IDX", [P, NE * 8], u32)
        idxc = sb("idxc", [P, 4, 4], u32)
        xg = sb("xg", [P, 2, 4, ROW])
        gcol = sb("gcol", [P, 2, 4])
        EWh, EWl = (sb(n, [P, 2, 2 * KD * HID], fp32r) for n in ("EWh", "EWl"))
        xTh, xTl = (sb(n, [P, 2, KD, T], fp32r) for n in ("xTh", "xTl"))
        routing_room = ExitStack()
        ctx = routing_room
        GE = sb("GE", [P, 2, NE, TILES])
        incl = sb("incl", [P, 2, NE, TILES])
        totS = sb("totS", [P, 2, NE, TILES])
        posx = sb("posx", [P, 2, NE, TILES])
        reset = sb("reset", [P, 2, NE, TILES])
        sel = sb("sel", [P, NE, TILES])
        slot = sb("slot", [P, NE, TILES])
        sloti = sb("sloti", [P, NE, TILES], i32)
        hii = sb("hii", [P, NE, TILES], i32)
        loi = sb("loi", [P, NE, TILES], i32)
        hif = sb("hif", [P, NE, TILES])
        lof = sb("lof", [P, NE, TILES])
        need = sb("need", [P, NE])
        iotaf = sb("iotaf", [P, P])
        iotab = sb("iotab", [P, P], bf16)
        pidx = sb("pidx", [P, 1])
        tidx = sb("tidx", [P, NE, TILES])
        oh8 = sb("oh8", [P, NE * TILES, 8])
        OHR = sb("OHR", [P, NE * TILES, 16], bf16)
        OL = sb("OL", [P, 4, P], bf16)
        routing_room.close()
        ctx = outer
        am4 = W0BIG[:, 0:2, :].rearrange("p a (b n) -> p (a b) n", b=2)
        amh, aml = (sb(n, [P, 2, HB, T], fp32r) for n in ("amh", "aml"))

        bank = [ctx.enter_context(nc.psum_tensor(f"bank{k}", [P, 512], fp32)) for k in range(8)]
        FRONT, BACK = bank[0:2], bank[2:4]
        SEG, INTRA, YO, MISC = bank[4:8]
        CUM = MISC[:, 0:96]
        GP = MISC[:, 128:256]
        BTP = MISC[:, 256:320]
        CNT = MISC[:, 384:392]

        xnT_d = nc.dram_tensor("xnT_d", [STEPS, P, KD, T], fp32).ap()
        x1_d = nc.dram_tensor("x1_d", [NT, D], fp32).ap()
        rows_d = nc.dram_tensor("rows_d", [NT, ROW], fp32).ap()
        x_rows = d["L0_attn_x"].rearrange("b t d -> (b t) d")
        out_rows = out.rearrange("b t d -> (b t) d")

        x_loaded = sig("x_loaded", 16)
        w_loaded = sem("w_loaded")
        w_rest = sem("w_rest")
        consts = sem("consts")
        prep = Chain(sem("prep"), 0)
        prepped = sem("prepped")
        fused_full = sem("fused_full")
        a_exp = sem("a_exp")
        pool_prep = sem("pool_prep")
        phase = sem("phase")
        places = sem("places")

        class Signals:

            def at(self, q):
                self.q = q
                (self.u_buf, self.Ct_buf, self.dtv_buf, self.ex_buf, self.hT_buf,
                 self.x_buf) = self.buffers[q]
                return self

        sets = []
        for L in LAYERS:
            s, n = Signals(), L.name + "_"
            s.buffers = [(u, Ct, dtv, ex, hT, xin)] + ([] if L.tree else [
                (am[:, 0:5, :], am[0:64, 5, :], dtv1, ex1, h2T, xn)])
            s.at(0)
            s.f_full = [sig(n + f"front_full{k}", (len(L.front) if k < 2 else len(L.head)) // 2)
                        for k in range(2 if L.tree else 4)]
            s.seg_full = sig(n + "seg_full", CH * L.segs)
            s.intra_full = sig(n + "intra_full", CH)
            s.yo_full = sig(n + "yo_full", 2 * CH)
            s.cum_full, s.ex = sig(n + "cum_full"), sig(n + "decay_exps")
            s.g_full, s.gm = sig(n + "g_full", CH), sig(n + "g_masked", CH)
            s.v = sig(n + "dt_read")
            s.t1 = sig(n + "inter_read", CH)
            s.bs = sig(n + "b_rows_ready", CH)
            if L.tree:
                s.hT = sig(n + "hT_ready", 2)
            else:
                s.hT_loaded = [sig(n + f"hT_loaded{q}", 8) for q in range(2)]
                s.x_loaded = [sig(n + f"x_loaded{q}", 8) for q in range(2)]
            s.e_in, s.e_out = sig(n + "dt_exp_in"), sig(n + "dt_exp_out")
            s.a = sig(n + "decay_log_ready")
            s.r = sig(n + "log1p_ratio")
            s.w_end = sig(n + "dt_to_end_ready")
            s.xb = sig(n + "proj_ready", 10)
            s.halo = sig(n + "halo_kept", 5)
            s.u = sig(n + "conv_ready", 5)
            s.th = sig(n + "conv_tanh", 5)
            s.xc = sig(n + "conv_silu", 6)
            s.thz = sig(n + "z_tanh", CH)
            s.zs = sig(n + "z_silu", CH)
            s.R = sig(n + "decay_terms", CH)
            s.E = sig(n + "decays", CH * L.segs)
            s.M = sig(n + "mask_ready", CH * L.segs)
            s.xsb = sig(n + "x_rows_ready", CH)
            s.xdt = sig(n + "x_dt_ready", CH)
            s.xs = sig(n + "x_end_ready", CH)
            s.xd = sig(n + "x_D_ready", CH)
            s.S = sig(n + "state_ready", CH + 1)
            s.y0 = sig(n + "y_sum_ready", CH)
            s.yg = sig(n + "y_gated", CH)
            s.ssq = sig(n + "y_squares", CH)
            s.ry = sig(n + "y_rms", CH)
            s.yT = sig(n + "yT_ready", CH)
            s.x2 = sig(n + "mixed", CH)
            sets.append(s)
        mv_sig = sig("var_ready")
        rs_sig = sig("rstd_ready")
        xn_sig = sig("xn_ready", CH)
        h_sig = sig("h_ready", CH)
        kept_sig = sig("xn3_kept")
        xnT_sig = sig("xnT_ready", 2)
        tg_sig = sig("gate_tanh", 2)
        leaf_sig = sig("leaves_ready")
        lT_sig = sig("leavesT_ready", 2)
        b_full = [sig(f"back_full{k}", len(LAYERS[0].back) // 2) for k in range(2)]
        sq2 = sig("x2_squares", CH)
        r2_sig = sig("x2_rms")
        h2_sig = sig("h2_ready", CH)
        h2T_sig = sig("h2T_ready", 2)
        xb_sig = sig("residual_ready")
        act2 = sig("up_tanh", 2 * HB)
        am_sig = sig("up_silu", HB)
        x1_sig = sig("x1_ready", CH)
        rt_sig = sig("router_read", 2)
        nve_sig = sig("next_var", CH)
        nrs_sig = sig("next_rstd", CH)
        xo_sig = sig("next_xn", CH)
        nT_sig = sig("next_xnT", 2)
        smx_sig = sig("router_shifted")
        sme_sig = sig("router_exp")
        sc_sig = sig("scores_ready")
        rows_stored = sig("rows_stored", 16)
        x1_stored = sig("x1_stored", 16)
        xp_sig = sig("x_residual_ready")
        nT_stored = sig("nT_stored", 16)
        sc_stored = sig("scores_stored", 16)
        out_stored = [counted(stored, 16) for stored in (rows_stored, x1_stored, nT_stored, sc_stored)]

        cnt_sig = sig("hits_counted", CH)
        ph0 = sem("first_count")
        rt_chain = sem("routing_steps")
        ge_ready, pre_full, idx_full, idx_ready = (sem(n) for n in ("above_ready", "prefix_full", "slots_full", "index_ready"))
        iotas = sem("iotas")
        ol_ready = sig("onehot_ready", TILES)
        ol_used = sig("onehot_used", TILES)
        HS = 4
        idxc_sig = sig("index_copied", HS)
        gathered = [sig(f"gathered{q}", 64 * HS // 2) for q in range(2)]
        xt_full = sig("tokensT_full", 2 * HS)
        xt_sig = sig("tokensT_ready", 2 * HS)
        eup_full = sig("e_up_full", HB * HS)
        gelu_sig = sig("gelu_ready", HB * HS)
        edown_full = sig("e_down_full", 4 * HS)
        gcol_sig = sig("gates_ready", HS)
        edown_read = sig("e_down_read", 4 * HS)
        ye_sig = sig("weighted_ready", 4 * HS)
        scattered = [sig(f"scattered{q}", 64 * HS // 2) for q in range(2)]
        ew_loaded = sig("expert_weights_loaded", 64)
        eb_loaded = [counted(x, 32) for x in (x_loaded, h_sig)]
        w_high, w_low = ([counted(x, 4) for x in pair] for pair in ((act2, am_sig), (x1_sig, rt_sig)))
        xt_low, am_high, am_low = counted(nve_sig, 2 * HS), counted(nrs_sig, HB * HS), counted(xo_sig, HB * HS)

        def apart(eng):
            eng.sem_inc(places, 1)

        def front_use(L, name):
            if name in L.head:
                n = L.head.index(name)
                return 2 + n % 2, n // 2
            n = L.front.index(name)
            return n % 2, n // 2

        def back_use(name):
            n = LAYERS[0].back.index(name)
            return n % 2, n // 2

        def front_wait(eng, L, s, i, name):
            k, m = front_use(L, name)
            s.f_full[k].wait_ge(eng, i, m + 1)
            return bank[k]

        def back_wait(eng, b, name):
            k, m = back_use(name)
            b_full[k].wait_ge(eng, b, m + 1)
            return BACK[k]

        def front_reader(s, name):
            kind, n = name.rstrip("0123"), int(name[-1]) if name[-1].isdigit() else 0
            if kind == "xnT":
                return xnT_sig, n + 1
            if kind == "hT":
                return s.hT, n + 1
            return {"dt": (s.v, 1), "gate": (tg_sig, n + 1),
                    "bc": (s.xb, 2), "x": (s.xb, 2 * (n + 2)), "z": (s.zs, n + 1), "xt": (s.xsb, n + 1),
                    "inter": (s.t1, n + 1), "state": (s.S, n + 2)}[kind]

        def back_reader(name):
            kind, n = name.rstrip("01234567"), int(name[-1])
            return {"h2T": (h2T_sig, n + 1), "lT": (lT_sig, n + 1), "up": (act2, 2 * n + 2),
                    "down": (x1_sig, n + 1), "nT": (nT_sig, n + 1), "rt": (rt_sig, n + 1)}[
                        "h2T" if name.startswith("h2T") else kind]

        def open_front(pe, L, s, i, name):
            uses = L.head if name in L.head else L.front
            n = uses.index(name)
            before, step = (uses[n - 2], i) if n >= 2 else (uses[n - 2], i - 1)
            signal, count = front_reader(s, before)
            signal.wait_ge(pe, step, count)
            return bank[front_use(L, name)[0]]

        def open_back(pe, b, name):
            use = LAYERS[0].back
            n = use.index(name)
            before, step = (use[n - 2], b) if n >= 2 else (use[n - 2], b - 1)
            signal, count = back_reader(before)
            signal.wait_ge(pe, step, count)
            return BACK[n % 2]

        def filled(ins, s, L, name):
            ins.then_inc(s.f_full[front_use(L, name)[0]].sem, 1)

        def back_filled(ins, name):
            ins.then_inc(b_full[back_use(name)[0]].sem, 1)

        def all_steps(eng, step):
            step(0, 0, True)
            step(1, 1, True)
            with eng.Fori(2, STEPS - 3, 2) as i:
                step(i, 0, True)
                step(i + 1, 1, True)
            step(STEPS - 2, 0, True)
            step(STEPS - 1, 1, False)

        block = ctx.enter_context(nc.Block())

        @block.sync
        def _(sp):
            def load(dst, src, s, n=16):
                sp.dma_start(dst, src).then_inc(s, 16)

            def rows(name, n):
                return d[name].partition_broadcast(P)

            def load_x(i):
                h_sig.wait_ge(sp, i, 0)
                xp_sig.wait_ge(sp, i, 0)
                sp.dma_start(xin[:, :, :], x_rows[bass.ds(T * i, T), :].rearrange("(c p) d -> p c d", p=P)
                             ).then_inc(x_loaded.sem, 16)

            load_x(0)
            def square_load(dst, name, s):
                load(dst, d[name].rearrange("(k p) n -> p k n", p=P), s)

            square_load(wq, "wq", w_loaded)
            square_load(wrT, "routersT", w_loaded)
            square_load(lvT, "leafT", w_loaded)
            square_load(woT, "treeoutT", w_loaded)
            load(n1w[:, :], d["n1w"], w_loaded)
            load(b2[:, 0, :], rows("b2", D), w_loaded)
            load(b2[:, 1, :], rows("treeb", D), w_loaded)
            for L, w, s in zip(LAYERS, W, (w_loaded, w_rest)):
                n = L.name
                square_load(w["dt"][:, :, :], n + "_wdt", s)
                square_load(w["bc"][:, :, :], n + "_wbc", s)
                square_load(w["x"][:, :, :], n + "_wx", s)
                square_load(w["z"][:, :, :], n + "_wz", s)
                load(w["conv"][:, :, :], d[n + "_conv"], s)
                load(w["dtb"][:, :], rows(n + "_dtb", L.heads), s)
                load(w["A"][:, :], rows(n + "_alog", L.heads), s)
                load(w["D"][:, :], rows(n + "_D", L.heads), s)
                square_load(w["out"][:, :, :], n + "_wo", s)
                load(w["gn"][:, :], d[n + "_gn"], s)
                if L.tree:
                    square_load(w1, "w1", w_rest)
                    square_load(w2, "w2", w_rest)
                    load(n2w[:, :], d["n2w"], w_rest)
                    square_load(wr[:, :, :], "wr", w_rest)
                    load(b1[:, :], d["b1"], w_rest)

            def store_back(b):
                xo_sig.wait_ge(sp, b, CH)
                sp.dma_start(rows_d[bass.ts(b, T), 0:D].rearrange("(c p) d -> p c d", p=P),
                             xo[:, :, :]).then_inc(rows_stored.sem, 16)
                sp.dma_start(x1_d[bass.ds(T * b, T), :].rearrange("(c p) d -> p c d", p=P),
                             xb[:, :, :]).then_inc(x1_stored.sem, 16)
                nT_sig.wait_ge(sp, b, 2)
                sp.dma_start(xnT_d[b], nT[:, :, :]).then_inc(nT_stored.sem, 16)
                sc_sig.wait_ge(sp, b, 1)
                sp.dma_start(rows_d[bass.ts(b, T), D:ROW].rearrange("(c p) d -> p c d", p=P),
                             SC[:, bass.ts(b, CH), :]).then_inc(sc_stored.sem, 16)

            load_x(1)
            load_x(2)
            store_back(0)
            with sp.Fori(1, STEPS - 2) as b:
                load_x(b + 2)
                store_back(b)
            store_back(STEPS - 2)
            store_back(STEPS - 1)
            for s in (rows_stored, nT_stored, sc_stored, x1_stored):
                sp.wait_ge(s.sem, 16 * STEPS)
            sp.wait_ge(phase, 4)
            sp.drain().then_inc(phase, 1)

            s = sets[1]

            def load_hT(i, q):
                front_wait(sp, LAYERS[1], s, i - 2, "z3")
                sp.dma_start(s.at(q).hT_buf[:, :, :], xnT_d[i]).then_inc(s.hT_loaded[q].sem, 16)

            def store_out(b, c):
                s.x2.wait_ge(sp, b, c + 1)
                sp.dma_start(out_rows[bass.ds(b * T + c * P, P), :], x2[:, c, :]).then_inc(out_stored[c].sem, 16)

            def load_x1(i, q):
                s.x2.wait_ge(sp, i - 1, 0)
                sp.dma_start(s.at(q).x_buf[:, :, :], x1_d[bass.ds(T * i, T), :].rearrange("(c p) d -> p c d", p=P)
                             ).then_inc(s.x_loaded[q].sem, 16)

            def load_weights(e):
                apart(sp)
                sl = bass.ds(e, 1)
                for dst, src in (
                        (EW[:, 0, 0:KD * HID].rearrange("p (k n) -> p k n", k=KD),
                         d["e_w1"][sl].rearrange("a (k p) n -> p (a k) n", p=P)),
                        (EW[:, 0, KD * HID:].rearrange("p (k n) -> p k n", k=HB),
                         d["e_w2"][sl].rearrange("a (k p) n -> p (a k) n", p=P))):
                    sp.dma_start(dst, src).then_inc(ew_loaded.sem, 16)

            def load_biases(e, j):
                sp.dma_start(eb1[:, j, :], d["e_b1"][bass.ds(e, 1)].rearrange("a p n -> p (a n)")
                             ).then_inc(eb_loaded[j].sem, 16)
                sp.dma_start(eb2[:, j, :], d["e_b2"][bass.ds(e, 1), :].rearrange("a n -> (a n)")
                             .partition_broadcast(P)).then_inc(eb_loaded[j].sem, 16)

            for q in range(2):
                load_hT(q, q)
                load_x1(q, q)
            load_weights(0)

            def step1(i, q):
                for c in range(CH - 1):
                    store_out(i, c)
                load_hT(i + 2, q)
                store_out(i, CH - 1)
                load_x1(i + 2, q)

            step1(0, 0)
            step1(1, 1)
            with sp.Fori(2, STEPS - 3, 2) as i:
                step1(i, 0)
                step1(i + 1, 1)
            for i in (STEPS - 2, STEPS - 1):
                for c in range(CH):
                    store_out(i, c)
            for c in range(CH):
                out_stored[c].wait_ge(sp, STEPS, 0)
            sp.wait_ge(phase, 9)
            sp.drain().then_inc(phase, 1)
            load_biases(0, 0)
            load_biases(1, 1)

            def second_weights(i):
                w_low[0].wait_ge(sp, i, 4)
                load_weights(2 * i + 1)

            second_weights(0)

            def next_experts(i):
                w_low[1].wait_ge(sp, i - 1, 4)
                load_weights(2 * i)
                for j in range(2):
                    edown_read.wait_ge(sp, i - 1, 4 * (2 * j + 2))
                    load_biases(2 * i + j, j)
                    if j == 0:
                        second_weights(i)

            with sp.Fori(1, NE // 2) as i:
                next_experts(i)
            for q in range(2):
                sp.wait_ge(scattered[q].sem, scattered[q].per * NE // 2)

        pool0 = Chain(sem("pool_steps"), 44)
        poolb = Chain(sem("pool_back0"), 2)
        pool1 = pool0.after(7)
        poolb1 = poolb.after(1)
        poolh1 = Chain(sem("pool_head1"), 21)

        @block.gpsimd
        def _(pool):
            g = nc.gpsimd
            g.memset(ident[:, :], 0.0).then_inc(consts, 1)
            g.memset(triU[:, :], 1.0).then_inc(consts, 1)
            g.memset(strL[:, :], 1.0).then_inc(consts, 1)
            g.memset(ones[:, :], 1.0).then_inc(consts, 1)
            g.memset(flags[:, :], 1.0).then_inc(consts, 1)
            g.memset(nhalf[:, :], -0.5).then_inc(consts, 1)
            pool.wait_ge(consts, 6)
            g.affine_select(out=ident[:, :], in_=ident[:, :], compare_op=ALU.not_equal, fill=1.0, base=0,
                            pattern=[[-1, P]], channel_multiplier=1).then_inc(consts, 1)
            g.affine_select(out=triU[:, :], in_=triU[:, :], compare_op=ALU.is_ge, fill=0.0, base=0,
                            pattern=[[1, P]], channel_multiplier=-1).then_inc(consts, 1)
            g.affine_select(out=strL[:, :], in_=strL[:, :], compare_op=ALU.is_ge, fill=0.0, base=-1,
                            pattern=[[-1, P]], channel_multiplier=1).then_inc(consts, 1)
            for q in range(0, STEPS + 1, STEPS // NB):
                g.memset(flags[:, q:q + 1], 0.0).then_inc(consts, 1)

            def rstd(i):
                mv_sig.wait_ge(pool, i, 1)
                h_sig.wait_ge(pool, i, 0)
                g.tensor_tensor(rs[:, :], ve[:, :], nhalf[:, 0:8], ALU.pow).then_inc(rs_sig.sem, 1)

            def softplus(L, s, i, ch):
                n, w = CH * L.heads, W[LAYERS.index(L)]
                t = [dts[:, k, 0:n] for k in range(8)]

                def op(ins):
                    ch.put(ins)
                    ch.see(pool)
                    apart(pool)

                s.r.wait_ge(pool, i, 1)
                op(g.tensor_tensor(t[3], t[2], t[2], ALU.mult))
                op(g.tensor_scalar(t[4], t[3], 1.0 / 17, 1.0 / 15, ALU.mult, ALU.add))
                for k in (13, 11, 9, 7, 5, 3, 1):
                    op(g.tensor_tensor(t[4], t[4], t[3], ALU.mult))
                    op(g.tensor_scalar(t[4], t[4], 1.0 / k, None, ALU.add))
                op(g.tensor_tensor(t[5], t[4], t[2], ALU.mult))
                op(g.tensor_scalar(t[6], t[0], 0.0, 0.5, ALU.max, ALU.mult))
                op(g.tensor_tensor(t[5], t[5], t[6], ALU.add))
                s.seg_full.wait_ge(pool, i + 1 - L.lag, 0)
                s.xdt.wait_ge(pool, i + 1 - L.lag, 0)
                apart(pool)
                op(g.tensor_scalar(s.dtv_buf[:, 0, 0:n], t[5], 2.0, None, ALU.mult))
                op(g.tensor_tensor(t[7].rearrange("p (c h) -> p c h", c=CH),
                                   s.dtv_buf[:, 0, 0:n].rearrange("p (c h) -> p c h", c=CH),
                                   w["A"][:, :].unsqueeze(1).to_broadcast([P, CH, L.heads]), ALU.mult))
                g.tensor_scalar(s.dtv_buf[:, 1, 0:n], t[7], LIM, None, ALU.max).then_inc(s.a.sem, 1)

            def terms(L, s, i, c, ch):
                s.a.wait_ge(pool, i, 1)
                s.seg_full.wait_ge(pool, i, c * L.segs)
                nh = L.heads
                v = R[:, 0:nh * P].rearrange("p (h t) -> p h t", h=nh)
                a = s.dtv_buf[:, 1, c * nh:(c + 1) * nh].unsqueeze(2).to_broadcast([P, nh, P])
                g.tensor_tensor(v, triU[:, :].unsqueeze(1).to_broadcast([P, nh, P]), a,
                                ALU.mult).then_inc(s.R.sem, 1)

            def xrows(L, s, i, c):
                nh, hp, q = L.heads, L.hp, c % 2
                s.xsb.wait_ge(pool, i, c + 1)
                s.w_end.wait_ge(pool, i, 1)
                if c >= 2:
                    front_wait(pool, L, s, i, f"state{c-2}")
                else:
                    front_wait(pool, L, s, i - 1, f"state{c+2}")
                x3 = Xsb[:, q, :].rearrange("p (h e) -> p h e", h=nh)
                g.tensor_tensor(Xs[:, q, :].rearrange("p (h e) -> p h e", h=nh), x3,
                                s.dtv_buf[:, 2, c * nh:(c + 1) * nh].unsqueeze(2).to_broadcast([P, nh, hp]),
                                ALU.mult).then_inc(s.xs.sem, 1)
                g.tensor_tensor(XD[:, q, :].rearrange("p (h e) -> p h e", h=nh), x3,
                                W[LAYERS.index(L)]["D"][:, :].unsqueeze(2).to_broadcast([P, nh, hp]),
                                ALU.mult).then_inc(s.xd.sem, 1)

            def gated(L, s, i, c, ch):
                q = c % 2
                s.y0.wait_ge(pool, i, c + 1)
                s.xd.wait_ge(pool, i, c + 1)
                ch.put(g.tensor_tensor(yb[:, q, :], yb[:, q, :], XD[:, q, :], ALU.add))
                ch.see(pool)
                s.zs.wait_ge(pool, i, c + 1)
                g.tensor_tensor(yb[:, q, :], yb[:, q, :], zs[:, q, :], ALU.mult).then_inc(s.yg.sem, 1)

            def y_rms(L, s, i, c, ch):
                s.ssq.wait_ge(pool, i, c + 1)
                s.x2.wait_ge(pool, i, c - 3)
                apart(pool)
                ch.put(g.tensor_scalar(ry[:, c:c + 1], ssq[:, c:c + 1], 1.0 / DI, 1e-5, ALU.mult, ALU.add))
                ch.see(pool)
                g.tensor_tensor(ry[:, c:c + 1], ry[:, c:c + 1], nhalf[:, 0:1], ALU.pow).then_inc(s.ry.sem, 1)

            def back_rms(b, ch):
                sets[0].x2.wait_ge(pool, b, CH)
                x1_stored.wait_ge(pool, b, 0)
                xo_sig.wait_ge(pool, b, 0)
                g.tensor_tensor(xb[:, :, :], x2[:, :, :], xp[:, :, :], ALU.add).then_inc(xb_sig.sem, 1)
                sq2.wait_ge(pool, b, CH)
                h2_sig.wait_ge(pool, b, 0)
                apart(pool)
                ch.put(g.tensor_scalar(ry[:, CH:], ssq[:, CH:], 1.0 / D, 1e-6, ALU.mult, ALU.add))
                ch.see(pool)
                g.tensor_tensor(ry[:, CH:], ry[:, CH:], nhalf[:, 0:CH], ALU.pow).then_inc(r2_sig.sem, 1)

            def tree(i, ch):
                tg_sig.wait_ge(pool, i, 2)
                apart(pool)
                ch.put(g.tensor_scalar(tg[:, :, :], tg[:, :, :], 0.5, 0.5, ALU.mult, ALU.add))
                ch.see(pool)
                n = 1
                src = None
                while n < LEAVES:
                    last = 2 * n == LEAVES
                    dst = (leaf[:, :, :] if last else lp[:, (n.bit_length()) % 2, :, 0:2 * n]
                           ).rearrange("p c (n two) -> p c n two", two=2)
                    gn = tg[:, :, n - 1:2 * n - 1]
                    if last:
                        back_wait(pool, i - 1, "lT1")
                    if n == 1:
                        apart(pool)
                        ch.put(g.tensor_copy(dst[:, :, :, 1], gn))
                        ch.put(g.tensor_scalar(dst[:, :, :, 0], gn, -1.0, 1.0, ALU.mult, ALU.add))
                    else:
                        ch.put(g.tensor_tensor(dst[:, :, :, 1], src, gn, ALU.mult))
                        ch.see(pool)
                        left = g.tensor_tensor(dst[:, :, :, 0], src, dst[:, :, :, 1], ALU.subtract)
                        if last:
                            left.then_inc(leaf_sig.sem, 1)
                        else:
                            ch.put(left)
                    ch.see(pool)
                    if not last:
                        src = lp[:, (n.bit_length()) % 2, :, 0:2 * n]
                    n *= 2

            def next_rstd(b, c):
                nve_sig.wait_ge(pool, b, c + 1)
                xo_sig.wait_ge(pool, b, c - 3)
                g.tensor_tensor(nrs[:, c:c + 1], nve[:, c:c + 1], nhalf[:, 0:1], ALU.pow).then_inc(nrs_sig.sem, 1)

            def step0(f, b, n):
                L, s = LAYERS[0], sets[0]
                if b is not None:
                    poolb.begin(b)
                    y_rms(L, s, b, 3, poolb)
                    back_rms(b, poolb)
                if f is not None:
                    pool0.begin(f)
                    softplus(L, s, f, pool0)
                    terms(L, s, f, 0, pool0)
                    xn_sig.wait_ge(pool, f, CH)
                    s.x2.wait_ge(pool, f, 0)
                    apart(pool)
                    g.tensor_copy(xr3[:, :], xn[:, CH - 1, :]).then_inc(kept_sig.sem, 1)
                    x_loaded.wait_ge(pool, f, 16)
                    g.tensor_tensor(xp[:, :, :], xin[:, :, :],
                                    b2[:, 0, :].unsqueeze(1).to_broadcast([P, CH, D]), ALU.add).then_inc(xp_sig.sem, 1)
                    xrows(L, s, f, 0)
                    for c in range(CH):
                        if c + 1 < CH:
                            terms(L, s, f, c + 1, pool0)
                            xrows(L, s, f, c + 1)
                        gated(L, s, f, c, pool0)
                        if c:
                            y_rms(L, s, f, c - 1, pool0)
                        if n is not None and c == 2:
                            rstd(n)
                    tree(f, pool0)
                    pool0.end()
                if b is not None:
                    for c in range(CH):
                        next_rstd(b, c)
                    poolb.end()

            rstd(0)
            pool.wait_ge(w_loaded, 16 * W_FIRST)
            g.tensor_tensor(b2[:, 0, :], b2[:, 0, :], b2[:, 1, :], ALU.add).then_inc(pool_prep, 1)
            pool.wait_ge(pool_prep, 1)
            step0(0, None, 1)
            step0(1, 0, 2)
            with pool.Fori(2, STEPS - 1) as i:
                step0(i, i - 1, i + 1)
            step0(STEPS - 1, STEPS - 2, None)
            step0(None, STEPS - 1, None)
            pool.drain().then_inc(phase, 1)
            pool.wait_ge(phase, 5)

            def dt_of(i):
                poolh1.begin(i)
                softplus(L1, s1, i, poolh1)
                poolh1.end()

            def step1(i, q, more):
                pool1.begin(i)
                for c in range(CH):
                    s1.at(q)
                    if c + 1 < CH:
                        xrows(L1, s1, i, c + 1)
                    gated(L1, s1, i, c, pool1)
                    if c:
                        y_rms(L1, s1, i, c - 1, pool1)
                    elif not (isinstance(i, int) and i == 0):
                        poolb1.begin(i - 1)
                        y_rms(L1, s1, i - 1, CH - 1, poolb1)
                        poolb1.end()
                    if c + 2 < CH:
                        terms(L1, s1, i, c + 2, pool1)
                    if more:
                        s1.at(1 - q)
                        if c == 1:
                            dt_of(i + 1)
                        elif c == 2:
                            terms(L1, s1, i + 1, 0, pool1)
                        elif c == 3:
                            xrows(L1, s1, i + 1, 0)
                            terms(L1, s1, i + 1, 1, pool1)
                pool1.end()

            L1, s1 = LAYERS[1], sets[1].at(0)
            dt_of(0)
            terms(L1, s1, 0, 0, pool1)
            xrows(L1, s1, 0, 0)
            terms(L1, s1, 0, 1, pool1)
            all_steps(pool, step1)
            poolb1.begin(STEPS - 1)
            y_rms(L1, s1, STEPS - 1, CH - 1, poolb1)
            poolb1.end()
            pool.drain().then_inc(phase, 1)
            pool.wait_ge(phase, 10)

            g.iota(iotaf[:, :], pattern=[[1, P]], base=0, channel_multiplier=0,
                   allow_small_or_imprecise_dtypes=True).then_inc(iotas, 1)
            g.iota(pidx[:, :], pattern=[[1, 1]], base=0, channel_multiplier=1,
                   allow_small_or_imprecise_dtypes=True).then_inc(iotas, 1)
            g.iota(tidx[:, :, :], pattern=[[0, NE], [1, TILES]], base=0, channel_multiplier=0,
                   allow_small_or_imprecise_dtypes=True).then_inc(iotas, 1)
            g.memset(reset[:, :, :, :], 1.0).then_inc(iotas, 1)
            pool.wait_ge(iotas, 4)
            g.memset(reset[:, :, :, 0:1], 0.0).then_inc(iotas, 1)

            def low_weights(i, j):
                for m in range(4):
                    w_high[j].wait_ge(pool, i, m + 1)
                    edown_full.wait_ge(pool, i - 1, 4 * (2 * j + 2))
                    sl = slice(m * KD * HID // 2, (m + 1) * KD * HID // 2)
                    g.tensor_tensor(EWl[:, j, sl], EW[:, 0, sl], EWh[:, j, sl],
                                    ALU.subtract).then_inc(w_low[j].sem, 1)

            low_weights(0, 0)
            pool.wait_ge(idx_ready, 1)

            def gather(i, s):
                k, q = s % HS, s % 2
                if s >= HS:
                    i, s = i + 1, s - HS
                scattered[q].wait_ge(pool, i, 64 * (s // 2 - 1))
                apart(pool)
                g.tensor_copy(idxc[:, k, :], IDX[:, bass.ds(i * 16 + s * 4, 4)]).then_inc(idxc_sig.sem, 1)
                idxc_sig.wait_ge(pool, i, s + 1)
                xt_full.wait_ge(pool, i, 2 * (s - 1))
                gcol_sig.wait_ge(pool, i, s - 1)
                apart(pool)
                for j in range(4):
                    g.indirect_dma_start(out=xg[:, q, j, :], out_offset=None, in_=rows_d,
                                         in_offset=bass.IndirectOffsetOnAxis(ap=idxc[:, k, j:j + 1], axis=0)
                                         ).then_inc(gathered[q].sem, 16)

            def scatter(i, s):
                scattered[s % 2].wait_ge(pool, i, 64 * (s // 2))
                if s % 2 == 0:
                    scattered[1].wait_ge(pool, i, 64 * (s // 2))
                for j in range(4):
                    ye_sig.wait_ge(pool, i, 4 * s + j + 1)
                    apart(pool)
                    g.indirect_dma_start(out=out_rows, out_offset=bass.IndirectOffsetOnAxis(
                        ap=idxc[:, s, j:j + 1], axis=0), in_=ye[:, s % 2, j, :], in_offset=None,
                        compute_op=ALU.add).then_inc(scattered[s % 2].sem, 16)

            gather(0, 0)
            gather(0, 1)

            def estep(i, more):
                for s in range(HS):
                    if more or s < 2:
                        gather(i, s + 2)
                    if s == 0:
                        low_weights(i, 1)
                    elif s == 2 and more:
                        low_weights(i + 1, 0)
                    scatter(i, s)

            estep(0, True)
            with pool.Fori(1, NE // 2 - 1) as i:
                estep(i, True)
            estep(NE // 2 - 1, False)
            for q in range(2):
                pool.wait_ge(scattered[q].sem, scattered[q].per * NE // 2)

        @block.scalar
        def _(act):
            a = nc.scalar

            act.wait_ge(w_loaded, 16 * W_FIRST)
            a.activation(W[0]["A"][:, :], W[0]["A"][:, :], ACT.Exp).then_inc(a_exp, 1)

            def dt_exp(L, s, i):
                s.e_in.wait_ge(act, i, 1)
                n = CH * L.heads
                a.activation(dts[:, 1, 0:n], dts[:, 1, 0:n], ACT.Exp).then_inc(s.e_out.sem, 1)

            def raw(L, s, i, j):
                blk = (j - 1) % 5
                p = front_wait(act, L, s, i, L.blocks[j])
                if j == 0:
                    front_wait(act, L, s, i - L.lag, "xt3")
                    s.g_full.wait_ge(act, i - L.lag, CH)
                w = W[LAYERS.index(L)]["conv"]
                a.activation(s.u_buf[:, blk, :], p[:, :], ACT.Identity, bias=w[:, blk, L.taps:L.taps + 1],
                             scale=w[:, blk, L.taps - 1:L.taps]).then_inc(s.xb.sem, 1)
                s.halo.wait_ge(act, i - 1, j + 1)
                a.activation(xbuf[:, blk, L.halo:L.halo + T], p[:, :], ACT.Copy).then_inc(s.xb.sem, 1)

            def conv_tanh(L, s, i, j):
                s.u.wait_ge(act, i, j + 1)
                s.xc.wait_ge(act, i, j)
                a.activation(th[:, j % 2, :], s.u_buf[:, (j - 1) % 5, :], ACT.Tanh).then_inc(s.th.sem, 1)

            def decay_exp(L, s, i):
                n = CH * L.heads
                s.cum_full.wait_ge(act, i, 1)
                a.activation(s.ex_buf[:, :, 0:n], CUM.rearrange("p (j n) -> p j n", j=3)[:, :, 0:n],
                             ACT.Exp).then_inc(s.ex.sem, 1)

            def rows_turned(L, s, i):
                for k in range(KD):
                    p = front_wait(act, L, s, i, f"xnT{k}")
                    front_wait(act, L, s, i - 1, "gate1")
                    a.activation(xnT[:, k, :], p[:, :], ACT.Copy).then_inc(xnT_sig.sem, 1)
                for k in range(KD):
                    p = front_wait(act, L, s, i, f"hT{k}")
                    front_wait(act, L, s, i - 1, "z3")
                    a.activation(s.hT_buf[:, k, :], p[:, :], ACT.Copy).then_inc(s.hT.sem, 1)

            def head(L, s, i, between=()):
                dt_exp(L, s, i)
                if between:
                    between[0]()
                for j in range(3):
                    raw(L, s, i, j)
                for j in range(5):
                    conv_tanh(L, s, i, j)
                    if j + 3 < 5:
                        raw(L, s, i, j + 3)
                    if j == 1:
                        leaf_sig.wait_ge(act, i, 0)
                        for k in range(2):
                            p = front_wait(act, L, s, i, f"gate{k}")
                            a.activation(tg[:, 2 * k:2 * k + 2, :],
                                         p[:, :].rearrange("p (c n) -> p c n", c=2), ACT.Tanh,
                                         scale=0.5).then_inc(tg_sig.sem, 1)
                    if between:
                        between[j + 1]()

            def chunk(L, s, i, c):
                q = c % 2
                p = front_wait(act, L, s, i, f"z{c}")
                s.zs.wait_ge(act, i, c)
                a.activation(thz[:, :], p[:, :], ACT.Tanh).then_inc(s.thz.sem, 1)

                def decays(j):
                    s.seg_full.wait_ge(act, i, c * L.segs + j + 1)
                    a.activation(E[:, q, 512 * j:512 * (j + 1)], SEG[:, :], ACT.Exp).then_inc(s.E.sem, 1)

                s.intra_full.wait_ge(act, i, c - 1)
                decays(0)
                p = front_wait(act, L, s, i, f"xt{c}")
                s.xdt.wait_ge(act, i, c - 1)
                s.xd.wait_ge(act, i, c - 1)
                a.activation(Xsb[:, q, :], p[:, :], ACT.Copy).then_inc(s.xsb.sem, 1)
                for j in range(1, L.segs):
                    decays(j)

            def square(L, s, i, c):
                s.yg.wait_ge(act, i, c + 1)
                s.ssq.wait_ge(act, i, c)
                if L.tree and c == 0:
                    sq2.wait_ge(act, i, 0)
                a.activation(junk[:, :], yb[:, c % 2, :], ACT.Square,
                             accum_out=ssq[:, c:c + 1]).then_inc(s.ssq.sem, 1)

            def transposed(L, s, i, c):
                s.yo_full.wait_ge(act, i, 2 * c + 1)
                a.activation(yT[:, :, :], YO[:, :].rearrange("p (k t) -> p k t", k=CH),
                             ACT.Copy).then_inc(s.yT.sem, 1)

            def square2(b, c):
                sets[0].x2.wait_ge(act, b, c + 1)
                if c == 0:
                    sets[0].ssq.wait_ge(act, b, CH)
                sq2.wait_ge(act, b, c)
                a.activation(junk[:, 0:D], x2[:, c, :], ACT.Square,
                             accum_out=ssq[:, CH + c:CH + c + 1]).then_inc(sq2.sem, 1)

            def up(b, k):
                p = back_wait(act, b, f"up{k}")
                am_sig.wait_ge(act, b, k - 1)
                back_wait(act, b - 1, "down3")
                a.activation(am[:, k, :], p[:, :], ACT.Identity, bias=b1[:, k:k + 1]).then_inc(act2.sem, 1)
                ins = a.activation(tt[:, k % 2, :], p[:, :], ACT.Tanh, bias=b1[:, k:k + 1])
                ins.then_inc(act2.sem, 1)

            def step0(f, b, n):
                L, s = LAYERS[0], sets[0]

                def last_chunk():
                    square(L, s, b, 3)
                    transposed(L, s, b, 3)
                    for c in range(CH - 1):
                        square2(b, c)

                def lT_copies():
                    for k in range(KD):
                        p = back_wait(act, b, f"lT{k}")
                        back_wait(act, b - 1, "down3")
                        a.activation(lT[:, k, :], p[:, :], ACT.Copy).then_inc(lT_sig.sem, 1)

                def h2T_copies():
                    for k in range(KD):
                        p = back_wait(act, b, f"h2T{k}")
                        back_wait(act, b - 1, "up7")
                        a.activation(h2T[:, k, :], p[:, :], ACT.Copy).then_inc(h2T_sig.sem, 1)

                between = () if b is None else (
                    last_chunk, lambda: square2(b, CH - 1), lT_copies, h2T_copies, lambda: None,
                    lambda: up(b, 0))
                if f is not None:
                    head(L, s, f, between)
                else:
                    for part in between:
                        part()
                if b is not None:
                    for j in EARLY_UPS[1:]:
                        up(b, j)
                if f is not None:
                    decay_exp(L, s, f)
                    chunk(L, s, f, 0)
                for c in range(CH):
                    if b is not None:
                        for j in LATE_UPS[c]:
                            up(b, j)
                    if f is not None:
                        if c + 1 < CH:
                            chunk(L, s, f, c + 1)
                        if c:
                            square(L, s, f, c - 1)
                            transposed(L, s, f, c - 1)
                if n is not None:
                    rows_turned(L, s, n)
                if b is not None:
                    for k in range(2):
                        p = back_wait(act, b, f"nT{k}")
                        back_wait(act, b - 1, "rt1")
                        nT_stored.wait_ge(act, b, 0)
                        a.activation(nT[:, :, 2 * P * k:2 * P * (k + 1)],
                                     p[:, :].rearrange("p (k n) -> p k n", k=KD), ACT.Copy).then_inc(nT_sig.sem, 1)
                    smx_sig.wait_ge(act, b, 1)
                    a.activation(sx[:, 1, :, :], sx[:, 0, :, :], ACT.Exp).then_inc(sme_sig.sem, 1)

            rows_turned(LAYERS[0], sets[0], 0)
            step0(0, None, 1)
            act.wait_ge(w_rest, 16 * W_REST)
            a.activation(W[1]["A"][:, :], W[1]["A"][:, :], ACT.Exp).then_inc(a_exp, 1)
            step0(1, 0, 2)
            with act.Fori(2, STEPS - 1) as i:
                step0(i, i - 1, i + 1)
            step0(STEPS - 1, STEPS - 2, None)
            step0(None, STEPS - 1, None)
            act.drain().then_inc(phase, 1)
            act.wait_ge(phase, 5)

            L1, s1 = LAYERS[1], sets[1].at(0)

            def head_part(i, c):
                if c == 0:
                    dt_exp(L1, s1, i)
                    raw(L1, s1, i, 0)
                elif c == 1:
                    raw(L1, s1, i, 1)
                    conv_tanh(L1, s1, i, 0)
                    raw(L1, s1, i, 2)
                    conv_tanh(L1, s1, i, 1)
                elif c == 2:
                    raw(L1, s1, i, 3)
                    conv_tanh(L1, s1, i, 2)
                    raw(L1, s1, i, 4)
                    conv_tanh(L1, s1, i, 3)
                    conv_tanh(L1, s1, i, 4)
                    decay_exp(L1, s1, i)

            def step1(i, q, more):
                for c in range(CH):
                    s1.at(q)
                    if c + 1 < CH:
                        chunk(L1, s1, i, c + 1)
                    if c:
                        square(L1, s1, i, c - 1)
                        transposed(L1, s1, i, c - 1)
                    elif not (isinstance(i, int) and i == 0):
                        square(L1, s1, i - 1, CH - 1)
                        transposed(L1, s1, i - 1, CH - 1)
                    if more:
                        s1.at(1 - q)
                        head_part(i + 1, c)
                if more:
                    chunk(L1, s1, i + 1, 0)

            for c in range(CH):
                head_part(0, c)
            chunk(L1, s1, 0, 0)
            all_steps(act, step1)
            square(L1, s1, STEPS - 1, CH - 1)
            transposed(L1, s1, STEPS - 1, CH - 1)
            act.drain().then_inc(phase, 1)
            act.wait_ge(phase, 10)

            def high_weights(i, j, m):
                if m == 0:
                    ew_loaded.wait_ge(act, i, 32 * (j + 1))
                    edown_full.wait_ge(act, i - 1, 4 * (2 * j + 2))
                sl = slice(m * KD * HID // 2, (m + 1) * KD * HID // 2)
                a.activation(EWh[:, j, sl], EW[:, 0, sl], ACT.Copy).then_inc(w_high[j].sem, 1)

            def high_tokens(i, s):
                q = s % 2
                if s == HS:
                    i, s = i + 1, 0
                for k in range(KD):
                    xt_full.wait_ge(act, i, 2 * s + k + 1)
                    eup_full.wait_ge(act, i, HB * (s - 1))
                    a.activation(xTh[:, q, k, :], bank[k][:, :], ACT.Copy).then_inc(xt_sig.sem, 1)

            def high_hidden(i, s, k):
                gelu_sig.wait_ge(act, i, HB * s + k + 1)
                edown_full.wait_ge(act, i, 4 * (s - 1))
                a.activation(amh[:, s % 2, k, :], am4[:, k % 4, :], ACT.Copy).then_inc(am_high.sem, 1)

            def estep(i, more):
                for s in range(HS):
                    if s % 2 == 0:
                        eb_loaded[s // 2].wait_ge(act, i, 32)
                    for k in range(HB):
                        eup_full.wait_ge(act, i, HB * s + k + 1)
                        am_low.wait_ge(act, i, HB * s + k - 3)
                        a.activation(am4[:, k % 4, :], bank[2 + k % 2][:, :], ACT.Gelu,
                                     bias=eb1[:, s // 2, k:k + 1]).then_inc(gelu_sig.sem, 1)
                        if k:
                            high_hidden(i, s, k - 1)
                        if k % 2 and s == 1:
                            high_weights(i, 1, k // 2)
                        elif k % 2 and s == 3 and more:
                            high_weights(i + 1, 0, k // 2)
                    high_hidden(i, s, HB - 1)
                    if more or s + 1 < HS:
                        high_tokens(i, s + 1)

            for m in range(4):
                high_weights(0, 0, m)
            high_tokens(0, 0)
            estep(0, True)
            with act.Fori(1, NE // 2 - 1) as i:
                estep(i, True)
            estep(NE // 2 - 1, False)

        dve0 = Chain(sem("dve_front0"), DF0)
        dven = Chain(sem("dve_norm"), DN)
        dveb = Chain(sem("dve_back0"), DB0)
        dve1 = dve0.after(DF1)
        dveh1 = dveb.after(DH1)

        @block.vector
        def _(dve):
            v = nc.vector

            count = 0

            def scale(out_, factor, second=None):
                nonlocal count
                v.tensor_scalar(out_, out_, factor, second, ALU.mult,
                                ALU.mult if second is not None else ALU.bypass).then_inc(prepped, 1)
                count += 1

            def mixer_weights(L, w):
                scale(w["conv"][:, :, :], 0.5)
                for k in range(CH):
                    scale(w["out"][:, k, :], w["gn"][:, k:k + 1])
                scale(w["A"][:, :], -1.0)

            v.memset(S[:, :], 0.0).then_inc(prepped, 1)
            v.memset(Ct[:, :], 0.0).then_inc(prepped, 1)
            v.memset(xbuf[:, :, 0:4], 0.0).then_inc(prepped, 1)
            v.memset(Bs[:, :, :], 0.0).then_inc(prepped, 1)
            count += 4
            dve.wait_ge(w_loaded, 16 * W_FIRST)
            for k in range(KD):
                scale(W[0]["z"][:, k, :], n1w[:, k:k + 1], 0.5)
                for n in ("x", "bc", "dt"):
                    scale(W[0][n][:, k, :], n1w[:, k:k + 1])
            dve.wait_ge(a_exp, 1)
            mixer_weights(LAYERS[0], W[0])
            dve.wait_ge(fused_full, 1)
            for k in range(KD):
                v.tensor_copy(wg[:, k, :], BACK[k][:, 0:LEAVES]).then_inc(prepped, 1)
                v.tensor_copy(wv[:, k, :], BACK[k][:, LEAVES:2 * LEAVES]).then_inc(prepped, 1)
                count += 2
            assert count == PREPPED_FIRST, count
            dve.wait_ge(prepped, PREPPED_FIRST)
            dve.wait_ge(consts, 9 + NB + 1)

            def rest_of_weights():
                dve.wait_ge(w_rest, 16 * W_REST)
                for k in range(KD):
                    scale(w1[:, k, :], n2w[:, k:k + 1], 0.5)
                    scale(W[1]["z"][:, k, :], 0.5)
                scale(b1[:, :], 0.5)
                dve.wait_ge(a_exp, 2)
                mixer_weights(LAYERS[1], W[1])
                assert count == PREPPED, count

            def norm(i):
                dven.begin(i)
                x_loaded.wait_ge(dve, i, 16)
                for c in range(CH):
                    dven.put(v.bn_stats(st6[:, c, :], xin[:, c, :]))
                dven.see(dve)
                rs_sig.wait_ge(dve, i, 0)
                apart(dve)
                for c in range(CH):
                    dven.put(v.bn_aggr(mv[:, c, :], st6[:, c, :]))
                dven.see(dve)
                dven.put(v.tensor_scalar(ve[:, 0:CH], mv[:, :, 1], 1e-5, None, ALU.add))
                v.tensor_scalar(ve[:, CH:], mv[:, :, 1], 1.0 + 1e-6, 1e-11, ALU.mult,
                                ALU.add).then_inc(mv_sig.sem, 1)
                dven.end()

            def dt_raw(L, s, i):
                n, nh = CH * L.heads, L.heads
                s.a.wait_ge(dve, i, 0)
                p = front_wait(dve, L, s, i, "dt")
                v.tensor_tensor(dts[:, 0, 0:n].rearrange("p (c h) -> p c h", c=CH),
                                p[:, 0:n].rearrange("p (c h) -> p c h", c=CH),
                                W[LAYERS.index(L)]["dtb"][:, :].unsqueeze(1).to_broadcast([P, CH, nh]),
                                ALU.add).then_inc(s.v.sem, 1)
                s.v.wait_ge(dve, i, 1)
                v.scalar_tensor_tensor(out=dts[:, 1, 0:n], in0=dts[:, 0, 0:n], scalar=-1.0,
                                       in1=dts[:, 0, 0:n], op0=ALU.mult,
                                       op1=ALU.min).then_inc(s.e_in.sem, 1)

            def conv(L, s, i, j, ch):
                blk = (j - 1) % 5
                w = W[LAYERS.index(L)]["conv"]
                s.xb.wait_ge(dve, i, 2 * (j + 1))
                for k in range(L.taps - 1):
                    if k:
                        ch.see(dve)
                    ins = v.scalar_tensor_tensor(out=s.u_buf[:, blk, :], in0=xbuf[:, blk, k:k + T],
                                                 scalar=w[:, blk, k:k + 1], in1=s.u_buf[:, blk, :], op0=ALU.mult,
                                                 op1=ALU.add)
                    if k < L.taps - 2:
                        ch.put(ins)
                    else:
                        ins.then_inc(s.u.sem, 1)

            def keep_halo(L, s, i, j):
                blk = (j - 1) % 5
                s.u.wait_ge(dve, i, j + 1)
                v.tensor_scalar(xbuf[:, blk, 0:L.halo], xbuf[:, blk, T:T + L.halo],
                                flags[:, bass.ds(i + 1, 1)], None, ALU.mult).then_inc(s.halo.sem, 1)

            def silu(L, s, i, j, ch):
                blk = (j - 1) % 5
                s.th.wait_ge(dve, i, j + 1)
                if j == 0:
                    n, cp = L.state, L.cpart
                    v.scalar_tensor_tensor(out=s.Ct_buf[0:n, :], in0=th[cp:cp + n, 0, :], scalar=1.0,
                                           in1=s.u_buf[cp:cp + n, 4, :], op0=ALU.add,
                                           op1=ALU.mult).then_inc(s.xc.sem, 1)
                    v.scalar_tensor_tensor(out=s.u_buf[0:n, 4, :], in0=th[0:n, 0, :], scalar=1.0,
                                           in1=s.u_buf[0:n, 4, :], op0=ALU.add, op1=ALU.mult).then_inc(s.xc.sem, 1)
                else:
                    v.scalar_tensor_tensor(out=s.u_buf[:, blk, :], in0=th[:, j % 2, :], scalar=1.0, in1=s.u_buf[:, blk, :],
                                           op0=ALU.add, op1=ALU.mult).then_inc(s.xc.sem, 1)

            def dt_ratio(L, s, i, ch):
                s.e_out.wait_ge(dve, i, 1)
                t = [dts[:, k, 0:CH * L.heads] for k in range(4)]
                ch.put(v.tensor_scalar(t[2], t[1], 2.0, None, ALU.add))
                ch.see(dve)
                ch.put(v.reciprocal(t[3], t[2]))
                ch.see(dve)
                v.tensor_tensor(t[2], t[1], t[3], ALU.mult).then_inc(s.r.sem, 1)

            def start(L, s, i):
                n = CH * L.heads
                s.ex.wait_ge(dve, i, 1)
                s.xs.wait_ge(dve, i + 1 - L.lag, 0)
                v.tensor_tensor(s.dtv_buf[:, 2, 0:n], s.dtv_buf[:, 0, 0:n], s.ex_buf[:, 1, 0:n],
                                ALU.mult).then_inc(s.w_end.sem, 1)
                s.S.wait_ge(dve, i, 0)
                v.tensor_scalar(S[:, :], S[:, :], flags[0:64, bass.ds(i, 1)], None,
                                ALU.mult).then_inc(s.S.sem, 1)

            def layer_norm(L, s, i):
                rs_sig.wait_ge(dve, i, 1)
                for c in range(CH):
                    if c == 0:
                        front_wait(dve, L, s, i - 1, "xnT1")
                        kept_sig.wait_ge(dve, i, 0)
                        s.x2.wait_ge(dve, i - 1, CH - 1)
                    v.tensor_scalar(xn[:, c, :], xin[:, c, :], mv[:, c, 0:1], rs[:, c:c + 1],
                                    ALU.subtract, ALU.mult).then_inc(xn_sig.sem, 1)
                front_wait(dve, L, s, i - 1, "hT1")
                for c in range(CH):
                    v.tensor_scalar(h[:, c, :], xin[:, c, :], mv[:, c, 0:1],
                                    rs[:, CH + c:CH + c + 1], ALU.subtract, ALU.mult).then_inc(h_sig.sem, 1)

            def head(L, s, i, ch, between=()):
                dt_raw(L, s, i)
                conv(L, s, i, 0, ch)
                dt_ratio(L, s, i, ch)
                keep_halo(L, s, i, 0)
                if between:
                    between[0]()
                for j in range(1, 5):
                    conv(L, s, i, j, ch)
                    silu(L, s, i, j - 1, ch)
                    keep_halo(L, s, i, j)
                    if between and j == NORMED_AT:
                        between[1]()
                silu(L, s, i, 4, ch)

            def chunk(L, s, i, c, ch):
                q, nh, hp = c % 2, L.heads, L.hp
                k, _ = front_use(L, f"z{c}")
                s.thz.wait_ge(dve, i, c + 1)
                s.yg.wait_ge(dve, i, c - 1)
                v.scalar_tensor_tensor(out=zs[:, q, :], in0=thz[:, :], scalar=1.0, in1=FRONT[k][:, :],
                                       op0=ALU.add, op1=ALU.mult).then_inc(s.zs.sem, 1)
                s.g_full.wait_ge(dve, i, c + 1)
                if not L.tree:
                    threshold(i, c, ch)
                v.tensor_tensor(Gm[:, q, :], GP, triU[:, :], ALU.mult).then_inc(s.gm.sem, 1)
                if c >= 2:
                    front_wait(dve, L, s, i, f"state{c-2}")
                else:
                    front_wait(dve, L, s, i - 1, f"state{c+2}")
                v.tensor_copy(Bs[:, q, 0:L.state], BTP[:, 0:L.state]).then_inc(s.bs.sem, 1)
                s.xsb.wait_ge(dve, i, c + 1)
                s.intra_full.wait_ge(dve, i, c - 1)
                v.tensor_tensor(Xdt[:, q, :].rearrange("p (h e) -> p h e", h=nh),
                                Xsb[:, q, :].rearrange("p (h e) -> p h e", h=nh),
                                s.dtv_buf[:, 0, c * nh:(c + 1) * nh].unsqueeze(2).to_broadcast([P, nh, hp]),
                                ALU.mult).then_inc(s.xdt.sem, 1)
                s.gm.wait_ge(dve, i, c + 1)
                for j in range(L.segs):
                    s.E.wait_ge(dve, i, c * L.segs + j + 1)
                    e3 = E[:, q, 512 * j:512 * (j + 1)].rearrange("p (h t) -> p h t", h=4)
                    v.tensor_tensor(e3, e3, Gm[:, q, :].unsqueeze(1).to_broadcast([P, 4, P]),
                                    ALU.mult).then_inc(s.M.sem, 1)

            def sums(L, s, i, c, ch):
                q, nh, hp, n = c % 2, L.heads, L.hp, 64
                ex3 = s.ex_buf[:, :, c * nh:(c + 1) * nh]
                p = front_wait(dve, L, s, i, f"inter{c}")
                if c >= 2:
                    s.ssq.wait_ge(dve, i, c - 1)
                    s.yo_full.wait_ge(dve, i, 2 * (c - 2) + 1)
                else:
                    s.ssq.wait_ge(dve, i - 1, c + 3)
                    s.yo_full.wait_ge(dve, i - 1, 2 * (c + 2) + 1)
                v.tensor_tensor(yb[:, q, :].rearrange("p (h e) -> p h e", h=nh),
                                p[:, :].rearrange("p (h e) -> p h e", h=nh),
                                ex3[:, 0, :].unsqueeze(2).to_broadcast([P, nh, hp]),
                                ALU.mult).then_inc(s.t1.sem, 1)
                s.S.wait_ge(dve, i, c + 1)
                s3 = S[:, :].rearrange("p (h e) -> p h e", h=nh)
                ch.put(v.tensor_tensor(s3, s3, ex3[0:n, 2, :].unsqueeze(2).to_broadcast([n, nh, hp]), ALU.mult))
                s.t1.wait_ge(dve, i, c + 1)
                s.intra_full.wait_ge(dve, i, c + 1)
                v.tensor_tensor(yb[:, q, :], yb[:, q, :], INTRA[:, :], ALU.add).then_inc(s.y0.sem, 1)
                p = front_wait(dve, L, s, i, f"state{c}")
                ch.see(dve)
                v.tensor_tensor(S[:, :], S[:, :], p[0:n, :], ALU.add).then_inc(s.S.sem, 1)

            def mixed0(s, i, c):
                s.yo_full.wait_ge(dve, i, 2 * c + 2)
                s.ry.wait_ge(dve, i, c + 1)
                if c == 0:
                    back_wait(dve, i - 1, "h2T1")
                v.scalar_tensor_tensor(out=x2[:, c, :], in0=YO[:, 0:D], scalar=ry[:, c:c + 1],
                                       in1=xr3[:, :] if c == CH - 1 else xn[:, c, :], op0=ALU.mult,
                                       op1=ALU.add).then_inc(s.x2.sem, 1)

            def step0(n, f, b):
                L, s = LAYERS[0], sets[0]

                def last_chunk():
                    kept_sig.wait_ge(dve, b, 1)
                    mixed0(s, b, CH - 1)

                def normed():
                    r2_sig.wait_ge(dve, b, 1)
                    xb_sig.wait_ge(dve, b, 1)
                    for c in range(CH):
                        v.tensor_scalar(x2[:, c, :], x2[:, c, :], ry[:, CH + c:CH + c + 1], None,
                                        ALU.mult).then_inc(h2_sig.sem, 1)

                def up(k):
                    act2.wait_ge(dve, b, 2 * k + 2)
                    v.scalar_tensor_tensor(out=am[:, k, :], in0=tt[:, k % 2, :], scalar=1.0,
                                           in1=am[:, k, :], op0=ALU.add,
                                           op1=ALU.mult).then_inc(am_sig.sem, 1)

                between = () if b is None else (last_chunk, normed)
                if b is not None:
                    dveb.begin(b)
                if f is not None:
                    dve0.begin(f)
                    head(L, s, f, dve0, between)
                else:
                    for part in between:
                        part()
                if b is not None:
                    for k in EARLY_UPS:
                        up(k)
                if f is not None:
                    start(L, s, f)
                    chunk(L, s, f, 0, dve0)
                for c in range(CH):
                    if b is not None:
                        for k in LATE_UPS[c]:
                            up(k)
                    if f is not None:
                        if c + 1 < CH:
                            chunk(L, s, f, c + 1, dve0)
                        sums(L, s, f, c, dve0)
                        if c:
                            mixed0(s, f, c - 1)
                    if n is not None and c == 1:
                        norm(n)
                if f is not None:
                    dve0.end()
                if n is not None:
                    layer_norm(L, s, n)
                if b is not None:
                    xb_sig.wait_ge(dve, b, 1)
                    for c in range(CH):
                        p = back_wait(dve, b, f"down{c}")
                        v.tensor_tensor(xb[:, c, :], p[:, 0:D], xb[:, c, :], ALU.add).then_inc(x1_sig.sem, 1)
                        x1_sig.wait_ge(dve, b, c + 1)
                        dveb.put(v.bn_stats(nst[:, 0:6], xb[:, c, :]))
                        dveb.see(dve)
                        xo_sig.wait_ge(dve, b, c - 3)
                        apart(dve)
                        dveb.put(v.bn_aggr(nmv[:, c, :], nst[:, 0:6]))
                        dveb.see(dve)
                        nrs_sig.wait_ge(dve, b, c - 3)
                        v.tensor_scalar(nve[:, c:c + 1], nmv[:, c, 1:2], 1e-5, None,
                                        ALU.add).then_inc(nve_sig.sem, 1)
                    back_wait(dve, b - 1, "nT1")
                    rows_stored.wait_ge(dve, b, 0)
                    for c in range(CH):
                        nrs_sig.wait_ge(dve, b, c + 1)
                        v.tensor_scalar(xo[:, c, :], xb[:, c, :],
                                        nmv[:, c, 0:1], nrs[:, c:c + 1], ALU.subtract,
                                        ALU.mult).then_inc(xo_sig.sem, 1)
                    for k in range(2):
                        p = back_wait(dve, b, f"rt{k}")
                        v.tensor_copy(sx[:, 0, 2 * k:2 * k + 2, :],
                                      p[:, 0:2 * NE].rearrange("p (c e) -> p c e", c=2)).then_inc(rt_sig.sem, 1)
                    rt_sig.wait_ge(dve, b, 2)
                    dveb.put(v.tensor_reduce(sm[:, 0, :], sx[:, 0, :, :], AXX, ALU.max))
                    dveb.see(dve)
                    v.tensor_tensor(sx[:, 0, :, :], sx[:, 0, :, :],
                                    sm[:, 0, :].unsqueeze(2).to_broadcast([P, CH, NE]),
                                    ALU.subtract).then_inc(smx_sig.sem, 1)
                    sme_sig.wait_ge(dve, b, 1)
                    dveb.put(v.tensor_reduce(sm[:, 1, :], sx[:, 1, :, :], AXX, ALU.add))
                    dveb.see(dve)
                    dveb.put(v.reciprocal(sm[:, 2, :], sm[:, 1, :]))
                    dveb.see(dve)
                    v.tensor_tensor(SC[:, bass.ts(b, CH), :], sx[:, 1, :, :],
                                    sm[:, 2, :].unsqueeze(2).to_broadcast([P, CH, NE]),
                                    ALU.mult).then_inc(sc_sig.sem, 1)
                    dveb.end()

            norm(0)
            layer_norm(LAYERS[0], sets[0], 0)
            step0(1, 0, None)
            rest_of_weights()
            step0(2, 1, 0)
            with dve.Fori(2, STEPS - 1) as i:
                step0(i + 1, i, i - 1)
            step0(None, STEPS - 1, STEPS - 2)
            step0(None, None, STEPS - 1)
            dve.drain().then_inc(phase, 1)
            dve.wait_ge(phase, 5)

            v.memset(S[:, :], 0.0).then_inc(prepped, 1)
            v.memset(xbuf[:, :, 0:4], 0.0).then_inc(prepped, 1)
            dve.wait_ge(prepped, PREPPED + 2)

            v.memset(thr[:, :], 0).then_inc(prepped, 1)
            v.memset(bit[:, :], 1 << 30).then_inc(prepped, 1)
            v.memset(cand[:, :], 1 << 30).then_inc(prepped, 1)
            dve.wait_ge(prepped, PREPPED + 5)
            v.tensor_tensor(hits[:, :, :], SC[:, :, :],
                            cand[:, :].bitcast(fp32).unsqueeze(1).to_broadcast([P, TILES, NE]),
                            ALU.is_ge).then_inc(ph0, 1)
            dve.wait_ge(ph0, 1)
            v.tensor_reduce(cnt[:, :], hits[:, :, :].rearrange("p t e -> p e t"), AXX, ALU.add).then_inc(ph0, 1)

            def threshold(i, c, ch):
                ch.put(v.tensor_scalar(okm[:, :], CNT, float(CAP), -1.0, ALU.is_ge, ALU.mult))
                ch.see(dve)
                ch.put(v.scalar_tensor_tensor(out=thr[:, :], in0=okm[:, :], scalar=bit[:, 0:1], in1=thr[:, :],
                                              op0=ALU.bitwise_and, op1=ALU.bitwise_or))
                ch.see(dve)
                ch.put(v.tensor_scalar(bit[:, :], bit[:, :], 1, None, ALU.logical_shift_right))
                ch.see(dve)
                ch.put(v.tensor_scalar(cand[:, :], thr[:, :], bit[:, 0:1], None, ALU.bitwise_or))
                ch.see(dve)
                ch.put(v.tensor_tensor(hits[:, :, :], SC[:, :, :],
                                       cand[:, :].bitcast(fp32).unsqueeze(1).to_broadcast([P, TILES, NE]),
                                       ALU.is_ge))
                ch.see(dve)
                v.tensor_reduce(cnt[:, :], hits[:, :, :].rearrange("p t e -> p e t"), AXX,
                                ALU.add).then_inc(cnt_sig.sem, 1)

            def mixed1(s, i, c):
                s.yo_full.wait_ge(dve, i, 2 * c + 2)
                s.ry.wait_ge(dve, i, c + 1)
                out_stored[c].wait_ge(dve, i - 1, 16)
                s.x_loaded[s.q].wait_ge(dve, i, 16 - 8 * s.q)
                v.scalar_tensor_tensor(out=x2[:, c, :], in0=YO[:, 0:D], scalar=ry[:, c:c + 1],
                                       in1=s.x_buf[:, c, :],
                                       op0=ALU.mult, op1=ALU.add).then_inc(s.x2.sem, 1)

            L1, s1 = LAYERS[1], sets[1].at(0)

            def conv_part(i, j):
                conv(L1, s1, i, j, dveh1)
                if j:
                    silu(L1, s1, i, j - 1, dveh1)
                keep_halo(L1, s1, i, j)

            def head_part(i, c):
                if c == 0:
                    dveh1.begin(i)
                    dt_raw(L1, s1, i)
                    conv_part(i, 0)
                    dt_ratio(L1, s1, i, dveh1)
                elif c == 1:
                    for j in range(1, 3):
                        conv_part(i, j)
                elif c == 2:
                    for j in range(3, 5):
                        conv_part(i, j)
                    silu(L1, s1, i, 4, dveh1)
                    dveh1.end()

            def first_chunk(i):
                start(L1, s1, i)
                dve1.begin(i)
                chunk(L1, s1, i, 0, dve1)

            def step1(i, q, more):
                dve1.resume(i)
                for c in range(CH):
                    s1.at(q)
                    if c + 1 < CH:
                        chunk(L1, s1, i, c + 1, dve1)
                    sums(L1, s1, i, c, dve1)
                    if more:
                        s1.at(1 - q)
                        head_part(i + 1, c)
                    if c == CH - 1:
                        dve1.end()
                        if more:
                            s1.at(1 - q)
                            first_chunk(i + 1)
                    if c:
                        mixed1(s1.at(q), i, c - 1)
                    elif not (isinstance(i, int) and i == 0):
                        mixed1(s1.at(1 - q), i - 1, CH - 1)

            for c in range(CH):
                head_part(0, c)
            first_chunk(0)
            all_steps(dve, step1)
            mixed1(s1, STEPS - 1, CH - 1)
            dve.drain().then_inc(phase, 1)
            dve.wait_ge(phase, 10)

            steps = 0

            def link(ins):
                nonlocal steps
                steps += 1
                ins.then_inc(rt_chain, 1)
                dve.wait_ge(rt_chain, steps)

            SCe = SC[:, :, :].rearrange("p t e -> p e t")
            thrb = thr[:, :].bitcast(fp32).unsqueeze(2).to_broadcast([P, NE, TILES])
            link(v.tensor_tensor(GE[:, 0, :, :], SCe, thrb, ALU.is_gt))
            v.tensor_tensor(GE[:, 1, :, :], SCe, thrb, ALU.is_equal).then_inc(ge_ready, 1)
            flat = "p a e t -> p (a e t)"
            dve.wait_ge(iotas, 5)
            dve.wait_ge(ge_ready, 1)
            v.tensor_copy(iotab[:, :], iotaf[:, :]).then_inc(iotas, 1)
            dve.wait_ge(iotas, 6)
            dve.wait_ge(pre_full, 2)
            link(v.tensor_copy(totS[:, :, :, :].rearrange(flat), bank[1][:, :]))
            link(v.tensor_tensor_scan(incl[:, :, :, :].rearrange(flat), reset[:, :, :, :].rearrange(flat),
                                      totS[:, :, :, :].rearrange(flat), 0.0, ALU.mult, ALU.add))
            link(v.tensor_tensor(posx[:, :, :, :].rearrange(flat), bank[0][:, :],
                                 incl[:, :, :, :].rearrange(flat), ALU.add))
            link(v.tensor_tensor(posx[:, :, :, :], posx[:, :, :, :], totS[:, :, :, :], ALU.subtract))
            link(v.tensor_tensor(posx[:, :, :, :], posx[:, :, :, :], GE[:, :, :, :], ALU.subtract))
            link(v.tensor_scalar(need[:, :], incl[:, 0, :, TILES - 1], -1.0, float(CAP), ALU.mult, ALU.add))
            needb = need[:, :].unsqueeze(2).to_broadcast([P, NE, TILES])
            link(v.tensor_tensor(sel[:, :, :], posx[:, 1, :, :], needb, ALU.is_lt))
            link(v.tensor_tensor(sel[:, :, :], sel[:, :, :], GE[:, 1, :, :], ALU.mult))
            link(v.tensor_tensor(sel[:, :, :], sel[:, :, :], GE[:, 0, :, :], ALU.add))
            link(v.tensor_tensor(slot[:, :, :], posx[:, 1, :, :], needb, ALU.min))
            link(v.tensor_tensor(slot[:, :, :], slot[:, :, :], posx[:, 0, :, :], ALU.add))
            link(v.tensor_scalar(sel[:, :, :], sel[:, :, :], -float(NT), float(NT), ALU.mult, ALU.add))
            link(v.tensor_tensor(sloti[:, :, :], slot[:, :, :], sel[:, :, :], ALU.add))
            link(v.tensor_scalar(hii[:, :, :], sloti[:, :, :], 7, None, ALU.logical_shift_right))
            link(v.tensor_scalar(loi[:, :, :], sloti[:, :, :], P - 1, None, ALU.bitwise_and))
            link(v.tensor_copy(hif[:, :, :], hii[:, :, :]))
            link(v.tensor_copy(lof[:, :, :], loi[:, :, :]))
            hi2 = hif[:, :, :].rearrange("p e t -> p (e t)")
            t2 = tidx[:, :, :].rearrange("p e t -> p (e t)")
            link(v.tensor_tensor(oh8[:, :, :], hi2.unsqueeze(2).to_broadcast([P, NE * TILES, 8]),
                                 iotaf[:, 0:8].unsqueeze(1).to_broadcast([P, NE * TILES, 8]), ALU.is_equal))
            link(v.tensor_scalar(OHR[:, :, 0:8], oh8[:, :, :], pidx[:, 0:1], None, ALU.mult))
            v.tensor_tensor(OHR[:, :, 8:16], oh8[:, :, :], t2.unsqueeze(2).to_broadcast([P, NE * TILES, 8]),
                            ALU.mult).then_inc(ge_ready, 1)

            def onehots(e):
                for k in range(TILES):
                    ol_used.wait_ge(dve, e, k - 3)
                    v.tensor_scalar(OL[:, k % 4, :], iotab[:, :],
                                    lof[:, :, :].rearrange("p e t -> p (e t)")[:, bass.ds(e * TILES + k, 1)],
                                    None, ALU.is_equal).then_inc(ol_ready.sem, 1)

            onehots(0)
            with dve.Fori(1, NE) as e:
                onehots(e)
            dve.wait_ge(idx_full, 1)
            link(v.tensor_copy(idxf[:, :, :].rearrange("p e n -> p (e n)"), bank[2][:, 0:NE * 16]))
            v.scalar_tensor_tensor(out=IDX[:, :].rearrange("p (e n) -> p e n", e=NE), in0=idxf[:, :, 8:16],
                                   scalar=float(P), in1=idxf[:, :, 0:8], op0=ALU.mult,
                                   op1=ALU.add).then_inc(idx_ready, 1)

            def low_tokens(i, s):
                q = s % 2
                if s == HS:
                    i, s = i + 1, 0
                for k in range(KD):
                    xt_sig.wait_ge(dve, i, 2 * s + k + 1)
                    v.tensor_tensor(xTl[:, q, k, :], bank[k][:, :], xTh[:, q, k, :],
                                    ALU.subtract).then_inc(xt_low.sem, 1)

            def weighted(i, s):
                q = s % 2
                if s % 2 == 0:
                    eb_loaded[s // 2].wait_ge(dve, i, 32)
                for j in range(4):
                    edown_full.wait_ge(dve, i, 4 * s + j + 1)
                    scattered[q].wait_ge(dve, i, 64 * (s // 2))
                    v.tensor_tensor(ye[:, q, j, :], bank[4 + j][:, 0:D], eb2[:, s // 2, :],
                                    ALU.add).then_inc(edown_read.sem, 1)
                    edown_read.wait_ge(dve, i, 4 * s + j + 1)
                    v.tensor_scalar(ye[:, q, j, :], ye[:, q, j, :], gcol[:, q, j:j + 1], None,
                                    ALU.mult).then_inc(ye_sig.sem, 1)

            def estep(i, more):
                for s in range(HS):
                    q = s % 2
                    gathered[q].wait_ge(dve, i, 64 * (s // 2 + 1))
                    ye_sig.wait_ge(dve, i, 4 * (s - 1))
                    v.tensor_copy(gcol[:, q, :].unsqueeze(2),
                                  xg[:, q, :, bass.ds(2 * i + D + s // 2, 1)]).then_inc(gcol_sig.sem, 1)
                    for k in range(HB):
                        am_high.wait_ge(dve, i, HB * s + k + 1)
                        v.tensor_tensor(aml[:, q, k, :], am4[:, k % 4, :], amh[:, q, k, :],
                                        ALU.subtract).then_inc(am_low.sem, 1)
                    if more or s + 1 < HS:
                        low_tokens(i, s + 1)
                    gcol_sig.wait_ge(dve, i, s + 1)
                    if s:
                        weighted(i, s - 1)
                    elif not (isinstance(i, int) and i == 0):
                        weighted(i - 1, HS - 1)

            low_tokens(0, 0)
            estep(0, True)
            with dve.Fori(1, NE // 2 - 1) as i:
                estep(i, True)
            estep(NE // 2 - 1, False)
            weighted(NE // 2 - 1, HS - 1)

        @block.tensor
        def _(pe):
            t = nc.tensor

            def mm(out_, lhsT, rhs, first=True, last=True):
                return t.matmul(out_, lhsT, rhs, start=first, stop=last)

            pe.wait_ge(w_loaded, 16 * W_FIRST)
            for k in range(KD):
                sl = slice(k * P, (k + 1) * P)
                for j in range(KD):
                    mm(BACK[k][:, 0:LEAVES], wq[:, j, sl], wrT[:, j, :], j == 0, j == KD - 1)
                for j in range(KD):
                    last = mm(BACK[k][:, LEAVES:2 * LEAVES], lvT[:, j, sl], woT[:, j, :], j == 0, j == KD - 1)
            last.then_inc(fused_full, 1)
            pe.wait_ge(consts, 9 + NB + 1)
            pe.wait_ge(prepped, PREPPED_FIRST)

            def cols(c):
                return slice(c * P, (c + 1) * P)

            def dt_proj(L, s, i):
                w, n = W[LAYERS.index(L)], L.heads
                p = open_front(pe, L, s, i, "dt")
                for c in range(CH):
                    for k in range(KD):
                        last = mm(p[:, c * n:(c + 1) * n], s.hT_buf[:, k, cols(c)], w["dt"][:, k, :], k == 0,
                                  k == 1)
                filled(last, s, L, "dt")

            def in_proj(L, s, i, j):
                w, name = W[LAYERS.index(L)], L.blocks[j]
                p = open_front(pe, L, s, i, name)
                for k in range(KD):
                    lhsT = w["bc"][:, k, :] if j == 0 else w["x"][:, k, cols(j - 1)]
                    last = mm(p[:, :], lhsT, s.hT_buf[:, k, :], k == 0, k == 1)
                filled(last, s, L, name)

            def decay_log_sums(L, s, i):
                s.a.wait_ge(pe, i, 1)
                s.bs.wait_ge(pe, i, 0)
                m = CH * L.heads
                for j, mat in enumerate((triU, strL, ones)):
                    last = mm(CUM[:, 32 * j:32 * j + m], mat[:, :], s.dtv_buf[:, 1, 0:m])
                last.then_inc(s.cum_full.sem, 1)

            def rows_turned(L, s, i):
                for src, name, ready in ((xn, "xnT", xn_sig), (h, "hT", h_sig)):
                    for k in range(KD):
                        p = open_front(pe, L, s, i, f"{name}{k}")
                        for c in range(CH):
                            if k == 0:
                                ready.wait_ge(pe, i, c + 1)
                            last = t.transpose(p[:, cols(c)], src[:, c, cols(k)], ident[:, :])
                        filled(last, s, L, f"{name}{k}")

            def head(L, s, i, between=()):
                s.hT.wait_ge(pe, i, 2)
                dt_proj(L, s, i)
                if between:
                    between[0]()
                in_proj(L, s, i, 0)
                if between:
                    between[1]()
                for j in range(1, 5):
                    in_proj(L, s, i, j)
                xnT_sig.wait_ge(pe, i, 2)
                for g in range(2):
                    p = open_front(pe, L, s, i, f"gate{g}")
                    for c in range(2):
                        for k in range(KD):
                            last = mm(p[:, c * LEAVES:(c + 1) * LEAVES], xnT[:, k, cols(2 * g + c)],
                                      wg[:, k, :], k == 0, k == 1)
                    filled(last, s, L, f"gate{g}")

            def chunk(L, s, i, c):
                w = W[LAYERS.index(L)]
                q = c % 2
                p = open_front(pe, L, s, i, f"z{c}")
                for k in range(KD):
                    last = mm(p[:, :], s.hT_buf[:, k, cols(c)], w["z"][:, k, :], k == 0, k == 1)
                filled(last, s, L, f"z{c}")

                def decay_sums(j):
                    s.E.wait_ge(pe, i, c * L.segs + j)
                    mm(SEG[:, :], strL[:, :], R[:, 512 * j:512 * (j + 1)]).then_inc(s.seg_full.sem, 1)

                s.R.wait_ge(pe, i, c + 1)
                decay_sums(0)
                if c == 0:
                    s.xc.wait_ge(pe, i, 6)
                p = open_front(pe, L, s, i, f"xt{c}")
                for k in range(CH):
                    last = t.transpose(p[:, cols(k)], s.u_buf[:, k, cols(c)], ident[:, :])
                filled(last, s, L, f"xt{c}")
                n = L.state
                s.bs.wait_ge(pe, i, c)
                if c == 0:
                    s.ex.wait_ge(pe, i, 1)
                if not L.tree:
                    if isinstance(i, int) and i == 0 and c == 0:
                        pe.wait_ge(ph0, 2)
                    cnt_sig.wait_ge(pe, i, c)
                    mm(CNT, ones[:, :], cnt[:, :])
                mm(GP, s.u_buf[0:n, 4, cols(c)], s.Ct_buf[0:n, cols(c)])
                t.transpose(BTP[:, 0:n], s.u_buf[0:n, 4, cols(c)], ident[0:n, 0:n]).then_inc(s.g_full.sem, 1)
                for j in range(1, L.segs):
                    decay_sums(j)

            def recur(L, s, i, c):
                q, hp = c % 2, L.hp
                p = open_front(pe, L, s, i, f"inter{c}")
                s.S.wait_ge(pe, i, c + 1)
                filled(mm(p[:, :], s.Ct_buf[:, cols(c)], S[:, :]), s, L, f"inter{c}")
                p = open_front(pe, L, s, i, f"state{c}")
                s.bs.wait_ge(pe, i, c + 1)
                s.xs.wait_ge(pe, i, c + 1)
                filled(mm(p[0:64, :], Bs[:, q, :], Xs[:, q, :]), s, L, f"state{c}")
                s.y0.wait_ge(pe, i, c)
                s.xdt.wait_ge(pe, i, c + 1)
                for j in range(L.heads):
                    if j % 4 == 0:
                        s.M.wait_ge(pe, i, c * L.segs + j // 4 + 1)
                    last = mm(INTRA[:, j * hp:(j + 1) * hp], E[:, q, j * P:(j + 1) * P],
                              Xdt[:, q, j * hp:(j + 1) * hp])
                last.then_inc(s.intra_full.sem, 1)

            def y_turned(L, s, i, c):
                s.yg.wait_ge(pe, i, c + 1)
                s.x2.wait_ge(pe, i, c)
                for k in range(CH):
                    last = t.transpose(YO[:, cols(k)], yb[:, c % 2, cols(k)], ident[:, :])
                last.then_inc(s.yo_full.sem, 1)

            def project(L, s, i, c):
                w = W[LAYERS.index(L)]
                s.yT.wait_ge(pe, i, c + 1)
                for k in range(CH):
                    last = mm(YO[:, 0:D], yT[:, k, :], w["out"][:, k, :], k == 0, k == CH - 1)
                last.then_inc(s.yo_full.sem, 1)

            def up(b, j):
                h2T_sig.wait_ge(pe, b, 2)
                p = open_back(pe, b, f"up{j}")
                for k in range(KD):
                    last = mm(p[:, :], w1[:, k, cols(j)], h2T[:, k, :], k == 0, k == 1)
                back_filled(last, f"up{j}")

            def step0(f, b, n):
                L, s = LAYERS[0], sets[0]
                between = () if b is None else (lambda: y_turned(L, s, b, CH - 1),
                                                lambda: project(L, s, b, CH - 1))
                if f is not None:
                    head(L, s, f, between)
                else:
                    for part in between:
                        part()
                if b is not None:
                    for src, name, ready, rows in ((leaf, "lT", leaf_sig, 1), (x2, "h2T", h2_sig, CH)):
                        ready.wait_ge(pe, b, rows)
                        for k in range(KD):
                            p = open_back(pe, b, f"{name}{k}")
                            for c in range(CH):
                                last = t.transpose(p[:, cols(c)], src[:, c, cols(k)], ident[:, :])
                            back_filled(last, f"{name}{k}")
                    for j in EARLY_UPS:
                        up(b, j)
                if f is not None:
                    decay_log_sums(L, s, f)
                    chunk(L, s, f, 0)
                for c in range(CH):
                    if b is not None:
                        for j in LATE_UPS[c]:
                            up(b, j)
                    if f is not None:
                        if c + 1 < CH:
                            chunk(L, s, f, c + 1)
                        if c:
                            y_turned(L, s, f, c - 1)
                        recur(L, s, f, c)
                        if c:
                            project(L, s, f, c - 1)
                if b is not None:
                    am_sig.wait_ge(pe, b, HB)
                    lT_sig.wait_ge(pe, b, 2)
                    for c in range(CH):
                        p = open_back(pe, b, f"down{c}")
                        for k in range(KD):
                            mm(p[:, 0:D], lT[:, k, cols(c)], wv[:, k, :], k == 0, False)
                        for k in range(HB):
                            last = mm(p[:, 0:D], am[:, k, cols(c)], w2[:, k, :], False, k == HB - 1)
                        back_filled(last, f"down{c}")
                if n is not None:
                    rows_turned(L, s, n)
                if b is not None:
                    for g in range(2):
                        p = open_back(pe, b, f"nT{g}")
                        xo_sig.wait_ge(pe, b, 2 * g + 2)
                        for k in range(KD):
                            for c in range(2):
                                last = t.transpose(p[:, (2 * k + c) * P:(2 * k + c + 1) * P],
                                                   xo[:, 2 * g + c, cols(k)], ident[:, :])
                        back_filled(last, f"nT{g}")
                    for g in range(2):
                        p = open_back(pe, b, f"rt{g}")
                        nT_sig.wait_ge(pe, b, g + 1)
                        for c in range(2):
                            for k in range(KD):
                                last = mm(p[:, c * NE:(c + 1) * NE], nT[:, k, cols(2 * g + c)], wr[:, k, :],
                                          k == 0, k == 1)
                        back_filled(last, f"rt{g}")

            rows_turned(LAYERS[0], sets[0], 0)
            step0(0, None, 1)
            pe.wait_ge(prepped, PREPPED)
            step0(1, 0, 2)
            with pe.Fori(2, STEPS - 1) as i:
                step0(i, i - 1, i + 1)
            step0(STEPS - 1, STEPS - 2, None)
            step0(None, STEPS - 1, None)
            pe.drain().then_inc(phase, 1)
            pe.wait_ge(phase, 5)

            L1, s1 = LAYERS[1], sets[1].at(0)

            def head_part(i, c):
                if c == 0:
                    s1.hT_loaded[s1.q].wait_ge(pe, i, 16 - 8 * s1.q)
                    dt_proj(L1, s1, i)
                    in_proj(L1, s1, i, 0)
                elif c == 1:
                    in_proj(L1, s1, i, 1)
                    in_proj(L1, s1, i, 2)
                elif c == 2:
                    in_proj(L1, s1, i, 3)
                    in_proj(L1, s1, i, 4)
                    decay_log_sums(L1, s1, i)

            def step1(i, q, more):
                for c in range(CH):
                    s1.at(q)
                    if c + 1 < CH:
                        chunk(L1, s1, i, c + 1)
                    recur(L1, s1, i, c)
                    first = isinstance(i, int) and i == 0 and c == 0
                    before = (i, c - 1) if c else (i - 1, CH - 1)
                    if not first:
                        y_turned(L1, s1, *before)
                    if more:
                        s1.at(1 - q)
                        head_part(i + 1, c)
                    if not first:
                        project(L1, s1, *before)
                if more:
                    chunk(L1, s1, i + 1, 0)

            for c in range(CH):
                head_part(0, c)
            chunk(L1, s1, 0, 0)
            all_steps(pe, step1)
            y_turned(L1, s1, STEPS - 1, CH - 1)
            project(L1, s1, STEPS - 1, CH - 1)
            pe.drain().then_inc(phase, 1)
            pe.wait_ge(phase, 10)

            pe.wait_ge(ge_ready, 1)
            ge = GE[:, :, :, :].rearrange("p a e t -> p (a e t)")
            mm(bank[0][:, :], triU[:, :], ge).then_inc(pre_full, 1)
            mm(bank[1][:, :], ones[:, :], ge).then_inc(pre_full, 1)
            pe.wait_ge(ge_ready, 2)

            def slots(e):
                for k in range(TILES):
                    ol_ready.wait_ge(pe, e, k + 1)
                    mm(bank[2][:, bass.ds(16 * e, 16)], OL[:, k % 4, :],
                       OHR[:, bass.ds(e * TILES + k, 1), :].rearrange("p a n -> p (a n)"), k == 0,
                       k == TILES - 1).then_inc(ol_used.sem, 1)

            slots(0)
            with pe.Fori(1, NE) as e:
                slots(e)
            pe.drain().then_inc(idx_full, 1)
            pe.wait_ge(idx_ready, 1)

            def parts(high, low):
                return ((high[0], high[1]), (high[0], low[1]), (low[0], high[1]))

            def tokens(i, s):
                q = s % 2
                if s == HS:
                    i, s = i + 1, 0
                gathered[q].wait_ge(pe, i, 64 * (s // 2 + 1))
                for k in range(KD):
                    xt_low.wait_ge(pe, i, 2 * s + k - 1)
                    for c in range(4):
                        last = t.transpose(bank[k][:, cols(c)], xg[:, q, c, cols(k)], ident[:, :])
                    last.then_inc(xt_full.sem, 1)

            def up(i, s):
                q = s % 2
                if s % 2 == 0:
                    w_low[s // 2].wait_ge(pe, i, 4)
                xt_low.wait_ge(pe, i, 2 * (s + 1))
                wh, wl = (w[:, s // 2, 0:KD * HID].rearrange("p (k n) -> p k n", k=KD) for w in (EWh, EWl))
                for j in range(HB):
                    gelu_sig.wait_ge(pe, i, HB * s + j - 1)
                    for k in range(KD):
                        for n, (w, x) in enumerate(parts((wh, xTh), (wl, xTl))):
                            last = mm(bank[2 + j % 2][:, :], w[:, k, cols(j)], x[:, q, k, :],
                                      k == 0 and n == 0, k == KD - 1 and n == 2)
                    last.then_inc(eup_full.sem, 1)

            def down(i, s):
                q = s % 2
                am_low.wait_ge(pe, i, HB * (s + 1))
                wh, wl = (w[:, s // 2, KD * HID:].rearrange("p (k n) -> p k n", k=HB) for w in (EWh, EWl))
                for c in range(4):
                    edown_read.wait_ge(pe, i, 4 * (s - 1) + c + 1)
                    for k in range(HB):
                        for n, (x, w) in enumerate(parts((amh, wh), (aml, wl))):
                            last = mm(bank[4 + c][:, 0:D], x[:, q, k, cols(c)], w[:, k, :],
                                      k == 0 and n == 0, k == HB - 1 and n == 2)
                    last.then_inc(edown_full.sem, 1)

            def estep(i, more):
                for s in range(HS):
                    up(i, s)
                    if more or s + 1 < HS:
                        tokens(i, s + 1)
                    if s:
                        down(i, s - 1)
                    elif not (isinstance(i, int) and i == 0):
                        down(i - 1, HS - 1)

            tokens(0, 0)
            estep(0, True)
            with pe.Fori(1, NE // 2 - 1) as i:
                estep(i, True)
            estep(NE // 2 - 1, False)
            down(NE // 2 - 1, HS - 1)


def kernel(**inputs):
    import numpy as np
    import concourse.bacc as bacc
    from concourse.bass_utils import run_bass_kernel_spmd as run

    def arr(name):
        return np.ascontiguousarray(inputs[name])

    def spread(a, rows, width):
        o = np.zeros((width,) + a.shape[1:], a.dtype)
        for at, lo, hi in rows:
            o[at:at + hi - lo] = a[lo:hi]
        return o

    def columns(a):
        return np.ascontiguousarray(a.reshape(-1, P).T)

    h = {"L0_attn_x": arr("L0_attn_x")}
    win = {"m0": arr("L0_attn_W_in"), "m1": arr("L1_attn_in_proj_w").T}
    cw = {"m0": arr("L0_attn_conv_w"), "m1": arr("L1_attn_conv_w")[:, 0, :]}
    cb = {"m0": arr("L0_attn_conv_b"), "m1": arr("L1_attn_conv_b")}
    for L, pre in zip(LAYERS, ("L0_attn_", "L1_attn_")):
        n, w = L.name, win[L.name]
        s, at = L.state, 2 * DI
        place = [(0, 0, s), (L.cpart, s, 2 * s)]
        h[n + "_wz"] = w[:, 0:DI]
        h[n + "_wx"] = w[:, DI:at]
        h[n + "_wbc"] = spread(w[:, at:at + 2 * s].T, place, P).T
        h[n + "_wdt"] = w[:, at + 2 * s:]
        taps = np.concatenate([cw[n], cb[n][:, None]], axis=1)
        taps = np.concatenate([taps[0:DI], spread(taps[DI:], place, P)], axis=0)
        h[n + "_conv"] = taps.reshape(5, P, L.taps + 1).transpose(1, 0, 2)
        h[n + "_dtb"] = arr(pre + "dt_bias")
        h[n + "_alog"] = arr(pre + "A_log")
    h["m0_D"], h["m1_D"] = arr("L0_attn_D"), arr("L1_attn_D_param")
    h["m0_wo"], h["m1_wo"] = arr("L0_attn_W_out"), arr("L1_attn_out_proj_w").T
    h["m0_gn"], h["m1_gn"] = columns(arr("L0_attn_norm_gate_w")), columns(arr("L1_attn_norm_w"))
    h["n1w"], h["n2w"] = columns(arr("L0_attn_norm1_w")), columns(arr("L0_attn_norm2_w"))
    h["wq"] = arr("L0_ffn_Wq")
    h["routersT"] = spread(arr("L0_ffn_routers"), [(0, 0, LEAVES - 1)], LEAVES).T
    h["leafT"] = arr("L0_ffn_leaf_values").T
    h["treeoutT"] = arr("L0_ffn_Wout_w").T
    h["w1"], h["w2"] = arr("L0_attn_mlp_w1"), arr("L0_attn_mlp_w2")
    h["b1"], h["b2"], h["treeb"] = columns(arr("L0_attn_mlp_b1")), arr("L0_attn_mlp_b2"), arr("L0_ffn_Wout_b")
    h["wr"] = arr("L1_ffn_Wr")
    h["e_w1"], h["e_w2"] = arr("L1_ffn_W1"), arr("L1_ffn_W2")
    h["e_b1"] = arr("L1_ffn_b1").reshape(NE, HB, P).transpose(0, 2, 1)
    h["e_b2"] = arr("L1_ffn_b2")

    nc = bacc.Bacc("TRN2", target_bir_lowering=False, num_devices=1)
    arrays, d = {}, {}
    for name, a in h.items():
        a = np.ascontiguousarray(a)
        arrays[f"in_{name}"] = a
        d[name] = nc.dram_tensor(f"in_{name}", a.shape, mybir.dt.from_np(a.dtype), kind="ExternalInput").ap()
    out = nc.dram_tensor("out_0", (NB, SEQ, D), fp32, kind="ExternalOutput").ap()
    program(nc, d, out)
    r = run(nc, [arrays], core_ids=[0])
    return r.results[0]["out_0"]
```
